# Optimizing a Trainium2 kernel written in Bass

```python
import numpy as np
import jax
import jax.numpy as jnp

def _softmax(x, axis=-1):
    return jax.nn.softmax(x, axis=axis)

def _gelu(x):
    return jax.nn.gelu(x, approximate=True)

def _silu(x):
    return jax.nn.silu(x)

def _sigmoid(x):
    return jax.nn.sigmoid(x)

def _layernorm(x, axis=-1, eps=1e-05):
    m = jnp.mean(x, axis=axis, keepdims=True)
    v = jnp.var(x, axis=axis, keepdims=True)
    return (x - m) / jnp.sqrt(v + eps)

def _scatter_add(tgt, idx, src, axis=0):
    return tgt.at[idx].add(src)

def _segment_sum(src, seg, n):
    return jax.ops.segment_sum(src, seg, n)
kernel_name = 'mk_xattn_ffn_d2_seqx_r4_4efaee'

def setup_inputs(seed: int=0):
    np.random.seed(seed)
    _w = jnp.asarray

    def _rec_inputs():
        import jax
        import jax.numpy as jnp
        _rk = jax.random.key(seed)
        x = 7.22e-05 + 1 * jax.random.normal(jax.random.fold_in(_rk, 1), (2, 1024, 256), jnp.float32)
        _lenS = 1024 - jax.random.randint(jax.random.fold_in(_rk, 7), (2,), 0, max(1, 1024 // 4) + 1, jnp.int32)
        _lenS2 = 77 - jax.random.randint(jax.random.fold_in(_rk, 8), (2,), 0, max(1, 77 // 4) + 1, jnp.int32)
        _ctx_1024P = jax.random.normal(jax.random.fold_in(_rk, 11), (2, 16, 256), jnp.float32)
        _ctx_1024c = jax.random.dirichlet(jax.random.fold_in(_rk, 511), 0.3 * jnp.ones((16,), jnp.float32), (2, 77))
        _ctx_1024t = jnp.einsum('bsk,bkd->bsd', _ctx_1024c, _ctx_1024P)
        _ctx_1024t = _ctx_1024t * jax.lax.rsqrt(jnp.mean(jnp.square(_ctx_1024t)) + 1e-12) * 0.953939
        ctx_1024 = 4.13588e-05 + 0.999923 * (_ctx_1024t + 0.3 * jax.random.normal(jax.random.fold_in(_rk, 611), (2, 77, 256), jnp.float32))
        return (x, ctx_1024)
    x, ctx_1024 = _rec_inputs()

    def _L0_xattn_setup():
        import jax, jax.numpy as jnp
        import numpy as np
        B, LQ, LK = (4, 512, 512)
        DQ, DK, DO = (256, 256, 256)
        key = jax.random.key(seed)
        ks = jax.random.split(key, 9)
        s = 0.02
        return {'query_input': jax.random.normal(ks[0], (B, LQ, DQ), jnp.float32), 'key_input': jax.random.normal(ks[1], (B, LK, DK), jnp.float32), 'value_input': jax.random.normal(ks[2], (B, LK, DK), jnp.float32), 'Wq': jax.random.normal(ks[3], (DQ, DO), jnp.float32) * s, 'bq': jax.random.normal(ks[4], (DO,), jnp.float32) * s, 'Wk': jax.random.normal(ks[5], (DK, DO), jnp.float32) * s, 'bk': jax.random.normal(ks[6], (DO,), jnp.float32) * s, 'Wv': jax.random.normal(ks[7], (DK, DO), jnp.float32) * s, 'bv': jax.random.normal(ks[8], (DO,), jnp.float32) * s}
    _L0_xattn_all = _L0_xattn_setup()
    _L0_xattn_in = {k: v for k, v in _L0_xattn_all.items() if k in ('Wq', 'bq', 'Wk', 'bk', 'Wv', 'bv')}
    del _L0_xattn_all

    def _L0_ffn_setup():
        import jax, jax.numpy as jnp
        import numpy as np
        import math
        B, S, D = (2, 512, 256)
        H = 16
        HD = D // H
        FFN = 512
        E = 8
        TOP_K = 2
        CAP_FACTOR = 1.25
        EPS = 1e-06
        BASE = 10000.0
        CAP = max(math.ceil(B * S * TOP_K * CAP_FACTOR / E), 1)

        def _rmsnorm(x, w):
            rms = jax.lax.rsqrt(jnp.mean(x * x, axis=-1, keepdims=True) + EPS)
            return w * x * rms

        def _rope(x, cos, sin):
            xr = x[..., 0::2]
            xi = x[..., 1::2]
            c = cos[None, None]
            s_ = sin[None, None]
            out_r = xr * c - xi * s_
            out_i = xr * s_ + xi * c
            return jnp.stack([out_r, out_i], axis=-1).reshape(x.shape)

        def _mha(x, w_qkv, w_o):
            b, s, d = x.shape
            qkv = x @ w_qkv
            q, k, v = jnp.split(qkv, 3, axis=-1)
            to_heads = lambda z: z.reshape(b, s, H, HD).transpose(0, 2, 1, 3)
            q, k, v = (to_heads(q), to_heads(k), to_heads(v))
            theta = BASE ** (-2.0 * (jnp.arange(HD // 2, dtype=jnp.float32) / HD))
            freqs = jnp.arange(s, dtype=jnp.float32)[:, None] * theta[None, :]
            cos, sin = (jnp.cos(freqs), jnp.sin(freqs))
            q = _rope(q, cos, sin)
            k = _rope(k, cos, sin)
            scores = jnp.einsum('bhqd,bhkd->bhqk', q, k) / jnp.sqrt(jnp.float32(HD))
            causal = jnp.tril(jnp.ones((s, s), dtype=bool))
            scores = jnp.where(causal, scores, -jnp.inf)
            attn = jax.nn.softmax(scores, axis=-1)
            y = jnp.einsum('bhqk,bhkd->bhqd', attn, v)
            y = y.transpose(0, 2, 1, 3).reshape(b, s, d)
            return y @ w_o

        def _moe(x, w_router, w1, w2):
            b, s, d = x.shape
            t = b * s
            xf = x.reshape(t, d)
            logits = xf.astype(jnp.float32) @ w_router.astype(jnp.float32)
            probs = jax.nn.softmax(logits, axis=-1)
            g, eidx = jax.lax.top_k(probs, TOP_K)
            fg = g.reshape(t * TOP_K)
            fe = eidx.reshape(t * TOP_K)
            tok_of = jnp.arange(t * TOP_K) // TOP_K
            masked = jnp.where(fe[None, :] == jnp.arange(E)[:, None], fg[None, :], -jnp.inf)
            vals, idx = jax.lax.top_k(masked, CAP)
            valid = jnp.isfinite(vals)
            gates = jnp.where(valid, vals, 0.0)
            tok = tok_of[idx]
            xe = xf[tok]
            h = jax.nn.relu(jnp.einsum('ecd,edf->ecf', xe, w1))
            ye = jnp.einsum('ecf,efd->ecd', h, w2) * gates[..., None]
            y = jnp.zeros_like(xf).at[tok.reshape(-1)].add(ye.reshape(-1, d))
            return y.reshape(b, s, d)
        key = jax.random.key(seed)
        ks = jax.random.split(key, 6)
        sd = 0.02
        return {'x': jax.random.normal(ks[0], (B, S, D), jnp.float32), 'g1': jnp.ones((D,), jnp.float32), 'w_qkv': jax.random.normal(ks[1], (D, 3 * D), jnp.float32) * sd, 'w_o': jax.random.normal(ks[2], (D, D), jnp.float32) * sd, 'g2': jnp.ones((D,), jnp.float32), 'w_router': jax.random.normal(ks[3], (D, E), jnp.float32) * sd, 'w1': jax.random.normal(ks[4], (E, D, FFN), jnp.float32) * sd, 'w2': jax.random.normal(ks[5], (E, FFN, D), jnp.float32) * sd}
    _L0_ffn_all = _L0_ffn_setup()
    _L0_ffn_in = {k: v for k, v in _L0_ffn_all.items() if k in ('g1', 'w_qkv', 'w_o', 'g2', 'w_router', 'w1', 'w2')}
    del _L0_ffn_all

    def _L1_xattn_setup():
        import jax, jax.numpy as jnp
        import numpy as np
        HEADS = 16
        EMBED = 256
        HEAD_DIM = EMBED // HEADS
        key = jax.random.key(seed)
        ks = jax.random.split(key, 11)
        B, S, E = (4, 512, EMBED)
        s = 1.0 / np.sqrt(E)
        return {'query': jax.random.normal(ks[0], (B, S, E), jnp.float32), 'key': jax.random.normal(ks[1], (B, S, E), jnp.float32), 'value': jax.random.normal(ks[2], (B, S, E), jnp.float32), 'Wq': jax.random.normal(ks[3], (E, E), jnp.float32) * s, 'bq': jax.random.normal(ks[4], (E,), jnp.float32) * s, 'Wk': jax.random.normal(ks[5], (E, E), jnp.float32) * s, 'bk': jax.random.normal(ks[6], (E,), jnp.float32) * s, 'Wv': jax.random.normal(ks[7], (E, E), jnp.float32) * s, 'bv': jax.random.normal(ks[8], (E,), jnp.float32) * s, 'Wo': jax.random.normal(ks[9], (E, E), jnp.float32) * s, 'bo': jax.random.normal(ks[10], (E,), jnp.float32) * s}
    _L1_xattn_all = _L1_xattn_setup()
    _L1_xattn_in = {k: v for k, v in _L1_xattn_all.items() if k in ('Wq', 'bq', 'Wk', 'bk', 'Wv', 'bv', 'Wo', 'bo')}
    del _L1_xattn_all

    def _L1_ffn_setup():
        import jax, jax.numpy as jnp
        import numpy as np
        B, T, D, H, E = (4, 512, 256, 1024, 8)
        key = jax.random.key(seed)
        ks = jax.random.split(key, 7)
        x = jax.random.normal(ks[0], (B, T, D), dtype=jnp.float32)
        Wg = jax.random.normal(ks[1], (D, E), dtype=jnp.float32) / np.sqrt(D)
        bg = jax.random.normal(ks[2], (E,), dtype=jnp.float32) * 0.01
        W1 = jax.random.normal(ks[3], (E, D, H), dtype=jnp.float32) / np.sqrt(D)
        b1 = jax.random.normal(ks[4], (E, H), dtype=jnp.float32) * 0.01
        W2 = jax.random.normal(ks[5], (E, H, D), dtype=jnp.float32) / np.sqrt(H)
        b2 = jax.random.normal(ks[6], (E, D), dtype=jnp.float32) * 0.01
        return {'x': x, 'Wg': Wg, 'bg': bg, 'W1': W1, 'b1': b1, 'W2': W2, 'b2': b2}
    _L1_ffn_all = _L1_ffn_setup()
    _L1_ffn_in = {k: v for k, v in _L1_ffn_all.items() if k in ('Wg', 'bg', 'W1', 'b1', 'W2', 'b2')}
    del _L1_ffn_all
    return {'x': x, 'ctx_1024': ctx_1024, 'L0_xattn_Wq': _L0_xattn_in['Wq'], 'L0_xattn_bq': _L0_xattn_in['bq'], 'L0_xattn_Wk': _L0_xattn_in['Wk'], 'L0_xattn_bk': _L0_xattn_in['bk'], 'L0_xattn_Wv': _L0_xattn_in['Wv'], 'L0_xattn_bv': _L0_xattn_in['bv'], 'L0_ffn_g1': _L0_ffn_in['g1'], 'L0_ffn_w_qkv': _L0_ffn_in['w_qkv'], 'L0_ffn_w_o': _L0_ffn_in['w_o'], 'L0_ffn_g2': _L0_ffn_in['g2'], 'L0_ffn_w_router': _L0_ffn_in['w_router'], 'L0_ffn_w1': _L0_ffn_in['w1'], 'L0_ffn_w2': _L0_ffn_in['w2'], 'L1_xattn_Wq': _L1_xattn_in['Wq'], 'L1_xattn_bq': _L1_xattn_in['bq'], 'L1_xattn_Wk': _L1_xattn_in['Wk'], 'L1_xattn_bk': _L1_xattn_in['bk'], 'L1_xattn_Wv': _L1_xattn_in['Wv'], 'L1_xattn_bv': _L1_xattn_in['bv'], 'L1_xattn_Wo': _L1_xattn_in['Wo'], 'L1_xattn_bo': _L1_xattn_in['bo'], 'L1_ffn_Wg': _L1_ffn_in['Wg'], 'L1_ffn_bg': _L1_ffn_in['bg'], 'L1_ffn_W1': _L1_ffn_in['W1'], 'L1_ffn_b1': _L1_ffn_in['b1'], 'L1_ffn_W2': _L1_ffn_in['W2'], 'L1_ffn_b2': _L1_ffn_in['b2']}

def reference(x, ctx_1024, L0_xattn_Wq, L0_xattn_bq, L0_xattn_Wk, L0_xattn_bk, L0_xattn_Wv, L0_xattn_bv, L0_ffn_g1, L0_ffn_w_qkv, L0_ffn_w_o, L0_ffn_g2, L0_ffn_w_router, L0_ffn_w1, L0_ffn_w2, L1_xattn_Wq, L1_xattn_bq, L1_xattn_Wk, L1_xattn_bk, L1_xattn_Wv, L1_xattn_bv, L1_xattn_Wo, L1_xattn_bo, L1_ffn_Wg, L1_ffn_bg, L1_ffn_W1, L1_ffn_b1, L1_ffn_W2, L1_ffn_b2):
    import jax
    import jax.numpy as jnp

    def _L0_xattn_ref(query_input, key_input, value_input, Wq, bq, Wk, bk, Wv, bv):
        import jax, jax.numpy as jnp
        import numpy as np
        B, LQ, LK = (4, 512, 512)
        DQ, DK, DO = (256, 256, 256)
        scale = jnp.asarray(DO, query_input.dtype) ** 0.5
        q = query_input @ Wq + bq
        k = key_input @ Wk + bk
        v = value_input @ Wv + bv
        attn = jnp.einsum('bqd,bkd->bqk', q, k) / scale
        attn = jax.nn.softmax(attn, axis=-1)
        return jnp.einsum('bqk,bkd->bqd', attn, v)

    def _L0_ffn_ref(x, g1, w_qkv, w_o, g2, w_router, w1, w2):
        import jax, jax.numpy as jnp
        import numpy as np
        import math
        B, S, D = (2, 512, 256)
        H = 16
        HD = D // H
        FFN = 512
        E = 8
        TOP_K = 2
        CAP_FACTOR = 1.25
        EPS = 1e-06
        BASE = 10000.0
        CAP = max(math.ceil(B * S * TOP_K * CAP_FACTOR / E), 1)

        def _rmsnorm(x, w):
            rms = jax.lax.rsqrt(jnp.mean(x * x, axis=-1, keepdims=True) + EPS)
            return w * x * rms

        def _rope(x, cos, sin):
            xr = x[..., 0::2]
            xi = x[..., 1::2]
            c = cos[None, None]
            s_ = sin[None, None]
            out_r = xr * c - xi * s_
            out_i = xr * s_ + xi * c
            return jnp.stack([out_r, out_i], axis=-1).reshape(x.shape)

        def _mha(x, w_qkv, w_o):
            b, s, d = x.shape
            qkv = x @ w_qkv
            q, k, v = jnp.split(qkv, 3, axis=-1)
            to_heads = lambda z: z.reshape(b, s, H, HD).transpose(0, 2, 1, 3)
            q, k, v = (to_heads(q), to_heads(k), to_heads(v))
            theta = BASE ** (-2.0 * (jnp.arange(HD // 2, dtype=jnp.float32) / HD))
            freqs = jnp.arange(s, dtype=jnp.float32)[:, None] * theta[None, :]
            cos, sin = (jnp.cos(freqs), jnp.sin(freqs))
            q = _rope(q, cos, sin)
            k = _rope(k, cos, sin)
            scores = jnp.einsum('bhqd,bhkd->bhqk', q, k) / jnp.sqrt(jnp.float32(HD))
            causal = jnp.tril(jnp.ones((s, s), dtype=bool))
            scores = jnp.where(causal, scores, -jnp.inf)
            attn = jax.nn.softmax(scores, axis=-1)
            y = jnp.einsum('bhqk,bhkd->bhqd', attn, v)
            y = y.transpose(0, 2, 1, 3).reshape(b, s, d)
            return y @ w_o

        def _moe(x, w_router, w1, w2):
            b, s, d = x.shape
            t = b * s
            xf = x.reshape(t, d)
            logits = xf.astype(jnp.float32) @ w_router.astype(jnp.float32)
            probs = jax.nn.softmax(logits, axis=-1)
            g, eidx = jax.lax.top_k(probs, TOP_K)
            fg = g.reshape(t * TOP_K)
            fe = eidx.reshape(t * TOP_K)
            tok_of = jnp.arange(t * TOP_K) // TOP_K
            masked = jnp.where(fe[None, :] == jnp.arange(E)[:, None], fg[None, :], -jnp.inf)
            vals, idx = jax.lax.top_k(masked, CAP)
            valid = jnp.isfinite(vals)
            gates = jnp.where(valid, vals, 0.0)
            tok = tok_of[idx]
            xe = xf[tok]
            h = jax.nn.relu(jnp.einsum('ecd,edf->ecf', xe, w1))
            ye = jnp.einsum('ecf,efd->ecd', h, w2) * gates[..., None]
            y = jnp.zeros_like(xf).at[tok.reshape(-1)].add(ye.reshape(-1, d))
            return y.reshape(b, s, d)
        x = x + _mha(_rmsnorm(x, g1), w_qkv, w_o)
        x = x + _moe(_rmsnorm(x, g2), w_router, w1, w2)
        return x

    def _L1_xattn_ref(query, key, value, Wq, bq, Wk, bk, Wv, bv, Wo, bo):
        import jax, jax.numpy as jnp
        import numpy as np
        HEADS = 16
        EMBED = 256
        HEAD_DIM = EMBED // HEADS
        B, Sq, E = query.shape
        Sk = key.shape[1]
        H, D = (HEADS, HEAD_DIM)
        q = (query @ Wq.T + bq).reshape(B, Sq, H, D)
        k = (key @ Wk.T + bk).reshape(B, Sk, H, D)
        v = (value @ Wv.T + bv).reshape(B, Sk, H, D)
        scores = jnp.einsum('bqhd,bkhd->bhqk', q, k) / np.sqrt(D).astype(jnp.float32)
        attn = jax.nn.softmax(scores, axis=-1)
        out = jnp.einsum('bhqk,bkhd->bqhd', attn, v).reshape(B, Sq, E)
        return out @ Wo.T + bo

    def _L1_ffn_ref(x, Wg, bg, W1, b1, W2, b2):
        import jax, jax.numpy as jnp
        import numpy as np
        B, T, D, H, E = (4, 512, 256, 1024, 8)
        gate_scores = x @ Wg + bg
        top1 = jnp.argmax(gate_scores, axis=-1)
        onehot = jax.nn.one_hot(top1, Wg.shape[-1], dtype=x.dtype)
        h = jax.nn.relu(jnp.einsum('btd,edh->beth', x, W1) + b1[None, :, None, :])
        y = jnp.einsum('beth,ehd->betd', h, W2) + b2[None, :, None, :]
        out = jnp.einsum('betd,bte->btd', y, onehot)
        return out
    x = x + _L0_xattn_ref(_layernorm(x, axis=-1), ctx_1024, ctx_1024, L0_xattn_Wq, L0_xattn_bq, L0_xattn_Wk, L0_xattn_bk, L0_xattn_Wv, L0_xattn_bv)
    x = x + _L0_ffn_ref(_layernorm(x, axis=-1), L0_ffn_g1, L0_ffn_w_qkv, L0_ffn_w_o, L0_ffn_g2, L0_ffn_w_router, L0_ffn_w1, L0_ffn_w2)
    x = x + _L1_xattn_ref(_layernorm(x, axis=-1), ctx_1024, ctx_1024, L1_xattn_Wq, L1_xattn_bq, L1_xattn_Wk, L1_xattn_bk, L1_xattn_Wv, L1_xattn_bv, L1_xattn_Wo, L1_xattn_bo)
    x = x + _L1_ffn_ref(_layernorm(x, axis=-1), L1_ffn_Wg, L1_ffn_bg, L1_ffn_W1, L1_ffn_b1, L1_ffn_W2, L1_ffn_b2)
    return x

_drawn_inputs = setup_inputs


def setup_inputs(seed=0):
    import zlib

    import numpy as np

    out = dict(_drawn_inputs(seed))
    spreads = {'L0_ffn_g1': (1.0, 0.6), 'L0_ffn_g2': (1.0, 0.6)}
    factors = {'L0_xattn_bq': 7.573,
     'L0_xattn_Wk': 3.323,
     'L0_xattn_bk': 8.0,
     'L1_xattn_bk': 8.0,
     'L1_ffn_b1': 8.0,
     'L1_ffn_b2': 8.0}
    for name, (base, spread) in spreads.items():
        noise = np.random.default_rng([zlib.crc32(name.encode()), seed]).standard_normal(out[name].shape)
        drawn = base * np.exp(spread * noise) if base else spread * noise
        out[name] = jnp.asarray(drawn.astype(out[name].dtype))
    for name, factor in factors.items():
        out[name] = (out[name] * factor).astype(out[name].dtype)
    return out
```

```python
import concourse.bass as bass
from concourse import mybir
from contextlib import ExitStack


class Chain:

    def __init__(self, eng, sem):
        self.eng, self.sem, self.base, self.n, self.i, self.per = eng, sem, 0, 0, None, 0

    def value(self):
        at = self.base + self.n
        return at if self.i is None else self.i * self.per + at

    def enter(self, i, per):
        self.base, self.n, self.i, self.per = self.base + self.n, 0, i, per

    def leave(self, passes):
        assert self.n == self.per, (self.n, self.per)
        self.base, self.n, self.i = self.base + passes * self.per, 0, None

    def __call__(self, ins, alone=None):
        self.n += 1
        ins.then_inc(self.sem, 1)
        self.eng.wait_ge(self.sem, self.value())
        if alone:
            self.eng.sem_inc(alone, 1)


def build_program(nc, x_in, ctxT_in, const_f_in, const_b_in, rope_in,
                  wq0T_in, bq0_in, wk0_in, bk0_in, wv0_in, bv0_in,
                  g1_in, wqk_in, wv_in, wo_in, g2_in, wr_in, w1e_in, w2e_in,
                  wq1_in, bq1_in, wk1_in, bk1_in, wv1_in, bv1_in, wo1_in, bo1_in,
                  wg_in, bg_in, w1_in, b1_in, w2_in, b2_in, out):
    f32, bf16 = mybir.dt.float32, mybir.dt.bfloat16
    i32, u32 = mybir.dt.int32, mybir.dt.uint32
    ALU, ACT, AX = mybir.AluOpType, mybir.ActivationFunctionType, mybir.AxisListType
    ds = bass.ds

    P = 128
    B, S, D = x_in.shape
    KC = D // P
    NT = B * S // P
    CT = 4
    CW = CT * P
    CPB = S // CW
    NCH = B * CPB
    LK = ctxT_in.shape[2] // B
    HEADS, HD = 16, 16
    GH = 4
    NG = HEADS // GH
    NS = B * NG
    PARTS = 3
    Q_PART = (0, 0, 0, 1, 1, 2)
    K_PART = (0, 1, 2, 0, 1, 0)
    QROWS = len(Q_PART) * HD
    AROWS = QROWS + PARTS
    E = 8
    F0 = w1e_in.shape[2]
    FC0 = F0 // P
    CAP = 320
    SLOTS0 = E * CAP
    F1 = w1_in.shape[2]
    FC1 = F1 // P
    NT1 = NT + E - 1
    SLOTS1 = NT1 * P
    VW = 32
    NEG = -1.0e30
    LN_EPS, RMS_EPS = 1e-5, 1e-6

    ctx = ExitStack()
    with ctx:
        def sb(name, shape, dt=f32):
            return ctx.enter_context(nc.sbuf_tensor(name, shape, dt))

        def sem(name):
            return ctx.enter_context(nc.semaphore(name))

        qk_dram = nc.dram_tensor("qk_dram", (2, PARTS, 2, NS, 32, S), bf16, kind="Internal").ap()
        xe_dram = nc.dram_tensor("xe_dram", (SLOTS0, D), f32, kind="Internal").ap()
        ye_dram = nc.dram_tensor("ye_dram", (SLOTS0 + 1, D), f32, kind="Internal").ap()
        xs_dram = nc.dram_tensor("xs_dram", (SLOTS1, D), f32, kind="Internal").ap()
        ys_dram = nc.dram_tensor("ys_dram", (SLOTS1, D), f32, kind="Internal").ap()
        bp_dram = nc.dram_tensor("bp_dram", (PARTS, E * (F1 + D)), bf16, kind="Internal").ap()

        X = sb("X", [P, NT, D])
        H = sb("H", [P, NT, D])
        XF = sb("XF", [P, NT, D])
        CF = sb("CF", [P, const_f_in.shape[1]])
        CB = sb("CB", [P, const_b_in.shape[1]], bf16)
        ident = CF[:, 0:P]
        ones_mat = CF[:, 2 * P:3 * P]
        CO = 3 * P
        w8 = CF[:, CO:CO + E]
        base0 = CF[:, CO + E:CO + 2 * E]
        j128 = CF[:, CO + 2 * E:CO + 2 * E + 16]
        jt = CF[0:1, CO + 32:CO + 32 + NT1]
        neg_half = CF[:, CO + 64:CO + 64 + NT]
        headmask = CF[:, CO + 80:CO + 88]
        ones_row = CF[0:1, 2 * P:3 * P]
        identb = CB[:, 0:P]
        mask_q = CB[:, P:2 * P]
        mask_k = CB[:, 2 * P:3 * P]
        ones_b = CB[:, 3 * P:4 * P]
        tri_b = CB[:, 4 * P:5 * P]
        ones3 = CB[0:PARTS, 3 * P:4 * P]
        top_bit = CF[:, CO + 88:CO + 96]

        REG = sb("REG", [P, 2 * E * KC * F1])

        class Carve:
            def __init__(self, at=0, buf=None):
                self.at, self.buf = at, REG if buf is None else buf

            def __call__(self, shape, dt=f32, parts=P):
                n = 1
                for m in shape:
                    n *= m
                words = n if dt == f32 else n // 2
                a = self.buf[0:parts, self.at:self.at + words]
                self.at += words
                assert self.at <= self.buf.shape[1], self.at
                if dt != f32:
                    a = a.bitcast(dt)
                names = "abcd"[:len(shape)]
                if len(shape) > 1:
                    a = a.rearrange(f"p ({' '.join(names)}) -> p {' '.join(names)}",
                                    **{k: m for k, m in zip(names[1:], shape[1:])})
                return a

        c1 = Carve()
        VB = c1((NS, S // P, GH * HD))
        after_v = c1.at
        ctxT = c1((KC, B * LK))
        wq0T, wk0, wv0 = c1((KC, D)), c1((KC, D)), c1((KC, D))
        bq0, bk0, g1c = c1((KC,)), c1((KC,)), c1((KC,))
        bv0 = c1((D,))
        KT0 = c1((KC, B * LK))
        A0 = c1((KC, B * LK))
        CB0 = c1((B * LK,), f32, 1)
        V0 = c1((B, D), f32, LK)
        wqk, wv = c1((KC, 4 * P)), c1((KC, D))
        rope = c1((2, S))
        Z = c1((CT, D))
        ZT = c1((KC, CW))
        P0 = c1((CT, LK + 1))
        PT0 = c1((CW,), f32, LK)
        U = c1((CT, D))
        UT = c1((KC, CW))
        RT = c1((4, 2, CW))
        ROT = c1((2, 2, CW))
        PARTB = c1((PARTS, 2, 2, CW), bf16)
        c2 = Carve(after_v)
        QT = c2((2, GH, S), bf16)
        KT = c2((2, GH, S), bf16)
        PB = c2((2, GH, CW))
        VS = c2((2, S // P, GH, VW))
        YT = c2((2, CW))
        MXP = c2((GH, 2 * CT, 2))
        NM = c2((GH, 2 * CT))
        NR = c2((GH, 2 * CT))
        MP = c2((PARTS, GH, 2 * CT), bf16)
        MT = c2((P,), bf16)
        RY = c2((CT, GH))
        ST = sb("ST", [P, CT, 6])
        MV = sb("MV", [P, CT, 2])
        SM = sb("SM", [P, 12, CT])
        VE, RSTD, MX, NB, RSUM, RRS, R1, R2, S1, TV, TA = (SM[:, n, :] for n in range(11))
        LG = sb("LG", [P, NT, E])

        XB = sb("XB", [P, 6900])
        ZERO = XB[:, 0:4 * D]

        PS = ctx.enter_context(nc.psum_tensor("PS", [P, 8, 512], f32))

        s_spare = sem("spare")
        ld_x, ld_c, ld_w = sem("ld_x"), sem("ld_consts"), sem("ld_weights1")
        s_chv, s_chp = sem("vector_chain"), sem("pool_chain")
        pre_k, pre_ks, pre_a, pre_as, pre_w = (sem("pre_" + n) for n in ("k", "ks", "a", "as", "w"))
        (s_var, s_rstd, s_z, s_zT, s_zTs, s_sc, s_nb, s_p, s_pT, s_pTs, s_o, s_var2, s_rstd2, s_u, s_uT, s_uTs,
         s_qk, s_v, s_rt, s_vs, s_rot, s_hi, s_res, s_mid, s_lo, s_qkst) = (
            sem("p1_" + n) for n in ("var", "rstd", "z", "zT", "zTs", "sc", "nb", "p", "pT", "pTs", "o", "var2",
                                     "rstd2", "u", "uT", "uTs", "qk", "v", "rt", "vs", "rot", "hi", "res", "mid",
                                     "lo", "qkst"))
        NK = S // P
        UNITS = []
        for i in range(NK):
            w = (i % CT + 1) * P
            per = max(1, 512 // w) if w != 3 * P else 1
            for h0 in range(0, GH, per):
                UNITS.append((i, h0, per, (i // CT) * CW, w, True))
            if i >= CT:
                for h0 in range(GH):
                    UNITS.append((i, h0, 1, 0, CW, False))
        NU = len(UNITS)
        STAGES = [(c, j) for c in range(CPB) for j in range(CT * (c + 1))]
        NSTG = len(STAGES)
        PER_STAGE = -(-NU // (NSTG - 3))
        NLD = 2 * len(Q_PART) * 2
        m_ps = [PS[:, n, :] for n in range(2)]
        s_ps = [PS[:, 2 + 2 * n:4 + 2 * n, :] for n in range(2)]
        y_ps = PS[:, 6, :]
        t_ps = PS[:, 7, :]
        ld_qk = [sem(f"ld_qk{n}") for n in range(2)]
        (s_ini, s_mx, s_mfree, s_mp, s_mpt, s_mt, s_mrow, s_sT, s_sfree, s_pvd, s_y, s_yev, s_yt, s_yn, s_vst) = (
            sem("p2_" + n) for n in ("init", "max_scores", "max_bank_free", "maxparts", "maxparts_T", "maxT",
                                     "maxrows", "scoresT", "exp_done", "pv_done", "y", "y_evac", "y_T", "y_norm",
                                     "v_staged"))

        def q0_of(c, j):
            return max(0, P * (j - CT * c))
        c3 = Carve(0, XB)
        WO = c3((KC, D))
        G2 = c3((D,))
        WR = c3((KC, E))
        YC = c3((CT, D))
        YCT = c3((KC, CW))
        XC = c3((CT, D))
        XCT = c3((KC, CW))
        c3r = Carve(E * KC * F1)
        PR, G, SEL1, SEL2, TE1, TE2, EX = (c3r((NT, E)) for _ in range(7))
        GEb, EQb, KEEPb = (c3r((NT, E), bf16) for _ in range(3))
        M1, M2, VM, SU, RSU, GATE1, GATE2, IDF = (c3r((NT,)) for _ in range(8))
        CUR, CAND, CNT, TK, BIT, NGT = (c3r((E,)) for _ in range(6))
        IDX1, IDX2 = (c3r((NT,)).bitcast(u32) for _ in range(2))
        gathered_at = c3r.at
        XEB = c3r((2, 3, D))
        XET = c3r((2, KC, CAP))
        HTE = c3r((FC0, CAP))
        assert c3r.at >= c2.at
        W1E = c3r((2, KC, F0))
        W2E = c3r((2, FC0, D))
        YEB = c3r((2, 3, D))
        TAIL = CAP - 2 * P
        ld_5 = sem("ld_last_experts")
        ld_3, ld_we, ld_xe = sem("ld_phase3"), [sem(f"ld_we{n}") for n in range(2)], [sem(f"ld_xe{n}") for n in range(2)]
        (p3_yc, p3_yT, p3_yTs, p3_o, p3_ms, p3_r, p3_xc, p3_xs, p3_xT, p3_xTs, p3_lg, p3_lgs) = (
            sem("p3_" + n) for n in ("yc", "yT", "yTs", "o", "ms", "r", "xc", "xs", "xT", "xTs", "lg", "lgs"))
        (rt_sub, rt_exp, rt_ge, rt_cnt, rt_gt, rt_ngt, rt_keep, rt_pos, rt_idx, rt_eqT) = (
            sem("route_" + n) for n in ("sub", "exp", "ge", "count", "gt", "gt_count", "keep", "pos", "idx", "eq_prefix"))
        s_scat = sem("scattered")
        (me_xT, me_xTs, me_h, me_hs, me_y, me_ys, me_out) = (
            sem("moe0_" + n) for n in ("xT", "xTs", "h", "hs", "y", "ys", "out"))
        BITS = 30
        yT3_ps, o3_ps = PS[:, 0:2, :], PS[:, 2:4, :].rearrange("p a (t d) -> p (a t) d", t=2)
        xT3_ps, lg_ps = PS[:, 4:6, :], PS[:, 6, 0:CT * E].rearrange("p (t e) -> p t e", t=CT)
        cnt_ps = PS[:, 0, 0:NT * E].rearrange("p (t e) -> p t e", t=NT)
        pfx_ps = PS[:, 1, 0:NT * E].rearrange("p (t e) -> p t e", t=NT)
        pos_ps = PS[:, 2, 0:NT * E].rearrange("p (t e) -> p t e", t=NT)
        xeT_ps = PS[:, 0:2, 0:CAP]
        he_ps = PS[:, 2:6, 0:CAP]
        ye_ps = PS[:, 6:8, :].rearrange("p a (t d) -> p (a t) d", t=2)
        HW = HD + 1
        SCW = LK * HEADS
        c4 = Carve(0, XB)
        KBD = c4((B, KC, 8, LK))
        V1 = c4((B, HEADS, HW), f32, LK)
        SS = c4((2, HEADS, LK))
        Q4T = c4((KC, CW))
        BO = c4((D,))
        WG = c4((KC, E))
        BG = c4((E,), f32, 1)
        BQ1 = c4((KC,))
        BK1 = c4((KC,))
        MX4 = c4((HEADS,))
        RO = c4((HEADS,))
        XFF = XF[:].rearrange("p t d -> p (t d)")
        c4f = Carve(0, XFF)
        Z4 = c4f((CT, D))
        Z4T = c4f((KC, CW))
        PT4 = c4f((HEADS, P), f32, LK)
        c4p = Carve(0, XFF)
        CT1, WK1, WV1 = c4p((KC, B * LK)), c4p((KC, D)), c4p((KC, D))
        KT1 = c4p((KC, B * LK))
        BV1 = c4p((D,))
        GB = Carve(gathered_at)((2, CT, 2, D))
        c4r = Carve(gathered_at + 4 * CT * D)
        WQ1, WO1 = c4r((KC, D)), c4r((KC, D))
        assert c4r.at <= 3 * E * KC * F1 // 2
        sc4_ps = PS[:, 0:3, 0:6 * LK]
        pT4_ps = PS[0:LK, 3:7, :].rearrange("p a (h n) -> p (a h) n", h=4)
        o4_ps = PS[:, 7, 0:HEADS * HW].rearrange("p (h n) -> p h n", h=HEADS)
        zT4_ps, q4_ps = PS[:, 3:5, :], PS[:, 5:7, :]
        out4_ps = PS[:, 5:7, :].rearrange("p a (t d) -> p (a t) d", t=2)
        SC4 = [(0, 0, 0, 0, 6), (1, 0, 0, 6, 2), (1, 2, 1, 0, 4), (2, 0, 1, 4, 4)]
        ld_4 = sem("ld_phase4")
        s_gath = [sem(f"gathered{n}") for n in range(2)]
        (k4_k, k4_ks, k4_kb, k4_v, k4_vs) = (sem("pre4_" + n) for n in ("k", "ks", "kbd", "v", "vs"))
        (q4_x, q4_var, q4_r, q4_z, q4_zT, q4_zTs, q4_q, q4_qs, q4_sc, q4_sub, q4_p, q4_pTa, q4_pTb, q4_pTas,
         q4_pTbs, q4_o, q4_on, q4_oT, q4_oTs, q4_out, q4_var3, q4_r3, q4_z3, q4_h, q4_z3T, q4_z3Ts, q4_g, q4_gs) = (
            sem("p4_" + n) for n in ("x", "var", "r", "z", "zT", "zTs", "q", "qs", "scores", "sub", "p",
                                     "pTa", "pTb", "pTas", "pTbs", "o", "on", "oT", "oTs", "out", "var3", "r3", "z3",
                                     "h", "z3T", "z3Ts", "g", "gs"))
        W1S = REG[:, 0:E * KC * F1].rearrange("p (e k f) -> p e k f", e=E, k=KC)
        W2S = REG[:, E * KC * F1:2 * E * KC * F1].rearrange("p (e k d) -> p e k d", e=E, k=FC1)
        EH = E // 2
        NB1, NB2 = E * F1, E * D
        c5 = Carve(0, XB)
        BPS = c5((NB1 + NB2,), bf16, PARTS)
        YB5 = c5((2, D))
        T5, SEL5, SELF5 = c5((NT, E)), c5((NT, E)), c5((NT, E), bf16)
        M5, IDF5 = c5((NT,)), c5((NT,))
        IDX5 = c5((NT,)).bitcast(u32)
        CN, NTL, CUM, OFFS = (c5((E,)) for _ in range(4))
        CMP = c5((E, NT))
        TEX = c5((NT1, E - 1), f32, 1)
        TEF, TEG = c5((NT1,), f32, 1), c5((NT1,), f32, 1)
        TEI, TEP = c5((NT1,), f32, 1).bitcast(i32), c5((NT1,), f32, 1).bitcast(i32)
        BBF = c5(((NB1 + NB2) // P,))
        BBR = c5(((NB1 + NB2) // P,))
        BBP = c5((PARTS, (NB1 + NB2) // P), bf16)
        c5f = Carve(0, XFF)
        XS5 = c5f((2, D))
        XT5 = c5f((2, KC, P))
        HS5 = c5f((2, F1))
        HT5 = c5f((FC1, P))
        ld_b, ld_b2, ld_bp = sem("ld_bias"), sem("bias_parts_out"), sem("ld_bias_parts")
        m5_out = [sem(f"p5_rows_out{n}") for n in range(2)]
        ld_xs = [sem(f"ld_xs{n}") for n in range(2)]
        s_gat5 = [sem(f"gathered5_{c}") for c in range(NCH)]
        (b5_p, r5_sel, r5_pos, r5_cnt, r5_idx, s_scat5, m5_xT, m5_xTs, m5_h, m5_hs, m5_hT, m5_hTs, m5_y, m5_ys, s_fin, s_out) = (
            sem("p5_" + n) for n in ("bias_parts", "sel", "pos", "count", "idx", "scattered", "xT", "xTs", "h", "hs", "hT", "hTs",
                                     "y", "ys", "final", "stored"))
        h5_ps = [PS[:, 2 * n:2 * n + 2, :] for n in range(2)]
        hT5_ps = PS[:, 4:6, :].rearrange("p a (f n) -> p (a f) n", f=4)
        xT5_ps = PS[:, 6, 0:KC * P].rearrange("p (k n) -> p k n", k=KC)
        y5_ps = PS[:, 7, 0:D]
        s_zero, s_fill = sem("zeros_made"), sem("dram_cleared")
        NFILL = -(-SLOTS0 // (4 * P)) + -(-SLOTS1 // (4 * P)) + 1
        FIRST = 1
        block = ctx.enter_context(nc.Block())

        zT_ps = PS[:, 0:2, :]
        sc_ps = PS[:, 2, :].rearrange("p (t k) -> p t k", t=CT)
        pT_ps = PS[0:LK, 3, :]
        o_ps = PS[:, 4:6, :].rearrange("p a (t d) -> p (a t) d", t=2)
        uT_ps = PS[:, 6:8, :]
        qk_ps = PS[:, 0:4, :].rearrange("p (a r) n -> p a r n", a=2)
        v_ps = o_ps

        @block.sync
        def _(sp):
            for primed in (s_qkst, m5_out[0], m5_out[1]):
                sp.sem_inc(primed, FIRST)
            sp.dma_start(CF[:], const_f_in).then_inc(ld_c, 16)
            sp.dma_start(CB[:], const_b_in).then_inc(ld_c, 16)
            for a, b in ((ctxT, ctxT_in), (wk0, wk0_in), (bk0, bk0_in), (bq0, bq0_in), (wq0T, wq0T_in),
                         (wv0, wv0_in), (bv0, bv0_in.partition_broadcast(P)), (wqk, wqk_in), (wv, wv_in),
                         (g1c, g1_in), (rope, rope_in)):
                sp.dma_start(a, b).then_inc(ld_w, 16)
            sp.dma_start(X[:], x_in.rearrange("b (t p) d -> p (b t) d", p=P)).then_inc(ld_x, 16)
            sp.wait_ge(s_zero, 1)
            for dram, n in ((xe_dram, SLOTS0), (xs_dram, SLOTS1)):
                for r0 in range(0, n, 4 * P):
                    m = min(4, (n - r0) // P)
                    sp.dma_start(dram[r0:r0 + m * P].rearrange("(a p) d -> p a d", p=P),
                                 ZERO[:, 0:m * D].rearrange("p (a d) -> p a d", a=m)).then_inc(s_fill, 16)
            sp.dma_start(ye_dram[SLOTS0:SLOTS0 + 1], ZERO[0:1, 0:D]).then_inc(s_fill, 16)
            with sp.Fori(0, B) as b:
                with sp.Fori(0, CPB) as cc:
                    sp.wait_ge(s_lo, b * CPB + cc + 1 + FIRST)
                    for a in range(2):
                        for n in range(PARTS):
                            for r in range(2):
                                dst = qk_dram[a, n, r].rearrange("s r t -> (s r) t")
                                sp.dma_start(dst[ds(b * P, P), ds(cc * CW, CW)], PARTB[:, n, a, r, :]).then_inc(s_qkst, 16)
            def load_qk(s, n):
                for r in range(len(Q_PART)):
                    for a, (buf, part) in enumerate(((QT, Q_PART[r]), (KT, K_PART[r]))):
                        for ri in range(2):
                            src = qk_dram[a, part, ri].rearrange("s (i h) t -> s i (h t)", h=GH)
                            row = HD * r + 8 * ri
                            sp.dma_start(buf[row:row + 8, n].rearrange("p h t -> p (h t)"),
                                         src[ds(s, 1)].squeeze(0) if not isinstance(s, int) else src[s]).then_inc(ld_qk[n], 16)

            def load_max_rows(s, n):
                sp.wait_ge(s_mt, s + 1)
                for p in range(PARTS):
                    sp.dma_start(QT[QROWS + p:QROWS + p + 1, n].rearrange("p h (i t) -> p (h i) t", t=P),
                                 MT[p * 32:(p + 1) * 32, :]).then_inc(s_mrow, 16)

            sp.wait_ge(s_qkst, 16 * 12 * NCH + FIRST)
            sp.wait_ge(s_v, NCH)
            sp.wait_ge(s_lo, NCH + FIRST)
            load_qk(0, 0)
            load_qk(1, 1)
            load_max_rows(0, 0)
            with sp.Fori(0, NS // 2 - 1) as it:
                for n in range(2):
                    s = 2 * it + n
                    load_max_rows(s + 1, 1 - n)
                    sp.wait_ge(s_sT, 2 * NSTG * (s + 1))
                    load_qk(s + 2, n)
            load_max_rows(NS - 1, 1)
            sp.wait_ge(s_fill, 16 * NFILL)
            for a, b in ((WO, wo_in), (G2, g2_in.partition_broadcast(P)), (WR, wr_in)):
                sp.dma_start(a, b).then_inc(ld_3, 16)

            def load_expert(e, n):
                sp.dma_start(W1E[:, n], w1e_in.rearrange("e (k p) f -> e p k f", p=P)[ds(e, 1)].squeeze(0)).then_inc(ld_we[n], 16)
                sp.dma_start(W2E[:, n], w2e_in.rearrange("e (k p) d -> e p k d", p=P)[ds(e, 1)].squeeze(0)).then_inc(ld_we[n], 16)

            def load_rows(e, n):
                sp.dma_start(XEB[:, n, 0:2], xe_dram[ds(e * CAP, 2 * P)].rearrange("(a p) d -> p a d", p=P)).then_inc(ld_xe[n], 16)
                sp.dma_start(XEB[0:TAIL, n, 2], xe_dram[ds(e * CAP + 2 * P, TAIL)]).then_inc(ld_xe[n], 16)

            load_expert(0, 0)
            load_expert(1, 1)
            sp.wait_ge(s_yn, 2 * NS)
            for e in range(E):
                sp.dma_start(REG[:, e * KC * F1:(e + 1) * KC * F1].rearrange("p (k f) -> p k f", k=KC),
                             w1_in.rearrange("e (k p) f -> e p k f", p=P)[e]).then_inc(ld_5, 16)
            sp.wait_ge(s_scat, 16 * 2 * NT)
            load_rows(0, 0)
            load_rows(1, 1)
            with sp.Fori(0, E // 2 - 1) as it:
                for n in range(2):
                    e = 2 * it + n
                    sp.wait_ge(me_y, e + 1)
                    load_expert(e + 2, n)
                    load_rows(e + 2, n)
            sp.wait_ge(p3_lg, NCH)
            sp.wait_ge(p3_lgs, NCH + FIRST)
            sp.wait_ge(me_y, E)
            sp.wait_ge(me_out, 32 * E + FIRST)
            for a, b in ((WQ1, wq1_in), (WO1, wo1_in)):
                sp.dma_start(a, b).then_inc(ld_4, 16)
            for a, b in ((BO, bo1_in.partition_broadcast(P)), (WG, wg_in), (BG, bg_in.unsqueeze(0)), (BQ1, bq1_in), (BK1, bk1_in),
                         (CT1, ctxT_in), (WK1, wk1_in), (WV1, wv1_in), (BV1, bv1_in.partition_broadcast(P))):
                sp.dma_start(a, b).then_inc(ld_4, 16)
            for e in range(E // 2):
                at = (3 * E // 2 + e) * KC * F1
                sp.dma_start(REG[:, at:at + KC * F1].rearrange("p (k d) -> p k d", d=D),
                             w2_in.rearrange("e (k p) d -> e p k d", p=P)[e]).then_inc(ld_5, 16)
            sp.wait_ge(q4_gs, NCH + FIRST)
            sp.wait_ge(q4_h, NCH + FIRST)
            sp.wait_ge(q4_out, NCH)
            for e in range(EH):
                sp.dma_start(W2S[:, e], w2_in.rearrange("e (k p) d -> e p k d", p=P)[EH + e]).then_inc(ld_5, 16)
            sp.dma_start(BBF[:, 0:NB1 // P], b1_in.rearrange("e f -> (e f)").rearrange("(p n) -> p n", p=P)).then_inc(ld_b, 16)
            sp.dma_start(BBF[:, NB1 // P:], b2_in.rearrange("e f -> (e f)").rearrange("(p n) -> p n", p=P)).then_inc(ld_b, 16)
            sp.wait_ge(b5_p, 1)
            for n in range(PARTS):
                sp.dma_start(bp_dram[n, 0:NB1].rearrange("(p n) -> p n", p=P), BBP[:, n, 0:NB1 // P]).then_inc(ld_b2, 16)
                sp.dma_start(bp_dram[n, NB1:].rearrange("(p n) -> p n", p=P), BBP[:, n, NB1 // P:]).then_inc(ld_b2, 16)
            sp.wait_ge(ld_b2, 16 * 2 * PARTS)
            sp.dma_start(BPS, bp_dram).then_inc(ld_bp, 16)
            sp.wait_ge(s_scat5, 16 * NT)

            def load_tile(j, n):
                sp.dma_start(XS5[:, n], xs_dram[ds(j * P, P)]).then_inc(ld_xs[n], 16)

            def send_tile(j, n):
                sp.wait_ge(m5_ys, j + 1 + FIRST)
                sp.dma_start(ys_dram[ds(j * P, P)], YB5[:, n]).then_inc(m5_out[n], 16)

            load_tile(0, 0)
            load_tile(1, 1)
            with sp.Fori(0, (NT1 - 3) // 2) as it:
                for n in range(2):
                    j = 2 * it + n
                    sp.wait_ge(m5_xT, j + 1)
                    load_tile(j + 2, n)
                    send_tile(j, n)
            sp.wait_ge(m5_xT, NT1 - 2)
            load_tile(NT1 - 1, 0)
            for j in range(NT1 - 3, NT1):
                send_tile(j, j % 2)
            for c in range(NCH):
                sp.wait_ge(s_fin, c + 1)
                sp.dma_start(out.rearrange("b (t p) d -> p (b t) d", p=P)[:, c * CT:(c + 1) * CT], X[:, c * CT:(c + 1) * CT, :]).then_inc(s_out, 16)
            sp.wait_ge(s_out, 16 * NCH)

        @block.gpsimd
        def _(pool):
            for primed in (s_lo, p3_xs, q4_h):
                pool.sem_inc(primed, FIRST)
            chain = Chain(pool, s_chp)
            nc.gpsimd.memset(ZERO, 0.0).then_inc(s_zero, 1)
            pool.wait_ge(ld_c, 32)
            with pool.Fori(0, NCH) as c:
                chain.enter(c, 7)
                pool.wait_ge(s_var, c + 1)
                nc.gpsimd.tensor_tensor(RSTD, VE, neg_half[:, 0:CT], ALU.pow).then_inc(s_rstd, 1)
                pool.wait_ge(s_var2, c + 1)
                chain(nc.gpsimd.tensor_tensor(R1, VE, neg_half[:, 0:CT], ALU.pow))
                chain(nc.gpsimd.tensor_tensor(TA, MV[:, :, 1], R1, ALU.mult))
                chain(nc.gpsimd.tensor_tensor(TV, TA, R1, ALU.mult), s_spare)
                chain(nc.gpsimd.tensor_scalar(TA, TV, RMS_EPS, None, ALU.add))
                chain(nc.gpsimd.tensor_tensor(R2, TA, neg_half[:, 0:CT], ALU.pow))
                nc.gpsimd.tensor_tensor(S1, R1, R2, ALU.mult).then_inc(s_rstd2, 1)
                pool.wait_ge(s_rt, c + 1 + FIRST)
                chain(nc.gpsimd.tensor_tensor(ROT[:, :, 0, :], RT[:, 0], RT[:, 1], ALU.subtract))
                nc.gpsimd.tensor_tensor(ROT[:, :, 1, :], RT[:, 2], RT[:, 3], ALU.add).then_inc(s_rot, 1)
                pool.wait_ge(s_hi, c + 1)
                flat = RT[:, 0:2].rearrange("p a b n -> p (a b n)")
                rot = ROT.rearrange("p a b n -> p (a b n)")
                part = PARTB.rearrange("p n a b m -> p n (a b m)")
                nc.gpsimd.tensor_tensor(flat, rot, part[:, 0], ALU.subtract).then_inc(s_res, 1)
                pool.wait_ge(s_mid, c + 1)
                chain(nc.gpsimd.tensor_tensor(part[:, 2], flat, part[:, 1], ALU.subtract))
                pool.sem_inc(s_lo, 1)
            chain.leave(NCH)
            pool.wait_ge(s_vs, NCH + FIRST)
            pool.wait_ge(s_v, NCH)
            pool.wait_ge(s_lo, NCH + FIRST)
            pool.wait_ge(s_qkst, 16 * 12 * NCH + FIRST)
            chain(nc.gpsimd.memset(VS, 0.0))
            chain(nc.gpsimd.memset(KT[QROWS:AROWS], 1.0))
            chain(nc.gpsimd.memset(VS[:, :, :, :, HD:HD + 1], 1.0))
            pool.sem_inc(s_ini, 1)

            def stage_v(s, n):
                nc.gpsimd.tensor_copy(VS[:, n, :, :, 0:HD],
                                      VB[:, ds(s, 1)].rearrange("p s t (h d) -> p (s t) h d", h=GH)).then_inc(s_vst, 1)

            stage_v(0, 0)
            stage_v(1, 1)
            with pool.Fori(0, NS // 2 - 1) as it:
                for n in range(2):
                    pool.wait_ge(s_y, 2 * (2 * it + n + 1))
                    pool.sem_inc(s_spare, 1)
                    stage_v(2 * it + n + 2, n)
            with pool.Fori(0, NCH) as c:
                pool.wait_ge(s_yn, 2 * NS)
                pool.wait_ge(s_fill, 16 * NFILL)
                pool.wait_ge(p3_yT, c + FIRST)
                pool.sem_inc(s_spare, 1)
                nc.gpsimd.tensor_copy(YC, XF[:, ds(c * CT, CT), :]).then_inc(p3_yc, 1)
                pool.wait_ge(p3_ms, c + 1)
                nc.gpsimd.tensor_tensor(R2, VE, neg_half[:, 0:CT], ALU.pow).then_inc(p3_r, 1)
                pool.wait_ge(p3_xc, c + 1)
                pool.sem_inc(s_spare, 1)
                nc.gpsimd.tensor_copy(XF[:, ds(c * CT, CT), :], XC).then_inc(p3_xs, 1)
            pool.wait_ge(p3_xs, NCH + FIRST)
            pool.wait_ge(rt_idx, 1)
            for t in range(NT):
                for idx in (IDX1, IDX2):
                    nc.gpsimd.indirect_dma_start(out=xe_dram, out_offset=bass.IndirectOffsetOnAxis(ap=idx[:, t:t + 1], axis=0),
                                                 in_=XF[:, t, :], in_offset=None, bounds_check=SLOTS0 - 1,
                                                 oob_is_err=False).then_inc(s_scat, 16)
            pool.wait_ge(me_out, 32 * E + FIRST)
            pool.wait_ge(s_fill, 16 * NFILL)

            def gather(c, n):
                for t in range(CT):
                    for a, idx in enumerate((IDX1, IDX2)):
                        nc.gpsimd.indirect_dma_start(out=GB[:, n, t, a, :], out_offset=None, in_=ye_dram,
                                                     in_offset=bass.IndirectOffsetOnAxis(ap=idx[:, c * CT + t:c * CT + t + 1], axis=0),
                                                     bounds_check=SLOTS0, oob_is_err=True).then_inc(s_gath[n], 16)

            gather(0, 0)
            gather(1, 1)
            for c in range(NCH):
                pool.wait_ge(q4_var, c + 1)
                nc.gpsimd.tensor_tensor(RSTD, VE, neg_half[:, 0:CT], ALU.pow).then_inc(q4_r, 1)
                if c + 2 < NCH:
                    pool.wait_ge(q4_x, c + 1)
                    gather(c + 2, c % 2)
                pool.wait_ge(q4_var3, c + 1)
                nc.gpsimd.tensor_tensor(RSTD, VE, neg_half[:, 0:CT], ALU.pow).then_inc(q4_r3, 1)
                pool.wait_ge(q4_z3, c + 1)
                nc.gpsimd.tensor_copy(H[:, c * CT:(c + 1) * CT, :], Z4).then_inc(q4_h, 1)
            pool.wait_ge(q4_h, NCH + FIRST)
            pool.wait_ge(r5_idx, 1)
            for t in range(NT):
                nc.gpsimd.indirect_dma_start(out=xs_dram, out_offset=bass.IndirectOffsetOnAxis(ap=IDX5[:, t:t + 1], axis=0),
                                             in_=H[:, t, :], in_offset=None, bounds_check=SLOTS1 - 1,
                                             oob_is_err=True).then_inc(s_scat5, 16)
            pool.wait_ge(s_scat5, 16 * NT)
            pool.wait_ge(m5_out[0], 16 * ((NT1 + 1) // 2) + FIRST)
            pool.wait_ge(m5_out[1], 16 * (NT1 // 2) + FIRST)
            for t in range(NT):
                nc.gpsimd.indirect_dma_start(out=H[:, t, :], out_offset=None, in_=ys_dram,
                                             in_offset=bass.IndirectOffsetOnAxis(ap=IDX5[:, t:t + 1], axis=0),
                                             bounds_check=SLOTS1 - 1, oob_is_err=True).then_inc(s_gat5[t // CT], 16)

        @block.scalar
        def _(act):
            for primed in (me_out, me_ys, s_vs, q4_pTas, q4_z3Ts, m5_hTs):
                act.sem_inc(primed, FIRST)
            for m in range(KC):
                act.wait_ge(pre_k, m + 1)
                nc.scalar.activation(KT0[:, m, :], PS[:, m, 0:B * LK], ACT.Identity, bias=bk0[:, m:m + 1]).then_inc(pre_ks, 1)
            act.wait_ge(pre_a, 1)
            nc.scalar.activation(A0, PS[:, 2:2 + KC, 0:B * LK], ACT.Copy)
            nc.scalar.activation(CB0, PS[0:1, 4, 0:B * LK], ACT.Copy).then_inc(pre_as, 1)
            with act.Fori(0, B) as b:
                with act.Fori(0, CPB) as cc:
                    c = b * CPB + cc
                    act.wait_ge(s_zT, c + 1)
                    nc.scalar.activation(ZT, zT_ps, ACT.Copy).then_inc(s_zTs, 1)
                    act.wait_ge(s_nb, c + 1)
                    for t in range(CT):
                        last = nc.scalar.activation(P0[:, t, 0:LK], sc_ps[:, t, 0:LK], ACT.Exp, bias=NB[:, t:t + 1],
                                                    scale=1.0 / 16.0, accum_out=RSUM[:, t:t + 1])
                    last.then_inc(s_p, 1)
                    act.wait_ge(s_pT, c + 1)
                    nc.scalar.activation(PT0, pT_ps, ACT.Copy).then_inc(s_pTs, 1)
                    act.wait_ge(s_uT, c + 1)
                    nc.scalar.activation(UT, uT_ps, ACT.Copy).then_inc(s_uTs, 1)
                    act.wait_ge(s_v, c + 1)
                    for t in range(CT):
                        last = nc.scalar.activation(
                            VB.rearrange("p (b g) t n -> p b t g n", b=B)[:, ds(b, 1), ds(cc * CT + t, 1)],
                            v_ps[:, t, :].rearrange("p (x y g n) -> p x y g n", x=1, y=1, g=NG), ACT.Copy)
                    last.then_inc(s_vs, 1)
                    act.wait_ge(s_rot, c + 1)
                    act.wait_ge(s_qkst, 16 * 12 * c + FIRST)
                    rot = ROT.rearrange("p a b n -> p (a b n)")
                    flat = RT[:, 0:2].rearrange("p a b n -> p (a b n)")
                    part = PARTB.rearrange("p n a b m -> p n (a b m)")
                    nc.scalar.activation(part[:, 0], rot, ACT.Copy).then_inc(s_hi, 1)
                    act.wait_ge(s_res, c + 1)
                    nc.scalar.activation(part[:, 1], flat, ACT.Copy).then_inc(s_mid, 1)
            def exps(s, n):
                for k, (c, j) in enumerate(STAGES):
                    q0 = q0_of(c, j)
                    act.wait_ge(s_pvd, NSTG * s + k + FIRST)
                    for pair in range(2):
                        act.wait_ge(s_sT, 2 * NSTG * s + 2 * k + pair + 1)
                        nc.scalar.activation(PB[:, k % 2, 2 * pair:2 * pair + 2, q0:CW], s_ps[pair][:, :, q0:CW],
                                             ACT.Exp, scale=0.25).then_inc(s_sfree, 1)

            act.wait_ge(s_v, NCH)
            act.wait_ge(s_lo, NCH + FIRST)
            act.wait_ge(s_qkst, 16 * 12 * NCH + FIRST)
            act.sem_inc(s_sfree, 2)
            with act.Fori(0, NS // 2) as it:
                for n in range(2):
                    exps(2 * it + n, n)
            with act.Fori(0, NCH) as c:
                act.wait_ge(p3_yT, c + 1 + FIRST)
                nc.scalar.activation(YCT, yT3_ps, ACT.Copy).then_inc(p3_yTs, 1)
                act.wait_ge(p3_xT, c + 1)
                nc.scalar.activation(XCT, xT3_ps, ACT.Copy).then_inc(p3_xTs, 1)
            act.wait_ge(rt_sub, 1)
            nc.scalar.activation(EX, TE1, ACT.Exp).then_inc(rt_exp, 1)

            def send_rows(e, n):
                act.dma_start(ye_dram[ds(e * CAP, 2 * P)].rearrange("(a p) d -> p a d", p=P), YEB[:, n, 0:2]).then_inc(me_out, 16)
                act.dma_start(ye_dram[ds(e * CAP + 2 * P, TAIL)], YEB[0:TAIL, n, 2]).then_inc(me_out, 16)

            def evac_xT(e, n):
                act.wait_ge(me_xT, e + 1)
                nc.scalar.activation(XET[:, n], xeT_ps, ACT.Copy).then_inc(me_xTs, 1)

            def expert_rows(e, n):
                act.wait_ge(me_y, e + 1)
                act.wait_ge(me_out, 32 * e + FIRST)
                nc.scalar.activation(YEB[:, n, 0:2], ye_ps[:, 0:2], ACT.Copy)
                nc.scalar.activation(YEB[0:TAIL, n, 2], ye_ps[0:TAIL, 2], ACT.Copy).then_inc(me_ys, 1)
                act.wait_ge(me_ys, e + 1 + FIRST)
                send_rows(e, n)

            evac_xT(0, 0)
            with act.Fori(0, E // 2 - 1) as it:
                for n in range(2):
                    evac_xT(2 * it + n + 1, 1 - n)
                    expert_rows(2 * it + n, n)
            evac_xT(E - 1, 1)
            expert_rows(E - 2, 0)
            expert_rows(E - 1, 1)
            act.wait_ge(ld_4, 16 * 11)
            for m in range(KC):
                act.wait_ge(k4_k, m + 1)
                nc.scalar.activation(KT1[:, m, :], PS[:, m, 0:B * LK], ACT.Identity, bias=BK1[:, m:m + 1]).then_inc(k4_ks, 1)
            with act.Fori(0, NCH) as c:
                act.wait_ge(q4_zT, c + 1)
                nc.scalar.activation(Z4T, zT4_ps, ACT.Copy).then_inc(q4_zTs, 1)
                act.wait_ge(q4_q, c + 1)
                for m in range(KC):
                    last = nc.scalar.activation(Q4T[:, m, :], q4_ps[:, m, :], ACT.Identity, bias=BQ1[:, m:m + 1])
                last.then_inc(q4_qs, 1)
                for t in range(CT):
                    act.wait_ge(q4_sub, c * CT + t + 1 + FIRST)
                    nc.scalar.activation(SS[:, t % 2], SS[:, t % 2], ACT.Exp, scale=0.25).then_inc(q4_p, 1)
                    act.wait_ge(q4_pTa, c * CT + t + 1)
                    nc.scalar.activation(PT4[:, 0:8, :], pT4_ps[:, 0:8, :], ACT.Copy).then_inc(q4_pTas, 1)
                act.wait_ge(q4_oT, c + 1)
                nc.scalar.activation(Z4T, zT4_ps, ACT.Copy).then_inc(q4_oTs, 1)
                act.wait_ge(q4_z3T, c + 1 + FIRST)
                nc.scalar.activation(Z4T, zT4_ps, ACT.Copy).then_inc(q4_z3Ts, 1)
            def evac_xT5(j, n):
                act.wait_ge(m5_xT, j + 1)
                nc.scalar.activation(XT5[:, n], xT5_ps, ACT.Copy).then_inc(m5_xTs, 1)

            def evac_hT5(j):
                act.wait_ge(m5_hT, j + 1)
                act.wait_ge(m5_y, j + FIRST)
                nc.scalar.activation(HT5, hT5_ps, ACT.Copy).then_inc(m5_hTs, 1)

            evac_xT5(0, 0)
            evac_xT5(1, 1)
            with act.Fori(0, (NT1 - 3) // 2) as it:
                for n in range(2):
                    evac_hT5(2 * it + n)
                    evac_xT5(2 * it + n + 2, n)
            evac_hT5(NT1 - 3)
            evac_xT5(NT1 - 1, 0)
            evac_hT5(NT1 - 2)
            evac_hT5(NT1 - 1)

        @block.vector
        def _(dve):
            for primed in (s_rt, s_yev, p3_lgs, q4_gs, q4_on, q4_sub, m5_ys):
                dve.sem_inc(primed, FIRST)
            chain = Chain(dve, s_chv)
            dve.wait_ge(ld_w, 16 * 11)
            for k in range(KC):
                nc.vector.tensor_scalar(wqk[:, k], wqk[:, k], g1c[:, k:k + 1], None, ALU.mult)
                last = nc.vector.tensor_scalar(wv[:, k], wv[:, k], g1c[:, k:k + 1], None, ALU.mult)
            last.then_inc(pre_w, 1)
            dve.wait_ge(pre_a, 1)
            nc.vector.tensor_tensor(V0, PS[0:LK, 5:7, 0:D], bv0[0:LK, :].unsqueeze(1).to_broadcast([LK, B, D]), ALU.add).then_inc(pre_w, 1)
            dve.wait_ge(ld_x, 16)
            with dve.Fori(0, B) as b:
                with dve.Fori(0, CPB) as cc:
                    c = b * CPB + cc
                    chain.enter(c, 8)
                    for t in range(CT):
                        last = nc.vector.bn_stats(ST[:, t, :].unsqueeze(1), X[:, ds(c * CT + t, 1), :])
                    chain(last, s_spare)
                    for t in range(CT):
                        last = nc.vector.bn_aggr(MV[:, t, :], ST[:, t, :])
                    chain(last)
                    nc.vector.tensor_scalar(VE, MV[:, :, 1], LN_EPS, None, ALU.add).then_inc(s_var, 1)
                    dve.wait_ge(s_rstd, c + 1)
                    for t in range(CT):
                        last = nc.vector.tensor_scalar(Z[:, t:t + 1, :], X[:, ds(c * CT + t, 1), :], MV[:, t, 0:1], RSTD[:, t:t + 1],
                                                       ALU.subtract, ALU.mult)
                    last.then_inc(s_z, 1)
                    dve.wait_ge(s_sc, c + 1)
                    chain(nc.vector.reduce_max(MX, sc_ps[:, :, 0:LK], AX.X))
                    nc.vector.tensor_scalar(NB, MX, -1.0 / 16.0, None, ALU.mult).then_inc(s_nb, 1)
                    dve.wait_ge(s_p, c + 1)
                    chain(nc.vector.reciprocal(RRS, RSUM))
                    dve.wait_ge(s_o, c + 1)
                    for t in range(CT):
                        xt = X[:, ds(c * CT + t, 1), :]
                        last = nc.vector.scalar_tensor_tensor(out=xt, in0=o_ps[:, t:t + 1, :], scalar=RRS[:, t:t + 1], in1=xt,
                                                              op0=ALU.mult, op1=ALU.add)
                    chain(last, s_spare)
                    for t in range(CT):
                        last = nc.vector.bn_stats(ST[:, t, :].unsqueeze(1), X[:, ds(c * CT + t, 1), :])
                    chain(last, s_spare)
                    for t in range(CT):
                        last = nc.vector.bn_aggr(MV[:, t, :], ST[:, t, :])
                    chain(last)
                    nc.vector.tensor_scalar(VE, MV[:, :, 1], LN_EPS, None, ALU.add).then_inc(s_var2, 1)
                    dve.wait_ge(s_rstd2, c + 1)
                    for t in range(CT):
                        last = nc.vector.tensor_scalar(U[:, t:t + 1, :], X[:, ds(c * CT + t, 1), :], MV[:, t, 0:1], S1[:, t:t + 1],
                                                       ALU.subtract, ALU.mult)
                    last.then_inc(s_u, 1)
                    for t in range(CT):
                        last = nc.vector.tensor_scalar(H[:, ds(c * CT + t, 1), :], X[:, ds(c * CT + t, 1), :], MV[:, t, 0:1], R1[:, t:t + 1],
                                                       ALU.subtract, ALU.mult)
                    chain(last)
                    dve.wait_ge(s_qk, c + 1)
                    dve.wait_ge(s_lo, c + FIRST)
                    for n, (r, t) in enumerate(((0, 0), (1, 1), (0, 1), (1, 0))):
                        table = rope[:, t:t + 1, ds(cc * CW, CW)].to_broadcast([P, 2, CW])
                        last = nc.vector.tensor_tensor(RT[:, n], qk_ps[:, :, r, :], table, ALU.mult)
                    last.then_inc(s_rt, 1)
            chain.leave(NCH)
            def reduce_unit(s, u):
                i, h0, nh, k0, w, masked = UNITS[u]
                dve.wait_ge(s_mx, NU * s + u + 1)
                src = m_ps[u % 2][:, 0:nh * w].rearrange("p (h w) -> p h w", h=nh)
                last = nc.vector.reduce_max(MXP[:, h0:h0 + nh, i, int(not masked)], src, AX.X)
                last.then_inc(s_mfree, 1)

            def max_parts(s):
                dve.wait_ge(s_mfree, NU * (s + 1) + 2)
                chain(nc.vector.reduce_max(NR, MXP, AX.X))
                chain(nc.vector.tensor_scalar(NM, NR, -1.0, None, ALU.mult))
                chain(nc.vector.tensor_copy(MP[:, 0], NM))
                chain(nc.vector.tensor_tensor(NR, NM, MP[:, 0], ALU.subtract))
                chain(nc.vector.tensor_copy(MP[:, 1], NR))
                nc.vector.tensor_tensor(MP[:, 2], NR, MP[:, 1], ALU.subtract).then_inc(s_mp, 1)

            def max_rows(s):
                dve.wait_ge(s_mpt, s + 1)
                dve.wait_ge(s_mrow, 16 * PARTS * s)
                nc.vector.tensor_copy(MT[0:96], t_ps.bitcast(bf16)[0:96, 0:P]).then_inc(s_mt, 1)

            def evac_y(s, c):
                dve.wait_ge(s_y, 2 * s + c + 1)
                nc.vector.tensor_copy(YT[:, c], y_ps).then_inc(s_yev, 1)

            def norm_y(s, c, b_, g):
                dve.wait_ge(s_yt, 2 * s + c + 1)
                back = t_ps.rearrange("p (t h d) -> p t h d", t=CT, h=GH)
                chain(nc.vector.reciprocal(RY, back[:, :, :, HD]))
                dst = XF.rearrange("p t (s x) -> p t s x", s=NG)
                for t in range(CT):
                    last = nc.vector.tensor_tensor(
                        dst[:, ds(b_ * NK + c * CT + t, 1), ds(g, 1), :].rearrange("p a b (h d) -> p (a b) h d", h=GH),
                        back[:, t:t + 1, :, 0:HD].rearrange("p a h d -> p a h d"),
                        RY[:, t:t + 1, :].unsqueeze(3).to_broadcast([P, 1, GH, HD]), ALU.mult)
                last.then_inc(s_yn, 1)

            dve.wait_ge(s_lo, NCH + FIRST)
            dve.wait_ge(s_rt, NCH + FIRST)
            dve.wait_ge(s_qkst, 16 * 12 * NCH + FIRST)
            chain(nc.vector.memset(MXP, -3.0e38))
            dve.sem_inc(s_mfree, 2)
            for u in range(NU):
                reduce_unit(0, u)
            max_parts(0)
            max_rows(0)

            def dve_step(s, b_, g, nxt):
                for k in range(NSTG):
                    if nxt:
                        for u in range(PER_STAGE * k, min(NU, PER_STAGE * (k + 1))):
                            reduce_unit(s + 1, u)
                    if k == 5:
                        evac_y(s, 0)
                    if k == 7:
                        norm_y(s, 0, b_, g)
                    if nxt and k == NSTG - 3:
                        max_parts(s + 1)
                        max_rows(s + 1)
                evac_y(s, 1)
                norm_y(s, 1, b_, g)

            STEP = 2 + 5
            with dve.Fori(0, B - 1) as b_:
                with dve.Fori(0, NG) as g:
                    chain.enter(b_ * NG + g, STEP)
                    dve_step(b_ * NG + g, b_, g, True)
            chain.leave((B - 1) * NG)
            with dve.Fori(0, NG - 1) as g:
                chain.enter(g, STEP)
                dve_step((B - 1) * NG + g, B - 1, g, True)
            chain.leave(NG - 1)
            dve_step(NS - 1, B - 1, NG - 1, False)
            dve.wait_ge(ld_3, 48)
            with dve.Fori(0, NCH) as c:
                chain.enter(c, 4)
                hc = H[:, ds(c * CT, CT), :]
                dve.wait_ge(p3_o, c + 1)
                chain(nc.vector.tensor_tensor(hc, o3_ps, hc, ALU.add), s_spare)
                for t in range(CT):
                    last = nc.vector.bn_stats(ST[:, t, :].unsqueeze(1), H[:, ds(c * CT + t, 1), :])
                chain(last, s_spare)
                for t in range(CT):
                    last = nc.vector.bn_aggr(MV[:, t, :], ST[:, t, :])
                chain(last)
                chain(nc.vector.tensor_tensor(TV, MV[:, :, 0], MV[:, :, 0], ALU.mult))
                nc.vector.scalar_tensor_tensor(out=VE, in0=TV, scalar=RMS_EPS, in1=MV[:, :, 1], op0=ALU.add, op1=ALU.add).then_inc(p3_ms, 1)
                dve.wait_ge(p3_r, c + 1)
                dve.wait_ge(p3_xs, c + FIRST)
                for t in range(CT):
                    last = nc.vector.scalar_tensor_tensor(out=XC[:, t:t + 1, :], in0=H[:, ds(c * CT + t, 1), :], scalar=R2[:, t:t + 1],
                                                          in1=G2.unsqueeze(1), op0=ALU.mult, op1=ALU.mult)
                last.then_inc(p3_xc, 1)
                dve.wait_ge(p3_lg, c + 1)
                nc.vector.tensor_copy(LG[:, ds(c * CT, CT), :], lg_ps).then_inc(p3_lgs, 1)
            chain.leave(NCH)

            def over_e(a):
                return a.unsqueeze(2).to_broadcast([P, NT, E])

            def over_t(a):
                return a.unsqueeze(1).to_broadcast([P, NT, E])

            def first_max(src, top, sel, tmp):
                chain(nc.vector.reduce_max(top, src, AX.X))
                chain(nc.vector.tensor_tensor(tmp, src, over_e(top), ALU.is_equal))
                chain(nc.vector.tensor_tensor(tmp, tmp, over_t(w8), ALU.mult))
                chain(nc.vector.reduce_max(VM, tmp, AX.X))
                chain(nc.vector.tensor_tensor(sel, tmp, over_e(VM), ALU.is_equal))

            dve.wait_ge(p3_lgs, NCH + FIRST)
            chain(nc.vector.reduce_max(M1, LG[:], AX.X))
            nc.vector.tensor_tensor(TE1, LG[:], over_e(M1), ALU.subtract).then_inc(rt_sub, 1)
            dve.wait_ge(rt_exp, 1)
            chain(nc.vector.reduce_sum(SU, EX, AX.X))
            chain(nc.vector.reciprocal(RSU, SU))
            chain(nc.vector.tensor_tensor(PR, EX, over_e(RSU), ALU.mult))
            first_max(PR, M1, SEL1, TE1)
            chain(nc.vector.scalar_tensor_tensor(out=TE2, in0=SEL1, scalar=-4.0, in1=PR, op0=ALU.mult, op1=ALU.add))
            first_max(TE2, M2, SEL2, TE1)
            chain(nc.vector.tensor_tensor(TE1, SEL1, SEL2, ALU.add))
            chain(nc.vector.tensor_tensor(G, TE1, PR, ALU.mult))
            chain(nc.vector.memset(CUR, 0.0))
            chain(nc.vector.tensor_copy(BIT, top_bit))
            with dve.Fori(0, BITS) as i:
                chain.enter(i, 5)
                chain(nc.vector.tensor_tensor(CAND.bitcast(i32), CUR.bitcast(i32), BIT.bitcast(i32), ALU.bitwise_or))
                nc.vector.tensor_tensor(GEb, G, over_t(CAND), ALU.is_ge).then_inc(rt_ge, 1)
                chain(nc.vector.tensor_scalar(BIT.bitcast(i32), BIT.bitcast(i32), 1, None, ALU.logical_shift_right))
                dve.wait_ge(rt_cnt, i + 1)
                chain(nc.vector.reduce_sum(CNT, cnt_ps.rearrange("p t e -> p e t"), AX.X))
                chain(nc.vector.scalar_tensor_tensor(out=TK, in0=CNT, scalar=CAP - 0.5, in1=CAND, op0=ALU.is_ge, op1=ALU.mult))
                chain(nc.vector.tensor_tensor(CUR, CUR, TK, ALU.max))
            chain.leave(BITS)
            chain(nc.vector.tensor_tensor(TE1, G, over_t(CUR), ALU.is_equal))
            chain(nc.vector.scalar_tensor_tensor(out=EQb, in0=G, scalar=0.0, in1=TE1, op0=ALU.is_gt, op1=ALU.mult))
            nc.vector.tensor_tensor(GEb, G, over_t(CUR), ALU.is_gt).then_inc(rt_gt, 1)
            dve.wait_ge(rt_ngt, 1)
            chain(nc.vector.reduce_sum(CNT, cnt_ps.rearrange("p t e -> p e t"), AX.X))
            chain(nc.vector.tensor_scalar(NGT, CNT, -1.0, float(CAP), ALU.mult, ALU.add))
            chain(nc.vector.tensor_tensor(TE1, pfx_ps, over_t(NGT), ALU.is_lt))
            chain(nc.vector.tensor_tensor(TE2, TE1, EQb, ALU.mult))
            chain(nc.vector.tensor_tensor(KEEPb, TE2, GEb, ALU.add))
            dve.sem_inc(rt_keep, 1)
            dve.wait_ge(rt_pos, 1)
            chain(nc.vector.tensor_tensor(TE1, pos_ps, over_t(base0), ALU.add))
            chain(nc.vector.tensor_tensor(TE1, TE1, KEEPb, ALU.mult))
            for sel, top, gate, idx in ((SEL1, M1, GATE1, IDX1), (SEL2, M2, GATE2, IDX2)):
                chain(nc.vector.tensor_tensor(TE2, TE1, sel, ALU.mult))
                chain(nc.vector.reduce_sum(IDF, TE2, AX.X))
                chain(nc.vector.tensor_scalar(idx, IDF, float(SLOTS0), None, ALU.add))
                chain(nc.vector.tensor_tensor(TE2, KEEPb, sel, ALU.mult))
                chain(nc.vector.reduce_sum(IDF, TE2, AX.X))
                chain(nc.vector.tensor_tensor(gate, IDF, top, ALU.mult))
            dve.sem_inc(rt_idx, 1)
            with dve.Fori(0, E) as e:
                dve.wait_ge(me_h, e + 1)
                nc.vector.tensor_scalar(HTE, he_ps, 0.0, None, ALU.max).then_inc(me_hs, 1)
            dve.wait_ge(ld_4, 16 * 11)
            dve.wait_ge(k4_ks, KC)
            for b in range(B):
                for k in range(KC):
                    for h in range(8):
                        last = nc.vector.tensor_scalar(KBD[:, b, k, h, :], KT1[:, k, b * LK:(b + 1) * LK], headmask[:, h:h + 1], None, ALU.mult)
            last.then_inc(k4_kb, 1)
            dve.wait_ge(k4_v, 1)
            nc.vector.memset(V1, 1.0).then_inc(k4_vs, 1)
            dve.wait_ge(k4_vs, 1)
            for b in range(B):
                last = nc.vector.tensor_tensor(V1[:, b, :, 0:HD], PS[0:LK, 2 + b, 0:D].rearrange("p (h d) -> p h d", h=HEADS),
                                               BV1[0:LK].rearrange("p (h d) -> p h d", h=HEADS), ALU.add)
            last.then_inc(k4_vs, 1)

            def stats(c, ready):
                for t in range(CT):
                    last = nc.vector.bn_stats(ST[:, t, :].unsqueeze(1), X[:, ds(c * CT + t, 1), :])
                chain(last, s_spare)
                for t in range(CT):
                    last = nc.vector.bn_aggr(MV[:, t, :], ST[:, t, :])
                chain(last)
                nc.vector.tensor_scalar(VE, MV[:, :, 1], LN_EPS, None, ALU.add).then_inc(ready, 1)

            def normed(c, ready):
                for t in range(CT):
                    last = nc.vector.tensor_scalar(Z4[:, t:t + 1, :], X[:, ds(c * CT + t, 1), :], MV[:, t, 0:1], RSTD[:, t:t + 1],
                                                   ALU.subtract, ALU.mult)
                last.then_inc(ready, 1)

            def subtract_max(c, t):
                dve.wait_ge(q4_sc, c * CT + t + 1)
                ab = sc4_ps[:, 0:2].rearrange("p a (h k) -> p a h k", h=6)
                cc_ = sc4_ps[:, 2, 0:4 * LK].rearrange("p (h k) -> p h k", h=4)
                nc.vector.reduce_max(MX4[:, 0:12], ab, AX.X)
                chain(nc.vector.reduce_max(MX4[:, 12:16], cc_, AX.X))
                for a in range(2):
                    nc.vector.tensor_tensor(SS[:, t % 2, 6 * a:6 * a + 6, :], ab[:, a], MX4[:, 6 * a:6 * a + 6].unsqueeze(2).to_broadcast([P, 6, LK]), ALU.subtract)
                nc.vector.tensor_tensor(SS[:, t % 2, 12:16, :], cc_, MX4[:, 12:16].unsqueeze(2).to_broadcast([P, 4, LK]), ALU.subtract).then_inc(q4_sub, 1)

            with dve.Fori(0, NCH // 2) as it:
                chain.enter(it, 2 * (5 + 2 * CT + 4))
                for n in range(2):
                    c = 2 * it + n
                    dve.wait_ge(s_gath[n], 16 * 2 * CT * (it + 1))
                    for a, gate in enumerate((GATE1, GATE2)):
                        for t in range(CT):
                            ht = H[:, ds(c * CT + t, 1), :]
                            last = nc.vector.scalar_tensor_tensor(out=ht, in0=GB[:, n, t, a:a + 1, :], scalar=gate[:, ds(c * CT + t, 1)], in1=ht,
                                                                  op0=ALU.mult, op1=ALU.add)
                        chain(last)
                    chain(nc.vector.tensor_tensor(X[:, ds(c * CT, CT), :], X[:, ds(c * CT, CT), :], H[:, ds(c * CT, CT), :], ALU.add))
                    dve.sem_inc(q4_x, 1)
                    stats(c, q4_var)
                    dve.wait_ge(q4_r, c + 1)
                    dve.wait_ge(q4_h, c + FIRST)
                    dve.wait_ge(q4_z3T, c + FIRST)
                    dve.wait_ge(k4_v, 1)
                    normed(c, q4_z)
                    subtract_max(c, 0)
                    for t in range(CT):
                        if t + 1 < CT:
                            subtract_max(c, t + 1)
                        dve.wait_ge(q4_pTb, c * CT + t + 1)
                        nc.vector.tensor_copy(PT4[:, 8:16, :], pT4_ps[:, 8:16, :]).then_inc(q4_pTbs, 1)
                        dve.wait_ge(q4_o, c * CT + t + 1)
                        chain(nc.vector.reciprocal(RO, o4_ps[:, :, HD]))
                        nc.vector.tensor_tensor(Z4[:, t, :].rearrange("p (h d) -> p h d", h=HEADS), o4_ps[:, :, 0:HD],
                                                RO.unsqueeze(2).to_broadcast([P, HEADS, HD]), ALU.mult).then_inc(q4_on, 1)
                    dve.wait_ge(q4_out, c + 1)
                    xc = X[:, ds(c * CT, CT), :]
                    chain(nc.vector.tensor_tensor(xc, out4_ps, xc, ALU.add))
                    chain(nc.vector.tensor_tensor(xc, xc, BO.unsqueeze(1).to_broadcast([P, CT, D]), ALU.add), s_spare)
                    stats(c, q4_var3)
                    dve.wait_ge(q4_r3, c + 1)
                    normed(c, q4_z3)
                    dve.wait_ge(q4_g, c + 1)
                    nc.vector.tensor_copy(LG[:, ds(c * CT, CT), :], o4_ps[:, :, :].rearrange("p h n -> p (h n)")[:, 0:CT * E].rearrange("p (t e) -> p t e", t=CT)).then_inc(q4_gs, 1)
            chain.leave(NCH // 2)
            dve.wait_ge(q4_gs, NCH + FIRST)
            dve.wait_ge(q4_g, NCH)
            chain(nc.vector.reduce_max(M5, LG[:], AX.X))
            chain(nc.vector.tensor_tensor(T5, LG[:], over_e(M5), ALU.is_equal))
            chain(nc.vector.tensor_tensor(T5, T5, over_t(w8), ALU.mult))
            chain(nc.vector.reduce_max(M5, T5, AX.X))
            chain(nc.vector.tensor_tensor(SEL5, T5, over_e(M5), ALU.is_equal))
            nc.vector.tensor_copy(SELF5, SEL5).then_inc(r5_sel, 1)
            dve.wait_ge(r5_cnt, 1)
            chain(nc.vector.reduce_sum(CN, cnt_ps.rearrange("p t e -> p e t"), AX.X))
            chain(nc.vector.tensor_tensor(CMP, CN.unsqueeze(2).to_broadcast([P, E, NT]), j128.unsqueeze(1).to_broadcast([P, E, NT]), ALU.is_gt))
            chain(nc.vector.reduce_sum(NTL, CMP, AX.X))
            chain(nc.vector.tensor_copy(CUM[:, 0:1], NTL[:, 0:1]))
            for e in range(1, E):
                chain(nc.vector.tensor_tensor(CUM[:, e:e + 1], CUM[:, e - 1:e], NTL[:, e:e + 1], ALU.add))
            chain(nc.vector.tensor_tensor(OFFS, CUM, NTL, ALU.subtract))
            chain(nc.vector.tensor_scalar(OFFS, OFFS, float(P), None, ALU.mult))
            dve.wait_ge(r5_pos, 1)
            chain(nc.vector.tensor_tensor(T5, pos_ps, over_t(OFFS), ALU.add))
            chain(nc.vector.tensor_tensor(T5, T5, SEL5, ALU.mult))
            chain(nc.vector.reduce_sum(IDF5, T5, AX.X))
            nc.vector.tensor_copy(IDX5, IDF5).then_inc(r5_idx, 1)
            chain(nc.vector.tensor_tensor(TEX, CUM[0:1, 0:E - 1].unsqueeze(1).to_broadcast([1, NT1, E - 1]),
                                          jt.unsqueeze(2).to_broadcast([1, NT1, E - 1]), ALU.is_le))
            chain(nc.vector.reduce_sum(TEF, TEX, AX.X))
            chain(nc.vector.tensor_scalar(TEG, TEF, EH - 0.5, -float(E), ALU.is_ge, ALU.mult))
            chain(nc.vector.tensor_copy(TEI, TEF))
            nc.vector.scalar_tensor_tensor(out=TEP, in0=TEF, scalar=float(EH), in1=TEG, op0=ALU.add, op1=ALU.add).then_inc(r5_idx, 1)
            dve.wait_ge(ld_b, 32)
            chain(nc.vector.tensor_copy(BBP[:, 0], BBF))
            chain(nc.vector.tensor_tensor(BBR, BBF, BBP[:, 0], ALU.subtract))
            chain(nc.vector.tensor_copy(BBP[:, 1], BBR))
            nc.vector.tensor_tensor(BBP[:, 2], BBR, BBP[:, 1], ALU.subtract).then_inc(b5_p, 1)

            def relu5(j, n):
                dve.wait_ge(m5_h, j + 1)
                nc.vector.tensor_scalar(HS5[:, n], h5_ps[n].rearrange("p a f -> p (a f)"), 0.0, None, ALU.max).then_inc(m5_hs, 1)

            def evac_y5(j, n, it):
                dve.wait_ge(m5_y, j + 1 + FIRST)
                dve.wait_ge(m5_out[n], 16 * it + FIRST)
                nc.vector.tensor_copy(YB5[:, n], y5_ps).then_inc(m5_ys, 1)

            relu5(0, 0)
            with dve.Fori(0, (NT1 - 3) // 2) as it:
                for n in range(2):
                    relu5(2 * it + n + 1, 1 - n)
                    evac_y5(2 * it + n, n, it)
            relu5(NT1 - 2, 1)
            evac_y5(NT1 - 3, 0, (NT1 - 3) // 2)
            relu5(NT1 - 1, 0)
            evac_y5(NT1 - 2, 1, (NT1 - 3) // 2)
            evac_y5(NT1 - 1, 0, (NT1 - 1) // 2)
            for c in range(NCH):
                dve.wait_ge(s_gat5[c], 16 * CT)
                xc = X[:, c * CT:(c + 1) * CT, :]
                nc.vector.tensor_tensor(xc, xc, H[:, c * CT:(c + 1) * CT, :], ALU.add).then_inc(s_fin, 1)

        @block.tensor
        def _(pe):
            for primed in (s_pvd, m5_y, q4_z3T, p3_yT):
                pe.sem_inc(primed, FIRST)
            pe.wait_ge(ld_c, 32)
            pe.wait_ge(ld_w, 16 * 11)
            for m in range(KC):
                for k in range(KC):
                    last = nc.tensor.matmul(PS[:, m, 0:B * LK], wk0[:, k, m * P:(m + 1) * P], ctxT[:, k, :],
                                            start=(k == 0), stop=(k == KC - 1))
                last.then_inc(pre_k, 1)
            pe.wait_ge(pre_ks, KC)
            for m in range(KC):
                for k in range(KC):
                    nc.tensor.matmul(PS[:, 2 + m, 0:B * LK], wq0T[:, k, m * P:(m + 1) * P], KT0[:, k, :],
                                     start=(k == 0), stop=(k == KC - 1))
            for k in range(KC):
                nc.tensor.matmul(PS[0:1, 4, 0:B * LK], bq0[:, k:k + 1], KT0[:, k, :], start=(k == 0), stop=(k == KC - 1))
            for b in range(B):
                for k in range(KC):
                    last = nc.tensor.matmul(PS[0:LK, 5 + b, 0:D], ctxT[:, k, b * LK:(b + 1) * LK], wv0[:, k, :],
                                            start=(k == 0), stop=(k == KC - 1))
            last.then_inc(pre_a, 1)
            pe.wait_ge(pre_as, 1)
            pe.wait_ge(pre_w, 2)
            with pe.Fori(0, B) as b:
                with pe.Fori(0, CPB) as cc:
                    c = b * CPB + cc
                    pe.wait_ge(s_z, c + 1)
                    pe.wait_ge(s_rt, c + FIRST)
                    for t in range(CT):
                        for k in range(KC):
                            last = nc.tensor.transpose(zT_ps[:, k, t * P:(t + 1) * P], Z[:, t, k * P:(k + 1) * P], ident)
                    last.then_inc(s_zT, 1)
                    pe.wait_ge(s_zTs, c + 1)
                    for t in range(CT):
                        for k in range(KC):
                            nc.tensor.matmul(sc_ps[:, t, 0:LK], ZT[:, k, t * P:(t + 1) * P], A0[:, k, ds(b * LK, LK)],
                                             start=(k == 0), stop=False)
                        last = nc.tensor.matmul(sc_ps[:, t, 0:LK], ones_row, CB0[:, ds(b * LK, LK)], start=False, stop=True)
                    last.then_inc(s_sc, 1)
                    pe.wait_ge(s_p, c + 1)
                    for t in range(CT):
                        last = nc.tensor.transpose(pT_ps[:, t * P:(t + 1) * P], P0[:, t, 0:LK], ident)
                    last.then_inc(s_pT, 1)
                    pe.wait_ge(s_pTs, c + 1)
                    pe.wait_ge(s_vs, c + FIRST)
                    for t in range(CT):
                        last = nc.tensor.matmul(o_ps[:, t:t + 1, :], PT0[:, t * P:(t + 1) * P], V0[:, ds(b, 1), :],
                                                start=True, stop=True)
                    last.then_inc(s_o, 1)
                    pe.wait_ge(s_u, c + 1)
                    for t in range(CT):
                        for k in range(KC):
                            last = nc.tensor.transpose(uT_ps[:, k, t * P:(t + 1) * P], U[:, t, k * P:(k + 1) * P], ident)
                    last.then_inc(s_uT, 1)
                    pe.wait_ge(s_uTs, c + 1)
                    for a in range(2):
                        for r in range(2):
                            for k in range(KC):
                                m = 2 * a + r
                                last = nc.tensor.matmul(qk_ps[:, a, r, :], wqk[:, k, m * P:(m + 1) * P], UT[:, k, :],
                                                        start=(k == 0), stop=(k == KC - 1))
                    last.then_inc(s_qk, 1)
                    for t in range(CT):
                        for k in range(KC):
                            last = nc.tensor.matmul(v_ps[:, t, :], UT[:, k, t * P:(t + 1) * P], wv[:, k, :],
                                                    start=(k == 0), stop=(k == KC - 1))
                    last.then_inc(s_v, 1)
            def max_unit(s, n, u):
                i, h0, nh, k0, w, masked = UNITS[u]
                pe.wait_ge(s_mfree, NU * s + u + 1)
                for h in range(nh):
                    dst = m_ps[u % 2][:, h * w:(h + 1) * w]
                    last = nc.tensor.matmul(dst, QT[0:QROWS, n, h0 + h, i * P:(i + 1) * P],
                                            KT[0:QROWS, n, h0 + h, k0:k0 + w], start=True, stop=not masked)
                    if masked:
                        last = nc.tensor.matmul(dst[:, w - P:w], identb, mask_q, start=False, stop=True)
                last.then_inc(s_mx, 1)

            def scores(s, n, k):
                c, j = STAGES[k]
                q0 = q0_of(c, j)
                for pair in range(2):
                    pe.wait_ge(s_sfree, 2 * NSTG * s + 2 * k + pair + 1)
                    for h in range(2):
                        hh = 2 * pair + h
                        dst = s_ps[pair][:, h, q0:CW]
                        masked = j >= CT * c
                        last = nc.tensor.matmul(dst, KT[0:AROWS, n, hh, j * P:(j + 1) * P],
                                                QT[0:AROWS, n, hh, c * CW + q0:(c + 1) * CW], start=True, stop=not masked)
                        if masked:
                            last = nc.tensor.matmul(dst[:, 0:P], identb, mask_k, start=False, stop=True)
                    last.then_inc(s_sT, 1)

            def weighted(s, n, k):
                c, j = STAGES[k]
                q0 = q0_of(c, j)
                if j == 0:
                    pe.wait_ge(s_yev, 2 * s + c + FIRST)
                pe.wait_ge(s_sfree, 2 * NSTG * s + 2 * k + 4)
                for h in range(GH):
                    last = nc.tensor.matmul(PS[VW * h:VW * (h + 1), 6, q0:CW], VS[:, n, j, h, :], PB[:, k % 2, h, q0:CW],
                                            start=(j == 0), stop=(j == CT * (c + 1) - 1))
                last.then_inc(s_pvd, 1)
                if j == CT * (c + 1) - 1:
                    pe.wait_ge(s_pvd, NSTG * s + k + 2 + FIRST)
                    pe.sem_inc(s_y, 1)

            def back(s, c):
                pe.wait_ge(s_yev, 2 * s + c + 1 + FIRST)
                for t in range(CT):
                    last = nc.tensor.transpose(t_ps[:, t * P:(t + 1) * P], YT[:, c, t * P:(t + 1) * P], ident)
                last.then_inc(s_yt, 1)

            def parts_T(s):
                pe.wait_ge(s_mp, s + 1)
                nc.tensor.transpose(t_ps.bitcast(bf16)[0:96, 0:P], MP.rearrange("p n h i -> p (n h i)"), identb).then_inc(s_mpt, 1)

            def pe_step(s, n, nxt, it):
                pe.wait_ge(s_mrow, 16 * PARTS * (s + 1))
                pe.wait_ge(s_vst, s + 1)
                if nxt:
                    pe.wait_ge(ld_qk[1 - n], 16 * NLD * (it + 1 + n))
                for k in range(NSTG):
                    scores(s, n, k)
                    if nxt:
                        for u in range(PER_STAGE * k, min(NU, PER_STAGE * (k + 1))):
                            max_unit(s + 1, 1 - n, u)
                    if k:
                        weighted(s, n, k - 1)
                    if k == 6:
                        back(s, 0)
                    if nxt and k == NSTG - 2:
                        pe.wait_ge(s_yn, 2 * s + 1)
                        parts_T(s + 1)
                weighted(s, n, NSTG - 1)
                if nxt:
                    pe.wait_ge(s_mt, s + 2)
                back(s, 1)

            pe.sem_inc(s_pvd, 1)
            pe.wait_ge(s_ini, 1)
            pe.wait_ge(s_rt, NCH + FIRST)
            pe.wait_ge(s_vs, NCH + FIRST)
            pe.wait_ge(ld_qk[0], 16 * NLD)
            for u in range(NU):
                max_unit(0, 0, u)
            parts_T(0)
            with pe.Fori(0, NS // 2 - 1) as it:
                for n in range(2):
                    pe_step(2 * it + n, n, True, it)
            pe_step(NS - 2, 0, True, NS // 2 - 1)
            pe_step(NS - 1, 1, False, NS // 2 - 1)
            pe.wait_ge(ld_3, 48)
            pe.wait_ge(s_yn, 2 * NS)
            with pe.Fori(0, NCH) as c:
                pe.wait_ge(p3_yc, c + 1)
                for t in range(CT):
                    for k in range(KC):
                        last = nc.tensor.transpose(yT3_ps[:, k, t * P:(t + 1) * P], YC[:, t, k * P:(k + 1) * P], ident)
                last.then_inc(p3_yT, 1)
                pe.wait_ge(p3_yTs, c + 1)
                for t in range(CT):
                    for k in range(KC):
                        last = nc.tensor.matmul(o3_ps[:, t, :], YCT[:, k, t * P:(t + 1) * P], WO[:, k, :], start=(k == 0), stop=(k == KC - 1))
                last.then_inc(p3_o, 1)
                pe.wait_ge(p3_xc, c + 1)
                for t in range(CT):
                    for k in range(KC):
                        last = nc.tensor.transpose(xT3_ps[:, k, t * P:(t + 1) * P], XC[:, t, k * P:(k + 1) * P], ident)
                last.then_inc(p3_xT, 1)
                pe.wait_ge(p3_xTs, c + 1)
                pe.wait_ge(p3_lgs, c + FIRST)
                for t in range(CT):
                    for k in range(KC):
                        last = nc.tensor.matmul(lg_ps[:, t, :], XCT[:, k, t * P:(t + 1) * P], WR[:, k, :], start=(k == 0), stop=(k == KC - 1))
                last.then_inc(p3_lg, 1)

            def prefix(dst, ones_zeros, done):
                nc.tensor.matmul(dst, tri_b, ones_zeros, start=True, stop=False)
                for d in range(1, NT):
                    last = nc.tensor.matmul(dst[:, d:NT, :], ones_b, ones_zeros[:, 0:NT - d, :], start=False, stop=(d == NT - 1))
                last.then_inc(done, 1)

            with pe.Fori(0, BITS) as i:
                pe.wait_ge(rt_ge, i + 1)
                nc.tensor.matmul(cnt_ps, ones_b, GEb, start=True, stop=True).then_inc(rt_cnt, 1)
            pe.wait_ge(rt_gt, 1)
            prefix(pfx_ps, EQb, rt_eqT)
            nc.tensor.matmul(cnt_ps, ones_b, GEb, start=True, stop=True).then_inc(rt_ngt, 1)
            pe.wait_ge(rt_keep, 1)
            prefix(pos_ps, KEEPb, rt_pos)

            def rows_T(n, count):
                pe.wait_ge(ld_xe[n], 32 * count)
                for t, w in ((0, P), (1, P), (2, TAIL)):
                    for k in range(KC):
                        last = nc.tensor.transpose(xeT_ps[:, k, t * P:t * P + w], XEB[0:w, n, t, k * P:(k + 1) * P], ident[0:w, 0:w])
                last.then_inc(me_xT, 1)

            pe.wait_ge(rt_idx, 1)
            rows_T(0, 1)

            def expert_mlp(e, n, it, nxt):
                pe.wait_ge(me_xTs, e + 1)
                pe.wait_ge(ld_we[n], 32 * (it + 1))
                for f in range(FC0):
                    for k in range(KC):
                        last = nc.tensor.matmul(he_ps[:, f, :], W1E[:, n, k, f * P:(f + 1) * P], XET[:, n, k, :], start=(k == 0), stop=(k == KC - 1))
                last.then_inc(me_h, 1)
                if nxt:
                    rows_T(1 - n, it + 1 + n)
                pe.wait_ge(me_hs, e + 1)
                pe.wait_ge(me_ys, e + FIRST)
                for t, w in ((0, P), (1, P), (2, TAIL)):
                    for f in range(FC0):
                        last = nc.tensor.matmul(ye_ps[0:w, t, :], HTE[:, f, t * P:t * P + w], W2E[:, n, f, :], start=(f == 0), stop=(f == FC0 - 1))
                last.then_inc(me_y, 1)

            with pe.Fori(0, E // 2 - 1) as it:
                for n in range(2):
                    expert_mlp(2 * it + n, n, it, True)
            expert_mlp(E - 2, 0, E // 2 - 1, True)
            expert_mlp(E - 1, 1, E // 2 - 1, False)
            pe.wait_ge(ld_4, 16 * 11)
            pe.wait_ge(me_hs, E)
            for m in range(KC):
                for k in range(KC):
                    last = nc.tensor.matmul(PS[:, m, 0:B * LK], WK1[:, k, m * P:(m + 1) * P], CT1[:, k, :], start=(k == 0), stop=(k == KC - 1))
                last.then_inc(k4_k, 1)
            for b in range(B):
                for k in range(KC):
                    last = nc.tensor.matmul(PS[0:LK, 2 + b, 0:D], CT1[:, k, b * LK:(b + 1) * LK], WV1[:, k, :], start=(k == 0), stop=(k == KC - 1))
            last.then_inc(k4_v, 1)
            pe.wait_ge(k4_kb, 1)
            pe.wait_ge(k4_vs, 2)
            pe.wait_ge(me_ys, E + FIRST)

            def rows_T4(done):
                for t in range(CT):
                    for k in range(KC):
                        last = nc.tensor.transpose(zT4_ps[:, k, t * P:(t + 1) * P], Z4[:, t, k * P:(k + 1) * P], ident)
                last.then_inc(done, 1)

            with pe.Fori(0, B) as b:
                with pe.Fori(0, CPB) as cc:
                    c = b * CPB + cc

                    def scores4(t):
                        pe.wait_ge(q4_sub, c * CT + t + FIRST)
                        for bank, off, k, h0, nh in SC4:
                            last = nc.tensor.matmul(sc4_ps[:, bank, off * LK:(off + nh) * LK], Q4T[:, k, t * P:(t + 1) * P],
                                                    KBD[:, ds(b, 1), k, h0:h0 + nh, :].rearrange("p b h k -> p (b h) k"), start=True, stop=True)
                        last.then_inc(q4_sc, 1)

                    pe.wait_ge(q4_z, c + 1)
                    pe.wait_ge(q4_pTas, c * CT + FIRST)
                    pe.wait_ge(q4_z3Ts, c + FIRST)
                    rows_T4(q4_zT)
                    pe.wait_ge(q4_zTs, c + 1)
                    for m in range(KC):
                        for k in range(KC):
                            last = nc.tensor.matmul(q4_ps[:, m, :], WQ1[:, k, m * P:(m + 1) * P], Z4T[:, k, :], start=(k == 0), stop=(k == KC - 1))
                    last.then_inc(q4_q, 1)
                    pe.wait_ge(q4_qs, c + 1)
                    scores4(0)
                    for t in range(CT):
                        n = c * CT + t
                        if t + 1 < CT:
                            scores4(t + 1)
                        pe.wait_ge(q4_p, n + 1)
                        for half, done in ((0, q4_pTa), (1, q4_pTb)):
                            for h in range(8 * half, 8 * half + 8):
                                last = nc.tensor.transpose(pT4_ps[:, h, :], SS[:, t % 2, h, :], ident)
                            last.then_inc(done, 1)
                        pe.wait_ge(q4_pTas, n + 1 + FIRST)
                        pe.wait_ge(q4_on, n + FIRST)
                        pe.wait_ge(q4_gs, c + FIRST)
                        for h in range(HEADS):
                            if h == 8:
                                pe.wait_ge(q4_pTbs, n + 1)
                            last = nc.tensor.matmul(o4_ps[:, h, :], PT4[:, h, :], V1[:, ds(b, 1), h, :].squeeze(1), start=True, stop=True)
                        last.then_inc(q4_o, 1)
                    pe.wait_ge(q4_on, (c + 1) * CT + FIRST)
                    rows_T4(q4_oT)
                    pe.wait_ge(q4_oTs, c + 1)
                    for t in range(CT):
                        for k in range(KC):
                            last = nc.tensor.matmul(out4_ps[:, t, :], Z4T[:, k, t * P:(t + 1) * P], WO1[:, k, :], start=(k == 0), stop=(k == KC - 1))
                    last.then_inc(q4_out, 1)
                    pe.wait_ge(q4_z3, c + 1)
                    rows_T4(q4_z3T)
                    pe.wait_ge(q4_z3Ts, c + 1 + FIRST)
                    gate_ps = PS[:, 7, 0:CT * E].rearrange("p (t e) -> p t e", t=CT)
                    for t in range(CT):
                        for k in range(KC):
                            nc.tensor.matmul(gate_ps[:, t, :], Z4T[:, k, t * P:(t + 1) * P], WG[:, k, :], start=(k == 0), stop=False)
                        last = nc.tensor.matmul(gate_ps[:, t, :], ones_row, BG, start=False, stop=True)
                    last.then_inc(q4_g, 1)
            pe.wait_ge(q4_gs, NCH + FIRST)
            pe.wait_ge(r5_sel, 1)
            nc.tensor.matmul(cnt_ps, ones_b, SELF5, start=True, stop=True).then_inc(r5_cnt, 1)
            prefix(pos_ps, SELF5, r5_pos)

            def xT5(j, n, it):
                pe.wait_ge(ld_xs[n], 16 * (it + 1))
                pe.wait_ge(m5_xTs, j)
                for k in range(KC):
                    last = nc.tensor.transpose(xT5_ps[:, k, :], XS5[:, n, k * P:(k + 1) * P], ident)
                last.then_inc(m5_xT, 1)

            def h5(j, n):
                pe.wait_ge(m5_xTs, j + 1)
                pe.sem_inc(s_spare, 1)
                e = pe.value_load(TEI[0:1, ds(j, 1)], min_val=0, max_val=E - 1)
                for f in range(F1 // 512):
                    for k in range(KC):
                        nc.tensor.matmul(h5_ps[n][:, f, :], XT5[:, n, k, :],
                                         W1S[:, ds(e, 1), k, f * 512:(f + 1) * 512].squeeze(1), start=(k == 0), stop=False)
                    last = nc.tensor.matmul(h5_ps[n][:, f, :], ones3, BPS[:, ds(e * F1 + f * 512, 512)], start=False, stop=True)
                last.then_inc(m5_h, 1)

            def hT5(j, n):
                pe.wait_ge(m5_hs, j + 1)
                pe.wait_ge(m5_hTs, j + FIRST)
                for f in range(FC1):
                    last = nc.tensor.transpose(hT5_ps[:, f, :], HS5[:, n, f * P:(f + 1) * P], ident)
                last.then_inc(m5_hT, 1)

            def y5(j):
                pe.wait_ge(m5_hTs, j + 1 + FIRST)
                pe.wait_ge(m5_ys, j + FIRST)
                pe.sem_inc(s_spare, 1)
                e = pe.value_load(TEI[0:1, ds(j, 1)], min_val=0, max_val=E - 1)
                at = pe.value_load(TEP[0:1, ds(j, 1)], min_val=0, max_val=E - 1)
                for f in range(FC1):
                    nc.tensor.matmul(y5_ps, HT5[:, f, :], W2S[:, ds(at, 1), f, :].squeeze(1), start=(f == 0), stop=False)
                nc.tensor.matmul(y5_ps, ones3, BPS[:, ds(e * D + NB1, D)], start=False, stop=True).then_inc(m5_y, 1)

            pe.wait_ge(r5_idx, 2)
            xT5(0, 0, 0)
            pe.wait_ge(ld_bp, 16)
            pe.wait_ge(ld_5, 16 * 2 * E)
            h5(0, 0)
            xT5(1, 1, 0)
            with pe.Fori(0, (NT1 - 3) // 2) as it:
                for n in range(2):
                    j = 2 * it + n
                    hT5(j, n)
                    h5(j + 1, 1 - n)
                    xT5(j + 2, n, it + 1)
                    y5(j)
            last_it = (NT1 - 1) // 2
            hT5(NT1 - 3, 0)
            h5(NT1 - 2, 1)
            xT5(NT1 - 1, 0, last_it)
            y5(NT1 - 3)
            hT5(NT1 - 2, 1)
            h5(NT1 - 1, 0)
            y5(NT1 - 2)
            hT5(NT1 - 1, 0)
            y5(NT1 - 1)


def _consts(D, S, NT, E, CAP):
    import numpy as np
    P = 128
    i = np.arange(P)
    cf = np.zeros((P, 3 * P + 96), np.float32)
    cf[:, 0:P] = np.eye(P)
    cf[:, P:2 * P] = i[:, None] < i[None, :]
    cf[:, 2 * P:3 * P] = 1.0
    o = 3 * P
    cf[:, o:o + E] = E - np.arange(E)
    cf[:, o + E:o + 2 * E] = np.arange(E) * CAP - E * CAP
    cf[:, o + 2 * E:o + 2 * E + 16] = P * np.arange(16)
    cf[:, o + 32:o + 32 + NT + E - 1] = np.arange(NT + E - 1)
    cf[:, o + 64:o + 64 + NT] = -0.5
    cf[:, o + 80:o + 88] = (i[:, None] // 16) == np.arange(8)[None, :]
    cf[:, o + 88:o + 96] = 2.0 ** -63
    cb = np.zeros((P, 5 * P), np.float32)
    cb[:, 0:P] = np.eye(P)
    cb[:, P:2 * P] = np.where(i[None, :] > i[:, None], -1.0e30, 0.0)
    cb[:, 2 * P:3 * P] = np.where(i[:, None] > i[None, :], -1.0e30, 0.0)
    cb[:, 3 * P:4 * P] = 1.0
    cb[:, 4 * P:5 * P] = i[:, None] < i[None, :]
    theta = (10000.0 ** (-2.0 * (np.arange(8, dtype=np.float32) / np.float32(16)))).astype(np.float32)
    pair = (i % 32) // 4
    angle = (np.arange(S, dtype=np.float32)[None, :] * theta[pair][:, None]).astype(np.float32).astype(np.float64)
    rope = np.stack([np.cos(angle), np.sin(angle)], 1).astype(np.float32)
    return cf, cb.astype(mybir.dt.np(mybir.dt.bfloat16)), rope


def _lay_out(i):
    import numpy as np
    P = 128

    def rows(w):
        return w.reshape(-1, P, w.shape[1]).transpose(1, 0, 2)

    def column(v):
        return v.reshape(-1, P).T

    x, ctx = i["x"], i["ctx_1024"]
    D = x.shape[2]
    cf, cb, rope = _consts(D, x.shape[1], x.shape[0] * x.shape[1] // P, 8, 320)
    wqkv = i["L0_ffn_w_qkv"]
    p = np.arange(P)
    g, pair, hh = p // 32, (p % 32) // 4, p % 4
    cols = [a * D + (4 * g + hh) * 16 + 2 * pair + r for a in range(2) for r in range(2)]
    wqk = wqkv[:, np.concatenate(cols)]
    return dict(
        x=x, ctxT=rows(ctx.transpose(2, 0, 1).reshape(D, -1)), const_f=cf, const_b=cb, rope=rope,
        wq0T=rows(i["L0_xattn_Wq"].T), bq0=column(i["L0_xattn_bq"]), wk0=rows(i["L0_xattn_Wk"]),
        bk0=column(i["L0_xattn_bk"]), wv0=rows(i["L0_xattn_Wv"]), bv0=i["L0_xattn_bv"],
        g1=column(i["L0_ffn_g1"]), wqk=rows(wqk), wv=rows(wqkv[:, 2 * D:]), wo=rows(i["L0_ffn_w_o"]),
        g2=i["L0_ffn_g2"], wr=rows(i["L0_ffn_w_router"]), w1e=i["L0_ffn_w1"], w2e=i["L0_ffn_w2"],
        wq1=rows(i["L1_xattn_Wq"].T), bq1=column(i["L1_xattn_bq"]), wk1=rows(i["L1_xattn_Wk"].T),
        bk1=column(i["L1_xattn_bk"]), wv1=rows(i["L1_xattn_Wv"].T), bv1=i["L1_xattn_bv"],
        wo1=rows(i["L1_xattn_Wo"].T), bo1=i["L1_xattn_bo"], wg=rows(i["L1_ffn_Wg"]), bg=i["L1_ffn_bg"],
        w1=i["L1_ffn_W1"], b1=i["L1_ffn_b1"], w2=i["L1_ffn_W2"], b2=i["L1_ffn_b2"])


def kernel(**inputs):
    import numpy as _np
    import concourse.bacc as _bacc
    from concourse import mybir as _mybir
    from concourse.bass_utils import run_bass_kernel_spmd as _run

    nc = _bacc.Bacc("TRN2", target_bir_lowering=False, num_devices=1)
    arrays, args = {}, []
    for name, a in _lay_out({k: _np.asarray(v) for k, v in inputs.items()}).items():
        a = _np.ascontiguousarray(a)
        arrays[name + "_dram"] = a
        args.append(nc.dram_tensor(name + "_dram", a.shape, _mybir.dt.from_np(a.dtype), kind="ExternalInput").ap())
    shape = inputs["x"].shape
    args.append(nc.dram_tensor("out_dram", shape, _mybir.dt.float32, kind="ExternalOutput").ap())
    build_program(nc, *args)
    r = _run(nc, [arrays], core_ids=[0])
    return r.results[0]["out_dram"]
```

```python
import concourse.bass as bass
from concourse import mybir
from contextlib import ExitStack


class Chain:

    def __init__(self, eng, sem):
        self.eng, self.sem, self.base, self.n, self.i, self.per = eng, sem, 0, 0, None, 0

    def value(self):
        at = self.base + self.n
        return at if self.i is None else self.i * self.per + at

    def enter(self, i, per):
        self.base, self.n, self.i, self.per = self.base + self.n, 0, i, per

    def leave(self, passes):
        assert self.n == self.per, (self.n, self.per)
        self.base, self.n, self.i = self.base + passes * self.per, 0, None

    def __call__(self, ins, alone=None):
        self.n += 1
        ins.then_inc(self.sem, 1)
        self.eng.wait_ge(self.sem, self.value())
        if alone:
            self.eng.sem_inc(alone, 1)


def build_program(nc, x_in, ctxT_in, const_f_in, const_b_in, rope_in,
                  wq0T_in, bq0_in, wk0_in, bk0_in, wv0_in, bv0_in,
                  g1_in, wqk_in, wv_in, wo_in, g2_in, wr_in, w1e_in, w2e_in,
                  wq1_in, bq1_in, wk1_in, bk1_in, wv1_in, bv1_in, wo1_in, bo1_in,
                  wg_in, bg_in, w1_in, b1_in, w2_in, b2_in, out):
    f32, bf16 = mybir.dt.float32, mybir.dt.bfloat16
    i32, u32 = mybir.dt.int32, mybir.dt.uint32
    ALU, ACT, AX = mybir.AluOpType, mybir.ActivationFunctionType, mybir.AxisListType
    ds = bass.ds

    P = 128
    B, S, D = x_in.shape
    KC = D // P
    NT = B * S // P
    CT = 4
    CW = CT * P
    CPB = S // CW
    NCH = B * CPB
    LK = ctxT_in.shape[2] // B
    HEADS, HD = 16, 16
    GH = 4
    NG = HEADS // GH
    NS = B * NG
    PARTS = 3
    RUNS = (3, 2, 1)
    QROWS = sum(RUNS) * HD
    AROWS = QROWS + PARTS
    E = 8
    F0 = w1e_in.shape[2]
    FC0 = F0 // P
    CAP = 320
    SLOTS0 = E * CAP
    F1 = w1_in.shape[2]
    FC1 = F1 // P
    NT1 = NT + E - 1
    SLOTS1 = NT1 * P
    BUFS = 3
    VW = 32
    NEG = -1.0e30
    LN_EPS, RMS_EPS = 1e-5, 1e-6

    ctx = ExitStack()
    with ctx:
        def sb(name, shape, dt=f32):
            return ctx.enter_context(nc.sbuf_tensor(name, shape, dt))

        def sem(name):
            return ctx.enter_context(nc.semaphore(name))

        qk_dram = nc.dram_tensor("qk_dram", (2, NS, PARTS, 2, 32, S), bf16, kind="Internal").ap()
        xe_dram = nc.dram_tensor("xe_dram", (SLOTS0, D), f32, kind="Internal").ap()
        ye_dram = nc.dram_tensor("ye_dram", (SLOTS0 + 1, D), f32, kind="Internal").ap()
        xs_dram = nc.dram_tensor("xs_dram", (SLOTS1, D), f32, kind="Internal").ap()
        ys_dram = nc.dram_tensor("ys_dram", (SLOTS1, D), f32, kind="Internal").ap()
        bp_dram = nc.dram_tensor("bp_dram", (PARTS, E * (F1 + D)), bf16, kind="Internal").ap()

        X = sb("X", [P, NT, D])
        H = sb("H", [P, NT, D])
        XF = sb("XF", [P, NT, D])
        CF = sb("CF", [P, const_f_in.shape[1]])
        CB = sb("CB", [P, const_b_in.shape[1]], bf16)
        ident = CF[:, 0:P]
        ones_mat = CF[:, 2 * P:3 * P]
        CO = 3 * P
        w8 = CF[:, CO:CO + E]
        base0 = CF[:, CO + E:CO + 2 * E]
        j128 = CF[:, CO + 2 * E:CO + 2 * E + 16]
        jt = CF[0:1, CO + 32:CO + 32 + NT1]
        neg_half = CF[:, CO + 64:CO + 64 + NT]
        headmask = CF[:, CO + 80:CO + 88]
        ones_row = CF[0:1, 2 * P:3 * P]
        identb = CB[:, 0:P]
        mask_q = CB[:, P:2 * P]
        mask_k = CB[:, 2 * P:3 * P]
        ones_b = CB[:, 3 * P:4 * P]
        tri_b = CB[:, 4 * P:5 * P]
        ones3 = CB[0:PARTS, 3 * P:4 * P]
        top_bit = CF[:, CO + 88:CO + 96]

        REG = sb("REG", [P, 2 * E * KC * F1])

        class Carve:
            def __init__(self, at=0, buf=None):
                self.at, self.buf = at, REG if buf is None else buf

            def __call__(self, shape, dt=f32, parts=P):
                n = 1
                for m in shape:
                    n *= m
                words = n if dt == f32 else n // 2
                a = self.buf[0:parts, self.at:self.at + words]
                self.at += words
                assert self.at <= self.buf.shape[1], self.at
                if dt != f32:
                    a = a.bitcast(dt)
                names = "abcd"[:len(shape)]
                if len(shape) > 1:
                    a = a.rearrange(f"p ({' '.join(names)}) -> p {' '.join(names)}",
                                    **{k: m for k, m in zip(names[1:], shape[1:])})
                return a

        c1 = Carve()
        VB = c1((NS, S // P, GH * HD))
        after_v = c1.at
        ctxT = c1((KC, B * LK))
        wq0T, wk0, wv0 = c1((KC, D)), c1((KC, D)), c1((KC, D))
        bq0, bk0, g1c = c1((KC,)), c1((KC,)), c1((KC,))
        bv0 = c1((D,))
        KT0 = c1((KC, B * LK))
        A0 = c1((KC, B * LK))
        CB0 = c1((B * LK,), f32, 1)
        V0 = c1((B, D), f32, LK)
        wqk, wv = c1((KC, 4 * P)), c1((KC, D))
        rope = c1((2, S))
        Z = c1((CT, D))
        ZT = c1((KC, CW))
        P0 = c1((CT, LK + 1))
        PT0 = c1((CW,), f32, LK)
        U = c1((CT, D))
        UT = c1((KC, CW))
        RT = c1((4, 2, CW))
        ROT = c1((2, 2, CW))
        PARTB = c1((PARTS, 2, 2, CW), bf16)
        c2 = Carve(after_v)
        QT = c2((BUFS, GH, S), bf16)
        KT = c2((BUFS, GH, S), bf16)
        PB = c2((2, GH, CW))
        VS = c2((BUFS, S // P, GH, VW))
        YT = c2((2, CW))
        MXP = c2((GH, 2 * CT, 2))
        NM = c2((GH, 2 * CT))
        NR = c2((GH, 2 * CT))
        MP = c2((PARTS, GH, 2 * CT), bf16)
        MT = c2((P,), bf16)
        RY = c2((CT, GH))
        ST = sb("ST", [P, CT, 6])
        MV = sb("MV", [P, CT, 2])
        SM = sb("SM", [P, 12, CT])
        VE, RSTD, MX, NB, RSUM, RRS, R1, R2, S1, TV, TA = (SM[:, n, :] for n in range(11))
        LG = sb("LG", [P, NT, E])

        XB = sb("XB", [P, 6900])
        ZERO = XB[:, 0:4 * D]

        PS = ctx.enter_context(nc.psum_tensor("PS", [P, 8, 512], f32))

        s_spare = sem("spare")
        ld_x, ld_c, ld_w = sem("ld_x"), sem("ld_consts"), sem("ld_weights1")
        s_chv, s_chp = sem("vector_chain"), sem("pool_chain")
        pre_k, pre_ks, pre_a, pre_as, pre_w = (sem("pre_" + n) for n in ("k", "ks", "a", "as", "w"))
        (s_var, s_rstd, s_z, s_zT, s_zTs, s_sc, s_nb, s_p, s_pT, s_pTs, s_o, s_var2, s_rstd2, s_u, s_uT, s_uTs,
         s_qk, s_v, s_rt, s_vs, s_rot, s_hi, s_res, s_mid, s_lo, s_qkst) = (
            sem("p1_" + n) for n in ("var", "rstd", "z", "zT", "zTs", "sc", "nb", "p", "pT", "pTs", "o", "var2",
                                     "rstd2", "u", "uT", "uTs", "qk", "v", "rt", "vs", "rot", "hi", "res", "mid",
                                     "lo", "qkst"))
        NK = S // P
        UNITS = []
        for i in range(NK):
            w = (i % CT + 1) * P
            per = max(1, 512 // w) if w != 3 * P else 1
            for h0 in range(0, GH, per):
                UNITS.append((i, h0, per, (i // CT) * CW, w, True))
            if i >= CT:
                for h0 in range(GH):
                    UNITS.append((i, h0, 1, 0, CW, False))
        NU = len(UNITS)
        STAGES = [(c, j) for c in range(CPB) for j in range(CT * (c + 1))]
        NSTG = len(STAGES)

        def q0_of(c, j):
            return max(0, P * (j - CT * c))

        def share():
            cost = [nh * w for _, _, nh, _, w, _ in UNITS]
            width = [CW - q0_of(c, j) for c, j in STAGES[:NSTG - 2]]
            cut, done, u = [0], 0, 0
            for k in range(NSTG - 2):
                done += width[k] * sum(cost) / sum(width)
                while u < NU and sum(cost[:u]) + cost[u] / 2 <= done:
                    u += 1
                cut.append(u)
            assert u == NU
            return cut + [NU, NU]

        CUT = share()

        NLD = 2 * len(RUNS)
        m_ps = [PS[:, n, :] for n in range(2)]
        s_ps = [PS[:, 2 + 2 * n:4 + 2 * n, :] for n in range(2)]
        y_ps = PS[:, 6, :]
        t_ps = PS[:, 7, :]
        s_ones = sem("ones_rows")
        ld_qk = [sem(f"ld_qk{n}") for n in range(BUFS)]
        (s_ini, s_mx, s_mfree, s_mp, s_mpt, s_mt, s_mrow, s_sT, s_sfree, s_pvd, s_y, s_yev, s_yt, s_yn, s_vst) = (
            sem("p2_" + n) for n in ("init", "max_scores", "max_bank_free", "maxparts", "maxparts_T", "maxT",
                                     "maxrows", "scoresT", "exp_done", "pv_done", "y", "y_evac", "y_T", "y_norm",
                                     "v_staged"))

        c3 = Carve(0, XB)
        WO = c3((KC, D))
        G2 = c3((D,))
        WR = c3((KC, E))
        YC = c3((CT, D))
        YCT = c3((KC, CW))
        XC = c3((CT, D))
        XCT = c3((KC, CW))
        c3r = Carve(E * KC * F1)
        PR, G, SEL1, SEL2, TE1, TE2, EX = (c3r((NT, E)) for _ in range(7))
        GEb, EQb, KEEPb = (c3r((NT, E), bf16) for _ in range(3))
        M1, M2, VM, SU, RSU, GATE1, GATE2, IDF = (c3r((NT,)) for _ in range(8))
        CUR, CAND, CNT, TK, BIT, NGT = (c3r((E,)) for _ in range(6))
        IDX1, IDX2 = (c3r((NT,)).bitcast(u32) for _ in range(2))
        gathered_at = c3r.at
        XEB = c3r((2, 3, D))
        XET = c3r((2, KC, CAP))
        HTE = c3r((FC0, CAP))
        c3r.at = max(c3r.at, c2.at)
        W1E = c3r((2, KC, F0))
        W2E = c3r((2, FC0, D))
        YEB = c3r((2, 3, D))
        TAIL = CAP - 2 * P
        ld_5 = sem("ld_last_experts")
        ld_3, ld_we, ld_xe = sem("ld_phase3"), [sem(f"ld_we{n}") for n in range(2)], [sem(f"ld_xe{n}") for n in range(2)]
        (p3_yc, p3_yT, p3_yTs, p3_o, p3_ms, p3_r, p3_xc, p3_xs, p3_xT, p3_xTs, p3_lg, p3_lgs) = (
            sem("p3_" + n) for n in ("yc", "yT", "yTs", "o", "ms", "r", "xc", "xs", "xT", "xTs", "lg", "lgs"))
        (rt_sub, rt_exp, rt_ge, rt_cnt, rt_gt, rt_ngt, rt_keep, rt_pos, rt_idx, rt_eqT) = (
            sem("route_" + n) for n in ("sub", "exp", "ge", "count", "gt", "gt_count", "keep", "pos", "idx", "eq_prefix"))
        s_scat = sem("scattered")
        (me_xT, me_xTs, me_h, me_hs, me_y, me_ys, me_out) = (
            sem("moe0_" + n) for n in ("xT", "xTs", "h", "hs", "y", "ys", "out"))
        BITS = 30
        yT3_ps, o3_ps = PS[:, 0:2, :], PS[:, 2:4, :].rearrange("p a (t d) -> p (a t) d", t=2)
        xT3_ps, lg_ps = PS[:, 4:6, :], PS[:, 6, 0:CT * E].rearrange("p (t e) -> p t e", t=CT)
        cnt_ps = PS[:, 0, 0:NT * E].rearrange("p (t e) -> p t e", t=NT)
        pfx_ps = PS[:, 1, 0:NT * E].rearrange("p (t e) -> p t e", t=NT)
        pos_ps = PS[:, 2, 0:NT * E].rearrange("p (t e) -> p t e", t=NT)
        xeT_ps = PS[:, 0:2, 0:CAP]
        he_ps = PS[:, 2:6, 0:CAP]
        ye_ps = PS[:, 6:8, :].rearrange("p a (t d) -> p (a t) d", t=2)
        HW = HD + 1
        SCW = LK * HEADS
        c4 = Carve(0, XB)
        KBD = c4((B, KC, 8, LK))
        V1 = c4((B, HEADS, HW), f32, LK)
        SS = c4((2, HEADS, LK))
        BO = c4((D,))
        WG = c4((KC, E))
        BG = c4((E,), f32, 1)
        BQ1 = c4((KC,))
        BK1 = c4((KC,))
        MX4 = c4((HEADS,))
        RO = c4((HEADS,))
        XFF = XF[:].rearrange("p t d -> p (t d)")
        c4f = Carve(0, XFF)
        Z4 = c4f((CT, D))
        Z4T = c4f((KC, CW))
        PT4 = c4f((HEADS, P), f32, LK)
        c4p = Carve(0, XFF)
        CT1, WK1, WV1 = c4p((KC, B * LK)), c4p((KC, D)), c4p((KC, D))
        KT1 = c4p((KC, B * LK))
        BV1 = c4p((D,))
        c4r = Carve(gathered_at)
        GB = c4r((CT, 2, D))
        WQ1, WO1 = c4r((KC, D)), c4r((KC, D))
        O4 = c4r((CT, D))
        Q4T = c4r((2, KC, CW))
        assert c4r.at <= 3 * E * KC * F1 // 2
        sc4_ps = PS[:, 0:3, 0:6 * LK]
        QH = 4
        NQ = HEADS // QH
        pT4_ps = [PS[0:LK, 3 + n, :].rearrange("p (h n) -> p h n", h=QH) for n in range(2)]
        o4_ps = PS[:, 5, 0:HEADS * HW].rearrange("p (h n) -> p h n", h=HEADS)
        zT4_ps = q4_ps = PS[:, 6:8, :]
        out4_ps = PS[:, 6:8, :].rearrange("p a (t d) -> p (a t) d", t=2)
        gate_ps = PS[:, 6, 0:CT * E].rearrange("p (t e) -> p t e", t=CT)
        SC4 = [(0, 0, 0, 0, 6), (1, 0, 0, 6, 2), (1, 2, 1, 0, 4), (2, 0, 1, 4, 4)]
        ld_4 = sem("ld_phase4")
        s_gath = sem("gathered")
        (k4_k, k4_ks, k4_kb, k4_v, k4_vs) = (sem("pre4_" + n) for n in ("k", "ks", "kbd", "v", "vs"))
        (q4_x, q4_var, q4_r, q4_z, q4_bo, q4_zT, q4_zTs, q4_q, q4_qs, q4_sc, q4_sub, q4_p, q4_pT, q4_pTs,
         q4_o, q4_on, q4_oT, q4_oTs, q4_out, q4_var3, q4_r3, q4_z3, q4_z3T, q4_z3Ts, q4_g, q4_gs) = (
            sem("p4_" + n) for n in ("x", "var", "r", "z", "bo", "zT", "zTs", "q", "qs", "scores", "sub", "p",
                                     "pT", "pTs", "o", "on", "oT", "oTs", "out", "var3", "r3", "z3",
                                     "z3T", "z3Ts", "g", "gs"))
        W1S = REG[:, 0:E * KC * F1].rearrange("p (e k f) -> p e k f", e=E, k=KC)
        W2S = REG[:, E * KC * F1:2 * E * KC * F1].rearrange("p (e k d) -> p e k d", e=E, k=FC1)
        EH = E // 2
        NB1, NB2 = E * F1, E * D
        c5 = Carve(0, XB)
        BPS = c5((NB1 + NB2,), bf16, PARTS)
        YB5 = c5((2, D))
        T5, SEL5, SELF5 = c5((NT, E)), c5((NT, E)), c5((NT, E), bf16)
        M5, IDF5 = c5((NT,)), c5((NT,))
        IDX5 = c5((NT,)).bitcast(u32)
        CN, NTL, CUM, OFFS = (c5((E,)) for _ in range(4))
        CMP = c5((E, NT))
        TEX = c5((NT1, E - 1), f32, 1)
        TEF, TEG = c5((NT1,), f32, 1), c5((NT1,), f32, 1)
        TEI, TEP = c5((NT1,), f32, 1).bitcast(i32), c5((NT1,), f32, 1).bitcast(i32)
        BBF = c5(((NB1 + NB2) // P,))
        BBR = c5(((NB1 + NB2) // P,))
        BBP = c5((PARTS, (NB1 + NB2) // P), bf16)
        c5f = Carve(0, XFF)
        XS5 = c5f((2, D))
        XT5 = c5f((2, KC, P))
        HS5 = c5f((2, F1))
        HT5 = c5f((FC1, P))
        ld_b, ld_b2, ld_bp = sem("ld_bias"), sem("bias_parts_out"), sem("ld_bias_parts")
        m5_out = [sem(f"p5_rows_out{n}") for n in range(2)]
        ld_xs = [sem(f"ld_xs{n}") for n in range(2)]
        s_gat5 = [sem(f"gathered5_{c}") for c in range(NCH)]
        (b5_p, r5_sel, r5_pos, r5_cnt, r5_idx, s_scat5, m5_xT, m5_xTs, m5_h, m5_hs, m5_hT, m5_hTs, m5_y, m5_ys, s_fin, s_out) = (
            sem("p5_" + n) for n in ("bias_parts", "sel", "pos", "count", "idx", "scattered", "xT", "xTs", "h", "hs", "hT", "hTs",
                                     "y", "ys", "final", "stored"))
        h5_ps = [PS[:, 2 * n:2 * n + 2, :] for n in range(2)]
        hT5_ps = PS[:, 4:6, :].rearrange("p a (f n) -> p (a f) n", f=4)
        xT5_ps = PS[:, 6, 0:KC * P].rearrange("p (k n) -> p k n", k=KC)
        y5_ps = PS[:, 7, 0:D]
        s_zero, s_fill = sem("zeros_made"), sem("dram_cleared")
        NFILL = -(-SLOTS0 // (4 * P)) + -(-SLOTS1 // (4 * P)) + 1
        FIRST = 1
        block = ctx.enter_context(nc.Block())

        zT_ps = PS[:, 0:2, :]
        sc_ps = PS[:, 2, :].rearrange("p (t k) -> p t k", t=CT)
        pT_ps = PS[0:LK, 3, :]
        o_ps = PS[:, 4:6, :].rearrange("p a (t d) -> p (a t) d", t=2)
        uT_ps = PS[:, 6:8, :]
        qk_ps = PS[:, 0:4, :].rearrange("p (a r) n -> p a r n", a=2)
        v_ps = o_ps

        @block.sync
        def _(sp):
            for primed in (s_qkst, m5_out[0], m5_out[1]):
                sp.sem_inc(primed, FIRST)
            sp.dma_start(CF[:], const_f_in).then_inc(ld_c, 16)
            sp.dma_start(CB[:], const_b_in).then_inc(ld_c, 16)
            for a, b in ((ctxT, ctxT_in), (wk0, wk0_in), (bk0, bk0_in), (bq0, bq0_in), (wq0T, wq0T_in),
                         (wv0, wv0_in), (bv0, bv0_in.partition_broadcast(P)), (wqk, wqk_in), (wv, wv_in),
                         (g1c, g1_in), (rope, rope_in)):
                sp.dma_start(a, b).then_inc(ld_w, 16)
            sp.dma_start(X[:], x_in.rearrange("b (t p) d -> p (b t) d", p=P)).then_inc(ld_x, 16)
            sp.wait_ge(s_zero, 1)
            for dram, n in ((xe_dram, SLOTS0), (xs_dram, SLOTS1)):
                for r0 in range(0, n, 4 * P):
                    m = min(4, (n - r0) // P)
                    sp.dma_start(dram[r0:r0 + m * P].rearrange("(a p) d -> p a d", p=P),
                                 ZERO[:, 0:m * D].rearrange("p (a d) -> p a d", a=m)).then_inc(s_fill, 16)
            sp.dma_start(ye_dram[SLOTS0:SLOTS0 + 1], ZERO[0:1, 0:D]).then_inc(s_fill, 16)
            with sp.Fori(0, B) as b:
                with sp.Fori(0, CPB) as cc:
                    sp.wait_ge(s_lo, b * CPB + cc + 1 + FIRST)
                    for a in range(2):
                        for n in range(PARTS):
                            for r in range(2):
                                at = n if a else PARTS - 1 - n
                                sp.dma_start(qk_dram[a, ds(b * NG, NG), at, r, :, ds(cc * CW, CW)],
                                             PARTB[:, n, a, r, :]).then_inc(s_qkst, 16)
            def load_qk(s, n):
                row = 0
                for run in RUNS:
                    for a, buf, p0 in ((0, QT, PARTS - run), (1, KT, 0)):
                        src = qk_dram[a].rearrange("s p r (i h) t -> s p (r i) (h t)", h=GH)
                        sp.dma_start(buf[row:row + run * HD, n].rearrange("p h t -> p (h t)"),
                                     src[s, p0:p0 + run].rearrange("p r c -> (p r) c")).then_inc(ld_qk[n], 16)
                    row += run * HD

            def load_max_rows(s, n):
                sp.wait_ge(s_mt, s + 1)
                for p in range(PARTS):
                    sp.dma_start(QT[QROWS + p:QROWS + p + 1, n].rearrange("p h (i t) -> p (h i) t", t=P),
                                 MT[p * 32:(p + 1) * 32, :]).then_inc(s_mrow, 16)

            sp.wait_ge(s_qkst, 16 * 12 * NCH + FIRST)
            sp.wait_ge(s_v, NCH)
            sp.wait_ge(s_lo, NCH + FIRST)
            load_qk(0, 0)
            sp.dma_start(KT[QROWS:AROWS].rearrange("p n h (a t) -> p (n h a) t", t=P),
                         const_b_in[0:PARTS, 3 * P:4 * P].unsqueeze(1).to_broadcast([PARTS, BUFS * GH * S // P, P])).then_inc(s_ones, 16)
            for n in range(1, BUFS):
                load_qk(n, n)
            load_max_rows(0, 0)
            for s in range(NS):
                if s + 1 < NS:
                    load_max_rows(s + 1, (s + 1) % BUFS)
                if s + BUFS < NS:
                    sp.wait_ge(s_sT, 2 * NSTG * (s + 1))
                    load_qk(s + BUFS, s % BUFS)
            sp.wait_ge(s_fill, 16 * NFILL)
            for a, b in ((WO, wo_in), (G2, g2_in.partition_broadcast(P)), (WR, wr_in)):
                sp.dma_start(a, b).then_inc(ld_3, 16)

            def load_expert(e, n):
                sp.dma_start(W1E[:, n], w1e_in.rearrange("e (k p) f -> e p k f", p=P)[ds(e, 1)].squeeze(0)).then_inc(ld_we[n], 16)
                sp.dma_start(W2E[:, n], w2e_in.rearrange("e (k p) d -> e p k d", p=P)[ds(e, 1)].squeeze(0)).then_inc(ld_we[n], 16)

            def load_rows(e, n):
                sp.dma_start(XEB[:, n, 0:2], xe_dram[ds(e * CAP, 2 * P)].rearrange("(a p) d -> p a d", p=P)).then_inc(ld_xe[n], 16)
                sp.dma_start(XEB[0:TAIL, n, 2], xe_dram[ds(e * CAP + 2 * P, TAIL)]).then_inc(ld_xe[n], 16)

            load_expert(0, 0)
            load_expert(1, 1)
            sp.wait_ge(s_yn, 2 * NS)
            for e in range(E):
                sp.dma_start(REG[:, e * KC * F1:(e + 1) * KC * F1].rearrange("p (k f) -> p k f", k=KC),
                             w1_in.rearrange("e (k p) f -> e p k f", p=P)[e]).then_inc(ld_5, 16)
            sp.wait_ge(s_scat, 16 * 2 * NT)
            load_rows(0, 0)
            load_rows(1, 1)
            with sp.Fori(0, E // 2 - 1) as it:
                for n in range(2):
                    e = 2 * it + n
                    sp.wait_ge(me_y, e + 1)
                    load_expert(e + 2, n)
                    load_rows(e + 2, n)
            sp.wait_ge(p3_lg, NCH)
            sp.wait_ge(p3_lgs, NCH + FIRST)
            sp.wait_ge(me_y, E)
            sp.wait_ge(me_out, 32 * E + FIRST)
            for a, b in ((WQ1, wq1_in), (WO1, wo1_in)):
                sp.dma_start(a, b).then_inc(ld_4, 16)
            for a, b in ((BO, bo1_in.partition_broadcast(P)), (WG, wg_in), (BG, bg_in.unsqueeze(0)), (BQ1, bq1_in), (BK1, bk1_in),
                         (CT1, ctxT_in), (WK1, wk1_in), (WV1, wv1_in), (BV1, bv1_in.partition_broadcast(P))):
                sp.dma_start(a, b).then_inc(ld_4, 16)
            for e in range(E // 2):
                at = (3 * E // 2 + e) * KC * F1
                sp.dma_start(REG[:, at:at + KC * F1].rearrange("p (k d) -> p k d", d=D),
                             w2_in.rearrange("e (k p) d -> e p k d", p=P)[e]).then_inc(ld_5, 16)
            sp.wait_ge(q4_gs, NCH)
            sp.wait_ge(q4_out, NCH)
            for e in range(EH):
                sp.dma_start(W2S[:, e], w2_in.rearrange("e (k p) d -> e p k d", p=P)[EH + e]).then_inc(ld_5, 16)
            sp.dma_start(BBF[:, 0:NB1 // P], b1_in.rearrange("e f -> (e f)").rearrange("(p n) -> p n", p=P)).then_inc(ld_b, 16)
            sp.dma_start(BBF[:, NB1 // P:], b2_in.rearrange("e f -> (e f)").rearrange("(p n) -> p n", p=P)).then_inc(ld_b, 16)
            sp.wait_ge(b5_p, 1)
            for n in range(PARTS):
                sp.dma_start(bp_dram[n, 0:NB1].rearrange("(p n) -> p n", p=P), BBP[:, n, 0:NB1 // P]).then_inc(ld_b2, 16)
                sp.dma_start(bp_dram[n, NB1:].rearrange("(p n) -> p n", p=P), BBP[:, n, NB1 // P:]).then_inc(ld_b2, 16)
            sp.wait_ge(ld_b2, 16 * 2 * PARTS)
            sp.dma_start(BPS, bp_dram).then_inc(ld_bp, 16)
            sp.wait_ge(s_scat5, 16 * NT)

            def load_tile(j, n):
                sp.dma_start(XS5[:, n], xs_dram[ds(j * P, P)]).then_inc(ld_xs[n], 16)

            def send_tile(j, n):
                sp.wait_ge(m5_ys, j + 1 + FIRST)
                sp.dma_start(ys_dram[ds(j * P, P)], YB5[:, n]).then_inc(m5_out[n], 16)

            load_tile(0, 0)
            load_tile(1, 1)
            with sp.Fori(0, (NT1 - 3) // 2) as it:
                for n in range(2):
                    j = 2 * it + n
                    sp.wait_ge(m5_xT, j + 1)
                    load_tile(j + 2, n)
                    send_tile(j, n)
            sp.wait_ge(m5_xT, NT1 - 2)
            load_tile(NT1 - 1, 0)
            for j in range(NT1 - 3, NT1):
                send_tile(j, j % 2)
            for c in range(NCH):
                sp.wait_ge(s_fin, c + 1)
                sp.dma_start(out.rearrange("b (t p) d -> p (b t) d", p=P)[:, c * CT:(c + 1) * CT], X[:, c * CT:(c + 1) * CT, :]).then_inc(s_out, 16)
            sp.wait_ge(s_out, 16 * NCH)

        @block.gpsimd
        def _(pool):
            for primed in (s_lo, p3_xs):
                pool.sem_inc(primed, FIRST)
            chain = Chain(pool, s_chp)
            nc.gpsimd.memset(ZERO, 0.0).then_inc(s_zero, 1)
            pool.wait_ge(ld_c, 32)
            with pool.Fori(0, NCH) as c:
                chain.enter(c, 7)
                pool.wait_ge(s_var, c + 1)
                nc.gpsimd.tensor_tensor(RSTD, VE, neg_half[:, 0:CT], ALU.pow).then_inc(s_rstd, 1)
                pool.wait_ge(s_var2, c + 1)
                chain(nc.gpsimd.tensor_tensor(R1, VE, neg_half[:, 0:CT], ALU.pow))
                chain(nc.gpsimd.tensor_tensor(TA, MV[:, :, 1], R1, ALU.mult))
                chain(nc.gpsimd.tensor_tensor(TV, TA, R1, ALU.mult), s_spare)
                chain(nc.gpsimd.tensor_scalar(TA, TV, RMS_EPS, None, ALU.add))
                chain(nc.gpsimd.tensor_tensor(R2, TA, neg_half[:, 0:CT], ALU.pow))
                nc.gpsimd.tensor_tensor(S1, R1, R2, ALU.mult).then_inc(s_rstd2, 1)
                pool.wait_ge(s_rt, c + 1 + FIRST)
                chain(nc.gpsimd.tensor_tensor(ROT[:, :, 0, :], RT[:, 0], RT[:, 1], ALU.subtract))
                nc.gpsimd.tensor_tensor(ROT[:, :, 1, :], RT[:, 2], RT[:, 3], ALU.add).then_inc(s_rot, 1)
                pool.wait_ge(s_hi, c + 1)
                flat = RT[:, 0:2].rearrange("p a b n -> p (a b n)")
                rot = ROT.rearrange("p a b n -> p (a b n)")
                part = PARTB.rearrange("p n a b m -> p n (a b m)")
                nc.gpsimd.tensor_tensor(flat, rot, part[:, 0], ALU.subtract).then_inc(s_res, 1)
                pool.wait_ge(s_mid, c + 1)
                chain(nc.gpsimd.tensor_tensor(part[:, 2], flat, part[:, 1], ALU.subtract))
                pool.sem_inc(s_lo, 1)
            chain.leave(NCH)
            pool.wait_ge(s_vs, NCH + FIRST)
            pool.wait_ge(s_v, NCH)
            pool.wait_ge(s_lo, NCH + FIRST)
            pool.wait_ge(s_qkst, 16 * 12 * NCH + FIRST)
            chain(nc.gpsimd.memset(VS, 0.0))
            chain(nc.gpsimd.memset(VS[:, :, :, :, HD:HD + 1], 1.0))
            pool.sem_inc(s_ini, 1)

            def stage_v(s, n):
                nc.gpsimd.tensor_copy(VS[:, n, :, :, 0:HD],
                                      VB[:, s].rearrange("p t (h d) -> p t h d", h=GH)).then_inc(s_vst, 1)

            for s in range(NS):
                if s >= BUFS:
                    pool.wait_ge(s_y, 2 * (s - BUFS + 1))
                stage_v(s, s % BUFS)
            with pool.Fori(0, NCH) as c:
                pool.wait_ge(s_yn, 2 * NS)
                pool.wait_ge(s_fill, 16 * NFILL)
                pool.wait_ge(p3_yT, c + FIRST)
                pool.sem_inc(s_spare, 1)
                nc.gpsimd.tensor_copy(YC, XF[:, ds(c * CT, CT), :]).then_inc(p3_yc, 1)
                pool.wait_ge(p3_ms, c + 1)
                nc.gpsimd.tensor_tensor(R2, VE, neg_half[:, 0:CT], ALU.pow).then_inc(p3_r, 1)
                pool.wait_ge(p3_xc, c + 1)
                pool.sem_inc(s_spare, 1)
                nc.gpsimd.tensor_copy(XF[:, ds(c * CT, CT), :], XC).then_inc(p3_xs, 1)
            pool.wait_ge(p3_xs, NCH + FIRST)
            pool.wait_ge(rt_idx, 1)
            for t in range(NT):
                for idx in (IDX1, IDX2):
                    nc.gpsimd.indirect_dma_start(out=xe_dram, out_offset=bass.IndirectOffsetOnAxis(ap=idx[:, t:t + 1], axis=0),
                                                 in_=XF[:, t, :], in_offset=None, bounds_check=SLOTS0 - 1,
                                                 oob_is_err=False).then_inc(s_scat, 16)
            pool.wait_ge(me_out, 32 * E + FIRST)
            pool.wait_ge(s_fill, 16 * NFILL)

            def gather(c):
                for t in range(CT):
                    for a, idx in enumerate((IDX1, IDX2)):
                        nc.gpsimd.indirect_dma_start(out=GB[:, t, a, :], out_offset=None, in_=ye_dram,
                                                     in_offset=bass.IndirectOffsetOnAxis(ap=idx[:, c * CT + t:c * CT + t + 1], axis=0),
                                                     bounds_check=SLOTS0, oob_is_err=True).then_inc(s_gath, 16)

            def enter4(c):
                pool.wait_ge(q4_var, c + 1)
                nc.gpsimd.tensor_tensor(RSTD, VE, neg_half[:, 0:CT], ALU.pow).then_inc(q4_r, 1)
                pool.wait_ge(ld_4, 16 * 11)
                pool.wait_ge(q4_z, c + 1)
                xc = X[:, c * CT:(c + 1) * CT, :]
                nc.gpsimd.tensor_tensor(xc, xc, BO.unsqueeze(1).to_broadcast([P, CT, D]), ALU.add).then_inc(q4_bo, 1)

            def leave4(c):
                pool.wait_ge(q4_var3, c + 1)
                nc.gpsimd.tensor_tensor(RSTD, VE, neg_half[:, 0:CT], ALU.pow).then_inc(q4_r3, 1)

            gather(0)
            pool.wait_ge(q4_x, 1)
            gather(1)
            enter4(0)
            for c in range(NCH):
                if c + 2 < NCH:
                    pool.wait_ge(q4_x, c + 2)
                    gather(c + 2)
                if c + 1 < NCH:
                    enter4(c + 1)
                if c:
                    leave4(c - 1)
            leave4(NCH - 1)
            pool.wait_ge(q4_z3, NCH)
            pool.wait_ge(r5_idx, 1)
            for t in range(NT):
                nc.gpsimd.indirect_dma_start(out=xs_dram, out_offset=bass.IndirectOffsetOnAxis(ap=IDX5[:, t:t + 1], axis=0),
                                             in_=H[:, t, :], in_offset=None, bounds_check=SLOTS1 - 1,
                                             oob_is_err=True).then_inc(s_scat5, 16)
            pool.wait_ge(s_scat5, 16 * NT)
            pool.wait_ge(m5_out[0], 16 * ((NT1 + 1) // 2) + FIRST)
            pool.wait_ge(m5_out[1], 16 * (NT1 // 2) + FIRST)
            for t in range(NT):
                nc.gpsimd.indirect_dma_start(out=H[:, t, :], out_offset=None, in_=ys_dram,
                                             in_offset=bass.IndirectOffsetOnAxis(ap=IDX5[:, t:t + 1], axis=0),
                                             bounds_check=SLOTS1 - 1, oob_is_err=True).then_inc(s_gat5[t // CT], 16)

        @block.scalar
        def _(act):
            for primed in (me_out, me_ys, s_vs, m5_hTs):
                act.sem_inc(primed, FIRST)
            for m in range(KC):
                act.wait_ge(pre_k, m + 1)
                nc.scalar.activation(KT0[:, m, :], PS[:, m, 0:B * LK], ACT.Identity, bias=bk0[:, m:m + 1]).then_inc(pre_ks, 1)
            act.wait_ge(pre_a, 1)
            nc.scalar.activation(A0, PS[:, 2:2 + KC, 0:B * LK], ACT.Copy)
            nc.scalar.activation(CB0, PS[0:1, 4, 0:B * LK], ACT.Copy).then_inc(pre_as, 1)
            with act.Fori(0, B) as b:
                with act.Fori(0, CPB) as cc:
                    c = b * CPB + cc
                    act.wait_ge(s_zT, c + 1)
                    nc.scalar.activation(ZT, zT_ps, ACT.Copy).then_inc(s_zTs, 1)
                    act.wait_ge(s_nb, c + 1)
                    for t in range(CT):
                        last = nc.scalar.activation(P0[:, t, 0:LK], sc_ps[:, t, 0:LK], ACT.Exp, bias=NB[:, t:t + 1],
                                                    scale=1.0 / 16.0, accum_out=RSUM[:, t:t + 1])
                    last.then_inc(s_p, 1)
                    act.wait_ge(s_pT, c + 1)
                    nc.scalar.activation(PT0, pT_ps, ACT.Copy).then_inc(s_pTs, 1)
                    act.wait_ge(s_uT, c + 1)
                    nc.scalar.activation(UT, uT_ps, ACT.Copy).then_inc(s_uTs, 1)
                    act.wait_ge(s_v, c + 1)
                    for t in range(CT):
                        last = nc.scalar.activation(
                            VB.rearrange("p (b g) t n -> p b t g n", b=B)[:, ds(b, 1), ds(cc * CT + t, 1)],
                            v_ps[:, t, :].rearrange("p (x y g n) -> p x y g n", x=1, y=1, g=NG), ACT.Copy)
                    last.then_inc(s_vs, 1)
                    act.wait_ge(s_rot, c + 1)
                    act.wait_ge(s_qkst, 16 * 12 * c + FIRST)
                    rot = ROT.rearrange("p a b n -> p (a b n)")
                    flat = RT[:, 0:2].rearrange("p a b n -> p (a b n)")
                    part = PARTB.rearrange("p n a b m -> p n (a b m)")
                    nc.scalar.activation(part[:, 0], rot, ACT.Copy).then_inc(s_hi, 1)
                    act.wait_ge(s_res, c + 1)
                    nc.scalar.activation(part[:, 1], flat, ACT.Copy).then_inc(s_mid, 1)
            def exps(s, n):
                for k, (c, j) in enumerate(STAGES):
                    q0 = q0_of(c, j)
                    act.wait_ge(s_pvd, NSTG * s + k + FIRST)
                    for pair in range(2):
                        act.wait_ge(s_sT, 2 * NSTG * s + 2 * k + pair + 1)
                        nc.scalar.activation(PB[:, k % 2, 2 * pair:2 * pair + 2, q0:CW], s_ps[pair][:, :, q0:CW],
                                             ACT.Exp, scale=0.25).then_inc(s_sfree, 1)

            act.wait_ge(s_v, NCH)
            act.wait_ge(s_lo, NCH + FIRST)
            act.wait_ge(s_qkst, 16 * 12 * NCH + FIRST)
            act.sem_inc(s_sfree, 2)
            with act.Fori(0, NS // 2) as it:
                for n in range(2):
                    exps(2 * it + n, n)
            with act.Fori(0, NCH) as c:
                act.wait_ge(p3_yT, c + 1 + FIRST)
                nc.scalar.activation(YCT, yT3_ps, ACT.Copy).then_inc(p3_yTs, 1)
                act.wait_ge(p3_xT, c + 1)
                nc.scalar.activation(XCT, xT3_ps, ACT.Copy).then_inc(p3_xTs, 1)
            act.wait_ge(rt_sub, 1)
            nc.scalar.activation(EX, TE1, ACT.Exp).then_inc(rt_exp, 1)

            def send_rows(e, n):
                act.dma_start(ye_dram[ds(e * CAP, 2 * P)].rearrange("(a p) d -> p a d", p=P), YEB[:, n, 0:2]).then_inc(me_out, 16)
                act.dma_start(ye_dram[ds(e * CAP + 2 * P, TAIL)], YEB[0:TAIL, n, 2]).then_inc(me_out, 16)

            def evac_xT(e, n):
                act.wait_ge(me_xT, e + 1)
                nc.scalar.activation(XET[:, n], xeT_ps, ACT.Copy).then_inc(me_xTs, 1)

            def expert_rows(e, n):
                act.wait_ge(me_y, e + 1)
                act.wait_ge(me_out, 32 * e + FIRST)
                nc.scalar.activation(YEB[:, n, 0:2], ye_ps[:, 0:2], ACT.Copy)
                nc.scalar.activation(YEB[0:TAIL, n, 2], ye_ps[0:TAIL, 2], ACT.Copy).then_inc(me_ys, 1)
                act.wait_ge(me_ys, e + 1 + FIRST)
                send_rows(e, n)

            evac_xT(0, 0)
            with act.Fori(0, E // 2 - 1) as it:
                for n in range(2):
                    evac_xT(2 * it + n + 1, 1 - n)
                    expert_rows(2 * it + n, n)
            evac_xT(E - 1, 1)
            expert_rows(E - 2, 0)
            expert_rows(E - 1, 1)
            act.wait_ge(ld_4, 16 * 11)
            for m in range(KC):
                act.wait_ge(k4_k, m + 1)
                nc.scalar.activation(KT1[:, m, :], PS[:, m, 0:B * LK], ACT.Identity, bias=BK1[:, m:m + 1]).then_inc(k4_ks, 1)

            def evac_T4(ready, done, c):
                act.wait_ge(ready, c + 1)
                nc.scalar.activation(Z4T, zT4_ps, ACT.Copy).then_inc(done, 1)

            def evac_q(c):
                act.wait_ge(q4_q, c + 1)
                for m in range(KC):
                    last = nc.scalar.activation(Q4T[:, c % 2, m, :], q4_ps[:, m, :], ACT.Identity, bias=BQ1[:, m:m + 1])
                last.then_inc(q4_qs, 1)

            def exp4(c, t):
                act.wait_ge(q4_sub, c * CT + t + 1)
                nc.scalar.activation(SS[:, t % 2], SS[:, t % 2], ACT.Exp, scale=0.25).then_inc(q4_p, 1)

            evac_T4(q4_zT, q4_zTs, 0)
            evac_q(0)
            exp4(0, 0)
            for c in range(NCH):
                for t in range(CT):
                    for q in range(NQ):
                        unit = (c * CT + t) * NQ + q
                        act.wait_ge(q4_pT, unit + 1)
                        nc.scalar.activation(PT4[:, q * QH:(q + 1) * QH, :], pT4_ps[q % 2], ACT.Copy).then_inc(q4_pTs, 1)
                        if (t, q) == (0, 1) and c:
                            evac_T4(q4_oT, q4_oTs, c - 1)
                        if (t, q) == (2, 3) and c + 1 < NCH:
                            evac_T4(q4_zT, q4_zTs, c + 1)
                        if (t, q) == (3, 0) and c + 1 < NCH:
                            evac_q(c + 1)
                        if (t, q) == (3, 2) and c:
                            evac_T4(q4_z3T, q4_z3Ts, c - 1)
                        if q == 2 and (c * CT + t + 1) < NT:
                            exp4(c + (t + 1) // CT, (t + 1) % CT)
            evac_T4(q4_oT, q4_oTs, NCH - 1)
            evac_T4(q4_z3T, q4_z3Ts, NCH - 1)
            def evac_xT5(j, n):
                act.wait_ge(m5_xT, j + 1)
                nc.scalar.activation(XT5[:, n], xT5_ps, ACT.Copy).then_inc(m5_xTs, 1)

            def evac_hT5(j):
                act.wait_ge(m5_hT, j + 1)
                act.wait_ge(m5_y, j + FIRST)
                nc.scalar.activation(HT5, hT5_ps, ACT.Copy).then_inc(m5_hTs, 1)

            evac_xT5(0, 0)
            evac_xT5(1, 1)
            with act.Fori(0, (NT1 - 3) // 2) as it:
                for n in range(2):
                    evac_hT5(2 * it + n)
                    evac_xT5(2 * it + n + 2, n)
            evac_hT5(NT1 - 3)
            evac_xT5(NT1 - 1, 0)
            evac_hT5(NT1 - 2)
            evac_hT5(NT1 - 1)

        @block.vector
        def _(dve):
            for primed in (s_rt, s_yev, p3_lgs, m5_ys):
                dve.sem_inc(primed, FIRST)
            chain = Chain(dve, s_chv)
            dve.wait_ge(ld_w, 16 * 11)
            for k in range(KC):
                nc.vector.tensor_scalar(wqk[:, k], wqk[:, k], g1c[:, k:k + 1], None, ALU.mult)
                last = nc.vector.tensor_scalar(wv[:, k], wv[:, k], g1c[:, k:k + 1], None, ALU.mult)
            last.then_inc(pre_w, 1)
            dve.wait_ge(pre_a, 1)
            nc.vector.tensor_tensor(V0, PS[0:LK, 5:7, 0:D], bv0[0:LK, :].unsqueeze(1).to_broadcast([LK, B, D]), ALU.add).then_inc(pre_w, 1)
            dve.wait_ge(ld_x, 16)
            with dve.Fori(0, B) as b:
                with dve.Fori(0, CPB) as cc:
                    c = b * CPB + cc
                    chain.enter(c, 8)
                    for t in range(CT):
                        last = nc.vector.bn_stats(ST[:, t, :].unsqueeze(1), X[:, ds(c * CT + t, 1), :])
                    chain(last, s_spare)
                    for t in range(CT):
                        last = nc.vector.bn_aggr(MV[:, t, :], ST[:, t, :])
                    chain(last)
                    nc.vector.tensor_scalar(VE, MV[:, :, 1], LN_EPS, None, ALU.add).then_inc(s_var, 1)
                    dve.wait_ge(s_rstd, c + 1)
                    for t in range(CT):
                        last = nc.vector.tensor_scalar(Z[:, t:t + 1, :], X[:, ds(c * CT + t, 1), :], MV[:, t, 0:1], RSTD[:, t:t + 1],
                                                       ALU.subtract, ALU.mult)
                    last.then_inc(s_z, 1)
                    dve.wait_ge(s_sc, c + 1)
                    chain(nc.vector.reduce_max(MX, sc_ps[:, :, 0:LK], AX.X))
                    nc.vector.tensor_scalar(NB, MX, -1.0 / 16.0, None, ALU.mult).then_inc(s_nb, 1)
                    dve.wait_ge(s_p, c + 1)
                    chain(nc.vector.reciprocal(RRS, RSUM))
                    dve.wait_ge(s_o, c + 1)
                    for t in range(CT):
                        xt = X[:, ds(c * CT + t, 1), :]
                        last = nc.vector.scalar_tensor_tensor(out=xt, in0=o_ps[:, t:t + 1, :], scalar=RRS[:, t:t + 1], in1=xt,
                                                              op0=ALU.mult, op1=ALU.add)
                    chain(last, s_spare)
                    for t in range(CT):
                        last = nc.vector.bn_stats(ST[:, t, :].unsqueeze(1), X[:, ds(c * CT + t, 1), :])
                    chain(last, s_spare)
                    for t in range(CT):
                        last = nc.vector.bn_aggr(MV[:, t, :], ST[:, t, :])
                    chain(last)
                    nc.vector.tensor_scalar(VE, MV[:, :, 1], LN_EPS, None, ALU.add).then_inc(s_var2, 1)
                    dve.wait_ge(s_rstd2, c + 1)
                    for t in range(CT):
                        last = nc.vector.tensor_scalar(U[:, t:t + 1, :], X[:, ds(c * CT + t, 1), :], MV[:, t, 0:1], S1[:, t:t + 1],
                                                       ALU.subtract, ALU.mult)
                    last.then_inc(s_u, 1)
                    for t in range(CT):
                        last = nc.vector.tensor_scalar(H[:, ds(c * CT + t, 1), :], X[:, ds(c * CT + t, 1), :], MV[:, t, 0:1], R1[:, t:t + 1],
                                                       ALU.subtract, ALU.mult)
                    chain(last)
                    dve.wait_ge(s_qk, c + 1)
                    dve.wait_ge(s_lo, c + FIRST)
                    for n, (r, t) in enumerate(((0, 0), (1, 1), (0, 1), (1, 0))):
                        table = rope[:, t:t + 1, ds(cc * CW, CW)].to_broadcast([P, 2, CW])
                        last = nc.vector.tensor_tensor(RT[:, n], qk_ps[:, :, r, :], table, ALU.mult)
                    last.then_inc(s_rt, 1)
            chain.leave(NCH)
            def reduce_unit(s, u):
                i, h0, nh, k0, w, masked = UNITS[u]
                dve.wait_ge(s_mx, NU * s + u + 1)
                src = m_ps[u % 2][:, 0:nh * w].rearrange("p (h w) -> p h w", h=nh)
                last = nc.vector.reduce_max(MXP[:, h0:h0 + nh, i, int(not masked)], src, AX.X)
                last.then_inc(s_mfree, 1)

            def max_parts(s):
                dve.wait_ge(s_mfree, NU * (s + 1) + 2)
                chain(nc.vector.reduce_max(NR, MXP, AX.X))
                chain(nc.vector.tensor_scalar(NM, NR, -1.0, None, ALU.mult))
                chain(nc.vector.tensor_copy(MP[:, 0], NM))
                chain(nc.vector.tensor_tensor(NR, NM, MP[:, 0], ALU.subtract))
                chain(nc.vector.tensor_copy(MP[:, 1], NR))
                nc.vector.tensor_tensor(MP[:, 2], NR, MP[:, 1], ALU.subtract).then_inc(s_mp, 1)

            def max_rows(s):
                dve.wait_ge(s_mpt, s + 1)
                dve.wait_ge(s_mrow, 16 * PARTS * s)
                nc.vector.tensor_copy(MT[0:96], t_ps.bitcast(bf16)[0:96, 0:P]).then_inc(s_mt, 1)

            def evac_y(s, c):
                dve.wait_ge(s_y, 2 * s + c + 1)
                nc.vector.tensor_copy(YT[:, c], y_ps).then_inc(s_yev, 1)

            def norm_y(s, c, b_, g):
                dve.wait_ge(s_yt, 2 * s + c + 1)
                back = t_ps.rearrange("p (t h d) -> p t h d", t=CT, h=GH)
                chain(nc.vector.reciprocal(RY, back[:, :, :, HD]))
                dst = XF.rearrange("p t (s x) -> p t s x", s=NG)
                for t in range(CT):
                    last = nc.vector.tensor_tensor(
                        dst[:, ds(b_ * NK + c * CT + t, 1), ds(g, 1), :].rearrange("p a b (h d) -> p (a b) h d", h=GH),
                        back[:, t:t + 1, :, 0:HD].rearrange("p a h d -> p a h d"),
                        RY[:, t:t + 1, :].unsqueeze(3).to_broadcast([P, 1, GH, HD]), ALU.mult)
                last.then_inc(s_yn, 1)

            dve.wait_ge(s_lo, NCH + FIRST)
            dve.wait_ge(s_rt, NCH + FIRST)
            dve.wait_ge(s_qkst, 16 * 12 * NCH + FIRST)
            chain(nc.vector.memset(MXP, -3.0e38))
            dve.sem_inc(s_mfree, 2)
            for u in range(NU):
                reduce_unit(0, u)
            max_parts(0)
            max_rows(0)

            def dve_step(s, b_, g, nxt):
                for k in range(NSTG):
                    if k == CT + 1:
                        evac_y(s, 0)
                    if nxt:
                        for u in range(CUT[k], CUT[k + 1]):
                            reduce_unit(s + 1, u)
                    if k == 7:
                        norm_y(s, 0, b_, g)
                    if nxt and k == NSTG - 3:
                        max_parts(s + 1)
                        max_rows(s + 1)
                evac_y(s, 1)
                norm_y(s, 1, b_, g)

            STEP = 2 + 5
            with dve.Fori(0, B - 1) as b_:
                with dve.Fori(0, NG) as g:
                    chain.enter(b_ * NG + g, STEP)
                    dve_step(b_ * NG + g, b_, g, True)
            chain.leave((B - 1) * NG)
            with dve.Fori(0, NG - 1) as g:
                chain.enter(g, STEP)
                dve_step((B - 1) * NG + g, B - 1, g, True)
            chain.leave(NG - 1)
            dve_step(NS - 1, B - 1, NG - 1, False)
            dve.wait_ge(ld_3, 48)
            with dve.Fori(0, NCH) as c:
                chain.enter(c, 4)
                hc = H[:, ds(c * CT, CT), :]
                dve.wait_ge(p3_o, c + 1)
                chain(nc.vector.tensor_tensor(hc, o3_ps, hc, ALU.add), s_spare)
                for t in range(CT):
                    last = nc.vector.bn_stats(ST[:, t, :].unsqueeze(1), H[:, ds(c * CT + t, 1), :])
                chain(last, s_spare)
                for t in range(CT):
                    last = nc.vector.bn_aggr(MV[:, t, :], ST[:, t, :])
                chain(last)
                chain(nc.vector.tensor_tensor(TV, MV[:, :, 0], MV[:, :, 0], ALU.mult))
                nc.vector.scalar_tensor_tensor(out=VE, in0=TV, scalar=RMS_EPS, in1=MV[:, :, 1], op0=ALU.add, op1=ALU.add).then_inc(p3_ms, 1)
                dve.wait_ge(p3_r, c + 1)
                dve.wait_ge(p3_xs, c + FIRST)
                for t in range(CT):
                    last = nc.vector.scalar_tensor_tensor(out=XC[:, t:t + 1, :], in0=H[:, ds(c * CT + t, 1), :], scalar=R2[:, t:t + 1],
                                                          in1=G2.unsqueeze(1), op0=ALU.mult, op1=ALU.mult)
                last.then_inc(p3_xc, 1)
                dve.wait_ge(p3_lg, c + 1)
                nc.vector.tensor_copy(LG[:, ds(c * CT, CT), :], lg_ps).then_inc(p3_lgs, 1)
            chain.leave(NCH)

            def over_e(a):
                return a.unsqueeze(2).to_broadcast([P, NT, E])

            def over_t(a):
                return a.unsqueeze(1).to_broadcast([P, NT, E])

            def first_max(src, top, sel, tmp):
                chain(nc.vector.reduce_max(top, src, AX.X))
                chain(nc.vector.tensor_tensor(tmp, src, over_e(top), ALU.is_equal))
                chain(nc.vector.tensor_tensor(tmp, tmp, over_t(w8), ALU.mult))
                chain(nc.vector.reduce_max(VM, tmp, AX.X))
                chain(nc.vector.tensor_tensor(sel, tmp, over_e(VM), ALU.is_equal))

            dve.wait_ge(p3_lgs, NCH + FIRST)
            chain(nc.vector.reduce_max(M1, LG[:], AX.X))
            nc.vector.tensor_tensor(TE1, LG[:], over_e(M1), ALU.subtract).then_inc(rt_sub, 1)
            dve.wait_ge(rt_exp, 1)
            chain(nc.vector.reduce_sum(SU, EX, AX.X))
            chain(nc.vector.reciprocal(RSU, SU))
            chain(nc.vector.tensor_tensor(PR, EX, over_e(RSU), ALU.mult))
            first_max(PR, M1, SEL1, TE1)
            chain(nc.vector.scalar_tensor_tensor(out=TE2, in0=SEL1, scalar=-4.0, in1=PR, op0=ALU.mult, op1=ALU.add))
            first_max(TE2, M2, SEL2, TE1)
            chain(nc.vector.tensor_tensor(TE1, SEL1, SEL2, ALU.add))
            chain(nc.vector.tensor_tensor(G, TE1, PR, ALU.mult))
            chain(nc.vector.memset(CUR, 0.0))
            chain(nc.vector.tensor_copy(BIT, top_bit))
            with dve.Fori(0, BITS) as i:
                chain.enter(i, 5)
                chain(nc.vector.tensor_tensor(CAND.bitcast(i32), CUR.bitcast(i32), BIT.bitcast(i32), ALU.bitwise_or))
                nc.vector.tensor_tensor(GEb, G, over_t(CAND), ALU.is_ge).then_inc(rt_ge, 1)
                chain(nc.vector.tensor_scalar(BIT.bitcast(i32), BIT.bitcast(i32), 1, None, ALU.logical_shift_right))
                dve.wait_ge(rt_cnt, i + 1)
                chain(nc.vector.reduce_sum(CNT, cnt_ps.rearrange("p t e -> p e t"), AX.X))
                chain(nc.vector.scalar_tensor_tensor(out=TK, in0=CNT, scalar=CAP - 0.5, in1=CAND, op0=ALU.is_ge, op1=ALU.mult))
                chain(nc.vector.tensor_tensor(CUR, CUR, TK, ALU.max))
            chain.leave(BITS)
            chain(nc.vector.tensor_tensor(TE1, G, over_t(CUR), ALU.is_equal))
            chain(nc.vector.scalar_tensor_tensor(out=EQb, in0=G, scalar=0.0, in1=TE1, op0=ALU.is_gt, op1=ALU.mult))
            nc.vector.tensor_tensor(GEb, G, over_t(CUR), ALU.is_gt).then_inc(rt_gt, 1)
            dve.wait_ge(rt_ngt, 1)
            chain(nc.vector.reduce_sum(CNT, cnt_ps.rearrange("p t e -> p e t"), AX.X))
            chain(nc.vector.tensor_scalar(NGT, CNT, -1.0, float(CAP), ALU.mult, ALU.add))
            chain(nc.vector.tensor_tensor(TE1, pfx_ps, over_t(NGT), ALU.is_lt))
            chain(nc.vector.tensor_tensor(TE2, TE1, EQb, ALU.mult))
            chain(nc.vector.tensor_tensor(KEEPb, TE2, GEb, ALU.add))
            dve.sem_inc(rt_keep, 1)
            dve.wait_ge(rt_pos, 1)
            chain(nc.vector.tensor_tensor(TE1, pos_ps, over_t(base0), ALU.add))
            chain(nc.vector.tensor_tensor(TE1, TE1, KEEPb, ALU.mult))
            for sel, top, gate, idx in ((SEL1, M1, GATE1, IDX1), (SEL2, M2, GATE2, IDX2)):
                chain(nc.vector.tensor_tensor(TE2, TE1, sel, ALU.mult))
                chain(nc.vector.reduce_sum(IDF, TE2, AX.X))
                chain(nc.vector.tensor_scalar(idx, IDF, float(SLOTS0), None, ALU.add))
                chain(nc.vector.tensor_tensor(TE2, KEEPb, sel, ALU.mult))
                chain(nc.vector.reduce_sum(IDF, TE2, AX.X))
                chain(nc.vector.tensor_tensor(gate, IDF, top, ALU.mult))
            dve.sem_inc(rt_idx, 1)
            with dve.Fori(0, E) as e:
                dve.wait_ge(me_h, e + 1)
                nc.vector.tensor_scalar(HTE, he_ps, 0.0, None, ALU.max).then_inc(me_hs, 1)
            dve.wait_ge(ld_4, 16 * 11)
            dve.wait_ge(k4_ks, KC)
            for b in range(B):
                for k in range(KC):
                    for h in range(8):
                        last = nc.vector.tensor_scalar(KBD[:, b, k, h, :], KT1[:, k, b * LK:(b + 1) * LK], headmask[:, h:h + 1], None, ALU.mult)
            last.then_inc(k4_kb, 1)
            dve.wait_ge(k4_v, 1)
            nc.vector.memset(V1, 1.0).then_inc(k4_vs, 1)
            dve.wait_ge(k4_vs, 1)
            for b in range(B):
                last = nc.vector.tensor_tensor(V1[:, b, :, 0:HD], PS[0:LK, 2 + b, 0:D].rearrange("p (h d) -> p h d", h=HEADS),
                                               BV1[0:LK].rearrange("p (h d) -> p h d", h=HEADS), ALU.add)
            last.then_inc(k4_vs, 1)

            def stats(c, ready):
                for t in range(CT):
                    last = nc.vector.bn_stats(ST[:, t, :], X[:, c * CT + t, :])
                chain(last)
                for t in range(CT):
                    last = nc.vector.bn_aggr(MV[:, t, :], ST[:, t, :])
                chain(last)
                nc.vector.tensor_scalar(VE, MV[:, :, 1], LN_EPS, None, ALU.add).then_inc(ready, 1)

            def combine(c):
                dve.wait_ge(s_gath, 16 * 2 * CT * (c + 1))
                for a, gate in enumerate((GATE1, GATE2)):
                    for t in range(CT):
                        ht = H[:, c * CT + t, :]
                        last = nc.vector.scalar_tensor_tensor(out=ht, in0=GB[:, t, a, :], scalar=gate[:, c * CT + t:c * CT + t + 1], in1=ht,
                                                              op0=ALU.mult, op1=ALU.add)
                    chain(last)
                xc = X[:, c * CT:(c + 1) * CT, :]
                chain(nc.vector.tensor_tensor(xc, xc, H[:, c * CT:(c + 1) * CT, :], ALU.add))
                dve.sem_inc(q4_x, 1)

            def normed(c):
                dve.wait_ge(q4_r, c + 1)
                if c:
                    dve.wait_ge(q4_zT, c)
                for t in range(CT):
                    last = nc.vector.tensor_scalar(Z4[:, t, :], X[:, c * CT + t, :], MV[:, t, 0:1], RSTD[:, t:t + 1],
                                                   ALU.subtract, ALU.mult)
                last.then_inc(q4_z, 1)

            def add_out(c):
                dve.wait_ge(q4_out, c + 1)
                dve.wait_ge(q4_bo, c + 1)
                xc = X[:, c * CT:(c + 1) * CT, :]
                chain(nc.vector.tensor_tensor(xc, out4_ps, xc, ALU.add))

            def normed3(c):
                dve.wait_ge(q4_r3, c + 1)
                for t in range(CT):
                    last = nc.vector.tensor_scalar(H[:, c * CT + t, :], X[:, c * CT + t, :], MV[:, t, 0:1], RSTD[:, t:t + 1],
                                                   ALU.subtract, ALU.mult)
                last.then_inc(q4_z3, 1)

            def gates(c):
                dve.wait_ge(q4_g, c + 1)
                nc.vector.tensor_copy(LG[:, c * CT:(c + 1) * CT, :], gate_ps).then_inc(q4_gs, 1)

            def subtract_max(c, t):
                dve.wait_ge(q4_sc, c * CT + t + 1)
                ab = sc4_ps[:, 0:2].rearrange("p a (h k) -> p a h k", h=6)
                cc_ = sc4_ps[:, 2, 0:4 * LK].rearrange("p (h k) -> p h k", h=4)
                nc.vector.reduce_max(MX4[:, 0:12], ab, AX.X)
                chain(nc.vector.reduce_max(MX4[:, 12:16], cc_, AX.X))
                for a in range(2):
                    nc.vector.tensor_tensor(SS[:, t % 2, 6 * a:6 * a + 6, :], ab[:, a], MX4[:, 6 * a:6 * a + 6].unsqueeze(2).to_broadcast([P, 6, LK]), ALU.subtract)
                nc.vector.tensor_tensor(SS[:, t % 2, 12:16, :], cc_, MX4[:, 12:16].unsqueeze(2).to_broadcast([P, 4, LK]), ALU.subtract).then_inc(q4_sub, 1)

            def heads_out(c, t):
                dve.wait_ge(q4_o, c * CT + t + 1)
                if c:
                    dve.wait_ge(q4_oT, c)
                chain(nc.vector.reciprocal(RO, o4_ps[:, :, HD]))
                nc.vector.tensor_tensor(O4[:, t, :].rearrange("p (h d) -> p h d", h=HEADS), o4_ps[:, :, 0:HD],
                                        RO.unsqueeze(2).to_broadcast([P, HEADS, HD]), ALU.mult).then_inc(q4_on, 1)

            dve.wait_ge(k4_v, 1)
            combine(0)
            stats(0, q4_var)
            normed(0)
            subtract_max(0, 0)
            for c in range(NCH):
                enters, leaves = c + 1 < NCH, c > 0
                subtract_max(c, 1)
                if enters:
                    combine(c + 1)
                heads_out(c, 0)
                subtract_max(c, 2)
                if enters:
                    stats(c + 1, q4_var)
                if leaves:
                    add_out(c - 1)
                heads_out(c, 1)
                subtract_max(c, 3)
                if enters:
                    normed(c + 1)
                if leaves:
                    stats(c - 1, q4_var3)
                heads_out(c, 2)
                if leaves:
                    normed3(c - 1)
                if enters:
                    subtract_max(c + 1, 0)
                if leaves:
                    gates(c - 1)
                heads_out(c, 3)
            add_out(NCH - 1)
            stats(NCH - 1, q4_var3)
            normed3(NCH - 1)
            gates(NCH - 1)
            dve.wait_ge(q4_gs, NCH)
            dve.wait_ge(q4_g, NCH)
            chain(nc.vector.reduce_max(M5, LG[:], AX.X))
            chain(nc.vector.tensor_tensor(T5, LG[:], over_e(M5), ALU.is_equal))
            chain(nc.vector.tensor_tensor(T5, T5, over_t(w8), ALU.mult))
            chain(nc.vector.reduce_max(M5, T5, AX.X))
            chain(nc.vector.tensor_tensor(SEL5, T5, over_e(M5), ALU.is_equal))
            nc.vector.tensor_copy(SELF5, SEL5).then_inc(r5_sel, 1)
            dve.wait_ge(r5_cnt, 1)
            chain(nc.vector.reduce_sum(CN, cnt_ps.rearrange("p t e -> p e t"), AX.X))
            chain(nc.vector.tensor_tensor(CMP, CN.unsqueeze(2).to_broadcast([P, E, NT]), j128.unsqueeze(1).to_broadcast([P, E, NT]), ALU.is_gt))
            chain(nc.vector.reduce_sum(NTL, CMP, AX.X))
            chain(nc.vector.tensor_copy(CUM[:, 0:1], NTL[:, 0:1]))
            for e in range(1, E):
                chain(nc.vector.tensor_tensor(CUM[:, e:e + 1], CUM[:, e - 1:e], NTL[:, e:e + 1], ALU.add))
            chain(nc.vector.tensor_tensor(OFFS, CUM, NTL, ALU.subtract))
            chain(nc.vector.tensor_scalar(OFFS, OFFS, float(P), None, ALU.mult))
            dve.wait_ge(r5_pos, 1)
            chain(nc.vector.tensor_tensor(T5, pos_ps, over_t(OFFS), ALU.add))
            chain(nc.vector.tensor_tensor(T5, T5, SEL5, ALU.mult))
            chain(nc.vector.reduce_sum(IDF5, T5, AX.X))
            nc.vector.tensor_copy(IDX5, IDF5).then_inc(r5_idx, 1)
            chain(nc.vector.tensor_tensor(TEX, CUM[0:1, 0:E - 1].unsqueeze(1).to_broadcast([1, NT1, E - 1]),
                                          jt.unsqueeze(2).to_broadcast([1, NT1, E - 1]), ALU.is_le))
            chain(nc.vector.reduce_sum(TEF, TEX, AX.X))
            chain(nc.vector.tensor_scalar(TEG, TEF, EH - 0.5, -float(E), ALU.is_ge, ALU.mult))
            chain(nc.vector.tensor_copy(TEI, TEF))
            nc.vector.scalar_tensor_tensor(out=TEP, in0=TEF, scalar=float(EH), in1=TEG, op0=ALU.add, op1=ALU.add).then_inc(r5_idx, 1)
            dve.wait_ge(ld_b, 32)
            chain(nc.vector.tensor_copy(BBP[:, 0], BBF))
            chain(nc.vector.tensor_tensor(BBR, BBF, BBP[:, 0], ALU.subtract))
            chain(nc.vector.tensor_copy(BBP[:, 1], BBR))
            nc.vector.tensor_tensor(BBP[:, 2], BBR, BBP[:, 1], ALU.subtract).then_inc(b5_p, 1)

            def relu5(j, n):
                dve.wait_ge(m5_h, j + 1)
                nc.vector.tensor_scalar(HS5[:, n], h5_ps[n].rearrange("p a f -> p (a f)"), 0.0, None, ALU.max).then_inc(m5_hs, 1)

            def evac_y5(j, n, it):
                dve.wait_ge(m5_y, j + 1 + FIRST)
                dve.wait_ge(m5_out[n], 16 * it + FIRST)
                nc.vector.tensor_copy(YB5[:, n], y5_ps).then_inc(m5_ys, 1)

            relu5(0, 0)
            with dve.Fori(0, (NT1 - 3) // 2) as it:
                for n in range(2):
                    relu5(2 * it + n + 1, 1 - n)
                    evac_y5(2 * it + n, n, it)
            relu5(NT1 - 2, 1)
            evac_y5(NT1 - 3, 0, (NT1 - 3) // 2)
            relu5(NT1 - 1, 0)
            evac_y5(NT1 - 2, 1, (NT1 - 3) // 2)
            evac_y5(NT1 - 1, 0, (NT1 - 1) // 2)
            for c in range(NCH):
                dve.wait_ge(s_gat5[c], 16 * CT)
                xc = X[:, c * CT:(c + 1) * CT, :]
                nc.vector.tensor_tensor(xc, xc, H[:, c * CT:(c + 1) * CT, :], ALU.add).then_inc(s_fin, 1)

        @block.tensor
        def _(pe):
            for primed in (s_pvd, m5_y, p3_yT):
                pe.sem_inc(primed, FIRST)
            pe.wait_ge(ld_c, 32)
            pe.wait_ge(ld_w, 16 * 11)
            for m in range(KC):
                for k in range(KC):
                    last = nc.tensor.matmul(PS[:, m, 0:B * LK], wk0[:, k, m * P:(m + 1) * P], ctxT[:, k, :],
                                            start=(k == 0), stop=(k == KC - 1))
                last.then_inc(pre_k, 1)
            pe.wait_ge(pre_ks, KC)
            for m in range(KC):
                for k in range(KC):
                    nc.tensor.matmul(PS[:, 2 + m, 0:B * LK], wq0T[:, k, m * P:(m + 1) * P], KT0[:, k, :],
                                     start=(k == 0), stop=(k == KC - 1))
            for k in range(KC):
                nc.tensor.matmul(PS[0:1, 4, 0:B * LK], bq0[:, k:k + 1], KT0[:, k, :], start=(k == 0), stop=(k == KC - 1))
            for b in range(B):
                for k in range(KC):
                    last = nc.tensor.matmul(PS[0:LK, 5 + b, 0:D], ctxT[:, k, b * LK:(b + 1) * LK], wv0[:, k, :],
                                            start=(k == 0), stop=(k == KC - 1))
            last.then_inc(pre_a, 1)
            pe.wait_ge(pre_as, 1)
            pe.wait_ge(pre_w, 2)
            with pe.Fori(0, B) as b:
                with pe.Fori(0, CPB) as cc:
                    c = b * CPB + cc
                    pe.wait_ge(s_z, c + 1)
                    pe.wait_ge(s_rt, c + FIRST)
                    for t in range(CT):
                        for k in range(KC):
                            last = nc.tensor.transpose(zT_ps[:, k, t * P:(t + 1) * P], Z[:, t, k * P:(k + 1) * P], ident)
                    last.then_inc(s_zT, 1)
                    pe.wait_ge(s_zTs, c + 1)
                    for t in range(CT):
                        for k in range(KC):
                            nc.tensor.matmul(sc_ps[:, t, 0:LK], ZT[:, k, t * P:(t + 1) * P], A0[:, k, ds(b * LK, LK)],
                                             start=(k == 0), stop=False)
                        last = nc.tensor.matmul(sc_ps[:, t, 0:LK], ones_row, CB0[:, ds(b * LK, LK)], start=False, stop=True)
                    last.then_inc(s_sc, 1)
                    pe.wait_ge(s_p, c + 1)
                    for t in range(CT):
                        last = nc.tensor.transpose(pT_ps[:, t * P:(t + 1) * P], P0[:, t, 0:LK], ident)
                    last.then_inc(s_pT, 1)
                    pe.wait_ge(s_pTs, c + 1)
                    pe.wait_ge(s_vs, c + FIRST)
                    for t in range(CT):
                        last = nc.tensor.matmul(o_ps[:, t:t + 1, :], PT0[:, t * P:(t + 1) * P], V0[:, ds(b, 1), :],
                                                start=True, stop=True)
                    last.then_inc(s_o, 1)
                    pe.wait_ge(s_u, c + 1)
                    for t in range(CT):
                        for k in range(KC):
                            last = nc.tensor.transpose(uT_ps[:, k, t * P:(t + 1) * P], U[:, t, k * P:(k + 1) * P], ident)
                    last.then_inc(s_uT, 1)
                    pe.wait_ge(s_uTs, c + 1)
                    for a in range(2):
                        for r in range(2):
                            for k in range(KC):
                                m = 2 * a + r
                                last = nc.tensor.matmul(qk_ps[:, a, r, :], wqk[:, k, m * P:(m + 1) * P], UT[:, k, :],
                                                        start=(k == 0), stop=(k == KC - 1))
                    last.then_inc(s_qk, 1)
                    for t in range(CT):
                        for k in range(KC):
                            last = nc.tensor.matmul(v_ps[:, t, :], UT[:, k, t * P:(t + 1) * P], wv[:, k, :],
                                                    start=(k == 0), stop=(k == KC - 1))
                    last.then_inc(s_v, 1)
            def max_unit(s, n, u):
                i, h0, nh, k0, w, masked = UNITS[u]
                pe.wait_ge(s_mfree, NU * s + u + 1)
                for h in range(nh):
                    dst = m_ps[u % 2][:, h * w:(h + 1) * w]
                    last = nc.tensor.matmul(dst, QT[0:QROWS, n, h0 + h, i * P:(i + 1) * P],
                                            KT[0:QROWS, n, h0 + h, k0:k0 + w], start=True, stop=not masked)
                    if masked:
                        last = nc.tensor.matmul(dst[:, w - P:w], identb, mask_q, start=False, stop=True)
                last.then_inc(s_mx, 1)

            def scores(s, n, k):
                c, j = STAGES[k]
                q0 = q0_of(c, j)
                for pair in range(2):
                    pe.wait_ge(s_sfree, 2 * NSTG * s + 2 * k + pair + 1)
                    for h in range(2):
                        hh = 2 * pair + h
                        dst = s_ps[pair][:, h, q0:CW]
                        masked = j >= CT * c
                        last = nc.tensor.matmul(dst, KT[0:AROWS, n, hh, j * P:(j + 1) * P],
                                                QT[0:AROWS, n, hh, c * CW + q0:(c + 1) * CW], start=True, stop=not masked)
                        if masked:
                            last = nc.tensor.matmul(dst[:, 0:P], identb, mask_k, start=False, stop=True)
                    last.then_inc(s_sT, 1)

            def weighted(s, n, k):
                c, j = STAGES[k]
                q0 = q0_of(c, j)
                if j == 0:
                    pe.wait_ge(s_yev, 2 * s + c + FIRST)
                pe.wait_ge(s_sfree, 2 * NSTG * s + 2 * k + 4)
                for h in range(GH):
                    last = nc.tensor.matmul(PS[VW * h:VW * (h + 1), 6, q0:CW], VS[:, n, j, h, :], PB[:, k % 2, h, q0:CW],
                                            start=(j == 0), stop=(j == CT * (c + 1) - 1))
                last.then_inc(s_pvd, 1)
                if j == CT * (c + 1) - 1:
                    pe.wait_ge(s_pvd, NSTG * s + k + 2 + FIRST)
                    pe.sem_inc(s_y, 1)

            def back(s, c):
                pe.wait_ge(s_yev, 2 * s + c + 1 + FIRST)
                for t in range(CT):
                    last = nc.tensor.transpose(t_ps[:, t * P:(t + 1) * P], YT[:, c, t * P:(t + 1) * P], ident)
                last.then_inc(s_yt, 1)

            def parts_T(s):
                pe.wait_ge(s_mp, s + 1)
                nc.tensor.transpose(t_ps.bitcast(bf16)[0:96, 0:P], MP.rearrange("p n h i -> p (n h i)"), identb).then_inc(s_mpt, 1)

            def pe_step(s, n, nxt, it):
                after = (n + 1) % BUFS
                pe.wait_ge(s_mrow, 16 * PARTS * (s + 1))
                pe.wait_ge(s_vst, s + 1)
                if nxt:
                    pe.wait_ge(ld_qk[after], 16 * NLD * (it + 1 + (n + 1) // BUFS))
                for k in range(NSTG):
                    scores(s, n, k)
                    if nxt:
                        half = (CUT[k] + CUT[k + 1] + 1) // 2
                        for u in range(CUT[k], half):
                            max_unit(s + 1, after, u)
                    if k:
                        weighted(s, n, k - 1)
                    if nxt:
                        for u in range(half, CUT[k + 1]):
                            max_unit(s + 1, after, u)
                    if k == 6:
                        back(s, 0)
                    if nxt and k == NSTG - 2:
                        pe.wait_ge(s_yn, 2 * s + 1)
                        parts_T(s + 1)
                weighted(s, n, NSTG - 1)
                if nxt:
                    pe.wait_ge(s_mt, s + 2)
                back(s, 1)

            pe.sem_inc(s_pvd, 1)
            pe.wait_ge(s_ini, 1)
            pe.wait_ge(s_ones, 16)
            pe.wait_ge(s_rt, NCH + FIRST)
            pe.wait_ge(s_vs, NCH + FIRST)
            pe.wait_ge(ld_qk[0], 16 * NLD)
            for u in range(NU):
                max_unit(0, 0, u)
            parts_T(0)
            with pe.Fori(0, (NS - 1) // BUFS) as it:
                for n in range(BUFS):
                    pe_step(BUFS * it + n, n, True, it)
            for s in range((NS - 1) // BUFS * BUFS, NS):
                pe_step(s, s % BUFS, s + 1 < NS, s // BUFS)
            pe.wait_ge(ld_3, 48)
            pe.wait_ge(s_yn, 2 * NS)
            with pe.Fori(0, NCH) as c:
                pe.wait_ge(p3_yc, c + 1)
                for t in range(CT):
                    for k in range(KC):
                        last = nc.tensor.transpose(yT3_ps[:, k, t * P:(t + 1) * P], YC[:, t, k * P:(k + 1) * P], ident)
                last.then_inc(p3_yT, 1)
                pe.wait_ge(p3_yTs, c + 1)
                for t in range(CT):
                    for k in range(KC):
                        last = nc.tensor.matmul(o3_ps[:, t, :], YCT[:, k, t * P:(t + 1) * P], WO[:, k, :], start=(k == 0), stop=(k == KC - 1))
                last.then_inc(p3_o, 1)
                pe.wait_ge(p3_xc, c + 1)
                for t in range(CT):
                    for k in range(KC):
                        last = nc.tensor.transpose(xT3_ps[:, k, t * P:(t + 1) * P], XC[:, t, k * P:(k + 1) * P], ident)
                last.then_inc(p3_xT, 1)
                pe.wait_ge(p3_xTs, c + 1)
                pe.wait_ge(p3_lgs, c + FIRST)
                for t in range(CT):
                    for k in range(KC):
                        last = nc.tensor.matmul(lg_ps[:, t, :], XCT[:, k, t * P:(t + 1) * P], WR[:, k, :], start=(k == 0), stop=(k == KC - 1))
                last.then_inc(p3_lg, 1)

            def prefix(dst, ones_zeros, done):
                nc.tensor.matmul(dst, tri_b, ones_zeros, start=True, stop=False)
                for d in range(1, NT):
                    last = nc.tensor.matmul(dst[:, d:NT, :], ones_b, ones_zeros[:, 0:NT - d, :], start=False, stop=(d == NT - 1))
                last.then_inc(done, 1)

            with pe.Fori(0, BITS) as i:
                pe.wait_ge(rt_ge, i + 1)
                nc.tensor.matmul(cnt_ps, ones_b, GEb, start=True, stop=True).then_inc(rt_cnt, 1)
            pe.wait_ge(rt_gt, 1)
            prefix(pfx_ps, EQb, rt_eqT)
            nc.tensor.matmul(cnt_ps, ones_b, GEb, start=True, stop=True).then_inc(rt_ngt, 1)
            pe.wait_ge(rt_keep, 1)
            prefix(pos_ps, KEEPb, rt_pos)

            def rows_T(n, count):
                pe.wait_ge(ld_xe[n], 32 * count)
                for t, w in ((0, P), (1, P), (2, TAIL)):
                    for k in range(KC):
                        last = nc.tensor.transpose(xeT_ps[:, k, t * P:t * P + w], XEB[0:w, n, t, k * P:(k + 1) * P], ident[0:w, 0:w])
                last.then_inc(me_xT, 1)

            pe.wait_ge(rt_idx, 1)
            rows_T(0, 1)

            def expert_mlp(e, n, it, nxt):
                pe.wait_ge(me_xTs, e + 1)
                pe.wait_ge(ld_we[n], 32 * (it + 1))
                for f in range(FC0):
                    for k in range(KC):
                        last = nc.tensor.matmul(he_ps[:, f, :], W1E[:, n, k, f * P:(f + 1) * P], XET[:, n, k, :], start=(k == 0), stop=(k == KC - 1))
                last.then_inc(me_h, 1)
                if nxt:
                    rows_T(1 - n, it + 1 + n)
                pe.wait_ge(me_hs, e + 1)
                pe.wait_ge(me_ys, e + FIRST)
                for t, w in ((0, P), (1, P), (2, TAIL)):
                    for f in range(FC0):
                        last = nc.tensor.matmul(ye_ps[0:w, t, :], HTE[:, f, t * P:t * P + w], W2E[:, n, f, :], start=(f == 0), stop=(f == FC0 - 1))
                last.then_inc(me_y, 1)

            with pe.Fori(0, E // 2 - 1) as it:
                for n in range(2):
                    expert_mlp(2 * it + n, n, it, True)
            expert_mlp(E - 2, 0, E // 2 - 1, True)
            expert_mlp(E - 1, 1, E // 2 - 1, False)
            pe.wait_ge(ld_4, 16 * 11)
            pe.wait_ge(me_hs, E)
            for m in range(KC):
                for k in range(KC):
                    last = nc.tensor.matmul(PS[:, m, 0:B * LK], WK1[:, k, m * P:(m + 1) * P], CT1[:, k, :], start=(k == 0), stop=(k == KC - 1))
                last.then_inc(k4_k, 1)
            for b in range(B):
                for k in range(KC):
                    last = nc.tensor.matmul(PS[0:LK, 2 + b, 0:D], CT1[:, k, b * LK:(b + 1) * LK], WV1[:, k, :], start=(k == 0), stop=(k == KC - 1))
            last.then_inc(k4_v, 1)
            pe.wait_ge(k4_kb, 1)
            pe.wait_ge(k4_vs, 2)
            pe.wait_ge(me_ys, E + FIRST)

            def rows_T4(rows, done):
                for t in range(CT):
                    for k in range(KC):
                        last = nc.tensor.transpose(zT4_ps[:, k, t * P:(t + 1) * P], rows[:, t, k * P:(k + 1) * P], ident)
                last.then_inc(done, 1)

            def enter_zT(c):
                pe.wait_ge(q4_z, c + 1)
                if c > 1:
                    pe.wait_ge(q4_var3, c - 1)
                rows_T4(Z4, q4_zT)

            def enter_q(c):
                pe.wait_ge(q4_zTs, c + 1)
                for m in range(KC):
                    for k in range(KC):
                        last = nc.tensor.matmul(q4_ps[:, m, :], WQ1[:, k, m * P:(m + 1) * P], Z4T[:, k, :], start=(k == 0), stop=(k == KC - 1))
                last.then_inc(q4_q, 1)

            def scores4(c, t):
                if t == 0:
                    pe.wait_ge(q4_qs, c + 1)
                if c or t:
                    pe.wait_ge(q4_sub, c * CT + t)
                for bank, off, k, h0, nh in SC4:
                    last = nc.tensor.matmul(sc4_ps[:, bank, off * LK:(off + nh) * LK], Q4T[:, c % 2, k, t * P:(t + 1) * P],
                                            KBD[:, c // CPB, k, h0:h0 + nh, :].rearrange("p h k -> p (h k)"), start=True, stop=True)
                last.then_inc(q4_sc, 1)

            def leave_oT(c):
                pe.wait_ge(q4_on, (c + 1) * CT)
                if c:
                    pe.wait_ge(q4_gs, c)
                rows_T4(O4, q4_oT)

            def leave_out(c):
                pe.wait_ge(q4_oTs, c + 1)
                for t in range(CT):
                    for k in range(KC):
                        last = nc.tensor.matmul(out4_ps[:, t, :], Z4T[:, k, t * P:(t + 1) * P], WO1[:, k, :], start=(k == 0), stop=(k == KC - 1))
                last.then_inc(q4_out, 1)

            def leave_z3T(c):
                pe.wait_ge(q4_z3, c + 1)
                if c + 2 < NCH:
                    pe.wait_ge(q4_qs, c + 3)
                rows_T4(H[:, c * CT:(c + 1) * CT], q4_z3T)

            def leave_gates(c):
                pe.wait_ge(q4_z3Ts, c + 1)
                for t in range(CT):
                    for k in range(KC):
                        nc.tensor.matmul(gate_ps[:, t, :], Z4T[:, k, t * P:(t + 1) * P], WG[:, k, :], start=(k == 0), stop=False)
                    last = nc.tensor.matmul(gate_ps[:, t, :], ones_row, BG, start=False, stop=True)
                last.then_inc(q4_g, 1)

            def weights_T(c, t, q):
                n = (c * CT + t) * NQ + q
                pe.wait_ge(q4_p, c * CT + t + 1)
                if n > 1:
                    pe.wait_ge(q4_pTs, n - 1)
                for h in range(QH):
                    last = nc.tensor.transpose(pT4_ps[q % 2][:, h, :], SS[:, t % 2, q * QH + h, :], ident)
                last.then_inc(q4_pT, 1)

            def heads(c, t, q):
                pe.wait_ge(q4_pTs, (c * CT + t) * NQ + q + 1)
                if q == 0 and (c or t):
                    pe.wait_ge(q4_on, c * CT + t)
                for h in range(q * QH, (q + 1) * QH):
                    last = nc.tensor.matmul(o4_ps[:, h, :], PT4[:, h, :], V1[:, c // CPB, h, :], start=True, stop=True)
                if q == NQ - 1:
                    last.then_inc(q4_o, 1)

            enter_zT(0)
            enter_q(0)
            scores4(0, 0)
            for c in range(NCH):
                for t in range(CT):
                    for q in range(NQ):
                        weights_T(c, t, q)
                        if q:
                            heads(c, t, q - 1)
                        elif c or t:
                            heads(c - (t == 0), (t - 1) % CT, NQ - 1)
                        if q == 0 and t + 1 < CT:
                            scores4(c, t + 1)
                        if (t, q) == (0, 1) and c:
                            leave_oT(c - 1)
                        if (t, q) == (0, 3) and c:
                            leave_out(c - 1)
                        if (t, q) == (2, 3) and c + 1 < NCH:
                            enter_zT(c + 1)
                        if (t, q) == (3, 0) and c + 1 < NCH:
                            enter_q(c + 1)
                        if (t, q) == (3, 1) and c + 1 < NCH:
                            scores4(c + 1, 0)
                        if (t, q) == (3, 2) and c:
                            leave_z3T(c - 1)
                        if (t, q) == (3, 3) and c:
                            leave_gates(c - 1)
            heads(NCH - 1, CT - 1, NQ - 1)
            leave_oT(NCH - 1)
            leave_out(NCH - 1)
            leave_z3T(NCH - 1)
            leave_gates(NCH - 1)
            pe.wait_ge(q4_gs, NCH)
            pe.wait_ge(r5_sel, 1)
            nc.tensor.matmul(cnt_ps, ones_b, SELF5, start=True, stop=True).then_inc(r5_cnt, 1)
            prefix(pos_ps, SELF5, r5_pos)

            def xT5(j, n, it):
                pe.wait_ge(ld_xs[n], 16 * (it + 1))
                pe.wait_ge(m5_xTs, j)
                for k in range(KC):
                    last = nc.tensor.transpose(xT5_ps[:, k, :], XS5[:, n, k * P:(k + 1) * P], ident)
                last.then_inc(m5_xT, 1)

            def h5(j, n):
                pe.wait_ge(m5_xTs, j + 1)
                pe.sem_inc(s_spare, 1)
                e = pe.value_load(TEI[0:1, ds(j, 1)], min_val=0, max_val=E - 1)
                for f in range(F1 // 512):
                    for k in range(KC):
                        nc.tensor.matmul(h5_ps[n][:, f, :], XT5[:, n, k, :],
                                         W1S[:, ds(e, 1), k, f * 512:(f + 1) * 512].squeeze(1), start=(k == 0), stop=False)
                    last = nc.tensor.matmul(h5_ps[n][:, f, :], ones3, BPS[:, ds(e * F1 + f * 512, 512)], start=False, stop=True)
                last.then_inc(m5_h, 1)

            def hT5(j, n):
                pe.wait_ge(m5_hs, j + 1)
                pe.wait_ge(m5_hTs, j + FIRST)
                for f in range(FC1):
                    last = nc.tensor.transpose(hT5_ps[:, f, :], HS5[:, n, f * P:(f + 1) * P], ident)
                last.then_inc(m5_hT, 1)

            def y5(j):
                pe.wait_ge(m5_hTs, j + 1 + FIRST)
                pe.wait_ge(m5_ys, j + FIRST)
                pe.sem_inc(s_spare, 1)
                e = pe.value_load(TEI[0:1, ds(j, 1)], min_val=0, max_val=E - 1)
                at = pe.value_load(TEP[0:1, ds(j, 1)], min_val=0, max_val=E - 1)
                for f in range(FC1):
                    nc.tensor.matmul(y5_ps, HT5[:, f, :], W2S[:, ds(at, 1), f, :].squeeze(1), start=(f == 0), stop=False)
                nc.tensor.matmul(y5_ps, ones3, BPS[:, ds(e * D + NB1, D)], start=False, stop=True).then_inc(m5_y, 1)

            pe.wait_ge(r5_idx, 2)
            xT5(0, 0, 0)
            pe.wait_ge(ld_bp, 16)
            pe.wait_ge(ld_5, 16 * 2 * E)
            h5(0, 0)
            xT5(1, 1, 0)
            with pe.Fori(0, (NT1 - 3) // 2) as it:
                for n in range(2):
                    j = 2 * it + n
                    hT5(j, n)
                    h5(j + 1, 1 - n)
                    xT5(j + 2, n, it + 1)
                    y5(j)
            last_it = (NT1 - 1) // 2
            hT5(NT1 - 3, 0)
            h5(NT1 - 2, 1)
            xT5(NT1 - 1, 0, last_it)
            y5(NT1 - 3)
            hT5(NT1 - 2, 1)
            h5(NT1 - 1, 0)
            y5(NT1 - 2)
            hT5(NT1 - 1, 0)
            y5(NT1 - 1)


def _consts(D, S, NT, E, CAP):
    import numpy as np
    P = 128
    i = np.arange(P)
    cf = np.zeros((P, 3 * P + 96), np.float32)
    cf[:, 0:P] = np.eye(P)
    cf[:, P:2 * P] = i[:, None] < i[None, :]
    cf[:, 2 * P:3 * P] = 1.0
    o = 3 * P
    cf[:, o:o + E] = E - np.arange(E)
    cf[:, o + E:o + 2 * E] = np.arange(E) * CAP - E * CAP
    cf[:, o + 2 * E:o + 2 * E + 16] = P * np.arange(16)
    cf[:, o + 32:o + 32 + NT + E - 1] = np.arange(NT + E - 1)
    cf[:, o + 64:o + 64 + NT] = -0.5
    cf[:, o + 80:o + 88] = (i[:, None] // 16) == np.arange(8)[None, :]
    cf[:, o + 88:o + 96] = 2.0 ** -63
    cb = np.zeros((P, 5 * P), np.float32)
    cb[:, 0:P] = np.eye(P)
    cb[:, P:2 * P] = np.where(i[None, :] > i[:, None], -1.0e30, 0.0)
    cb[:, 2 * P:3 * P] = np.where(i[:, None] > i[None, :], -1.0e30, 0.0)
    cb[:, 3 * P:4 * P] = 1.0
    cb[:, 4 * P:5 * P] = i[:, None] < i[None, :]
    theta = (10000.0 ** (-2.0 * (np.arange(8, dtype=np.float32) / np.float32(16)))).astype(np.float32)
    pair = (i % 32) // 4
    angle = (np.arange(S, dtype=np.float32)[None, :] * theta[pair][:, None]).astype(np.float32).astype(np.float64)
    rope = np.stack([np.cos(angle), np.sin(angle)], 1).astype(np.float32)
    return cf, cb.astype(mybir.dt.np(mybir.dt.bfloat16)), rope


def _lay_out(i):
    import numpy as np
    P = 128

    def rows(w):
        return w.reshape(-1, P, w.shape[1]).transpose(1, 0, 2)

    def column(v):
        return v.reshape(-1, P).T

    x, ctx = i["x"], i["ctx_1024"]
    D = x.shape[2]
    cf, cb, rope = _consts(D, x.shape[1], x.shape[0] * x.shape[1] // P, 8, 320)
    wqkv = i["L0_ffn_w_qkv"]
    p = np.arange(P)
    g, pair, hh = p // 32, (p % 32) // 4, p % 4
    cols = [a * D + (4 * g + hh) * 16 + 2 * pair + r for a in range(2) for r in range(2)]
    wqk = wqkv[:, np.concatenate(cols)]
    return dict(
        x=x, ctxT=rows(ctx.transpose(2, 0, 1).reshape(D, -1)), const_f=cf, const_b=cb, rope=rope,
        wq0T=rows(i["L0_xattn_Wq"].T), bq0=column(i["L0_xattn_bq"]), wk0=rows(i["L0_xattn_Wk"]),
        bk0=column(i["L0_xattn_bk"]), wv0=rows(i["L0_xattn_Wv"]), bv0=i["L0_xattn_bv"],
        g1=column(i["L0_ffn_g1"]), wqk=rows(wqk), wv=rows(wqkv[:, 2 * D:]), wo=rows(i["L0_ffn_w_o"]),
        g2=i["L0_ffn_g2"], wr=rows(i["L0_ffn_w_router"]), w1e=i["L0_ffn_w1"], w2e=i["L0_ffn_w2"],
        wq1=rows(i["L1_xattn_Wq"].T), bq1=column(i["L1_xattn_bq"]), wk1=rows(i["L1_xattn_Wk"].T),
        bk1=column(i["L1_xattn_bk"]), wv1=rows(i["L1_xattn_Wv"].T), bv1=i["L1_xattn_bv"],
        wo1=rows(i["L1_xattn_Wo"].T), bo1=i["L1_xattn_bo"], wg=rows(i["L1_ffn_Wg"]), bg=i["L1_ffn_bg"],
        w1=i["L1_ffn_W1"], b1=i["L1_ffn_b1"], w2=i["L1_ffn_W2"], b2=i["L1_ffn_b2"])


def kernel(**inputs):
    import numpy as _np
    import concourse.bacc as _bacc
    from concourse import mybir as _mybir
    from concourse.bass_utils import run_bass_kernel_spmd as _run

    nc = _bacc.Bacc("TRN2", target_bir_lowering=False, num_devices=1)
    arrays, args = {}, []
    for name, a in _lay_out({k: _np.asarray(v) for k, v in inputs.items()}).items():
        a = _np.ascontiguousarray(a)
        arrays[name + "_dram"] = a
        args.append(nc.dram_tensor(name + "_dram", a.shape, _mybir.dt.from_np(a.dtype), kind="ExternalInput").ap())
    shape = inputs["x"].shape
    args.append(nc.dram_tensor("out_dram", shape, _mybir.dt.float32, kind="ExternalOutput").ap())
    build_program(nc, *args)
    r = _run(nc, [arrays], core_ids=[0])
    return r.results[0]["out_dram"]
```

```python
import concourse.bass as bass
from concourse import mybir
from contextlib import ExitStack


class Chain:

    def __init__(self, eng, sem):
        self.eng, self.sem, self.base, self.n, self.i, self.per = eng, sem, 0, 0, None, 0

    def value(self):
        at = self.base + self.n
        return at if self.i is None else self.i * self.per + at

    def enter(self, i, per):
        self.base, self.n, self.i, self.per = self.base + self.n, 0, i, per

    def leave(self, passes):
        assert self.n == self.per, (self.n, self.per)
        self.base, self.n, self.i = self.base + passes * self.per, 0, None

    def __call__(self, ins):
        self.n += 1
        ins.then_inc(self.sem, 1)
        self.eng.wait_ge(self.sem, self.value())


def build_program(nc, x_in, ctxT_in, const_f_in, const_b_in, rope_in,
                  wq0T_in, bq0_in, wk0_in, bk0_in, wv0_in, bv0_in,
                  g1_in, wqk_in, wv_in, wo_in, g2_in, wr_in, w1e_in, w2e_in,
                  wq1_in, bq1_in, wk1_in, bk1_in, wv1_in, bv1_in, wo1_in, bo1_in,
                  wg_in, bg_in, w1_in, b1_in, w2_in, b2_in, out):
    f32, bf16 = mybir.dt.float32, mybir.dt.bfloat16
    i32, u32 = mybir.dt.int32, mybir.dt.uint32
    ALU, ACT, AX = mybir.AluOpType, mybir.ActivationFunctionType, mybir.AxisListType
    ds = bass.ds

    P = 128
    B, S, D = x_in.shape
    KC = D // P
    NT = B * S // P
    CT = 4
    CW = CT * P
    CPB = S // CW
    NCH = B * CPB
    LK = ctxT_in.shape[2] // B
    HEADS, HD = 16, 16
    GH = 4
    NG = HEADS // GH
    NS = B * NG
    PARTS = 3
    RUNS = (3, 2, 1)
    QROWS = sum(RUNS) * HD
    AROWS = QROWS + PARTS
    E = 8
    BITS, BSTEP = 30, 3
    NCAND = 2 ** BSTEP - 1
    F0 = w1e_in.shape[2]
    FC0 = F0 // P
    CAP = 320
    SLOTS0 = E * CAP
    F1 = w1_in.shape[2]
    FC1 = F1 // P
    NT1 = NT + E - 1
    SLOTS1 = NT1 * P
    BUFS = 3
    VW = 32
    NEG = -1.0e30
    LN_EPS, RMS_EPS = 1e-5, 1e-6

    ctx = ExitStack()
    with ctx:
        def sb(name, shape, dt=f32):
            return ctx.enter_context(nc.sbuf_tensor(name, shape, dt))

        def sem(name):
            return ctx.enter_context(nc.semaphore(name))

        qk_dram = nc.dram_tensor("qk_dram", (2, NS, PARTS, 2, 32, S), bf16, kind="Internal").ap()
        xe_dram = nc.dram_tensor("xe_dram", (SLOTS0, D), f32, kind="Internal").ap()
        ye_dram = nc.dram_tensor("ye_dram", (SLOTS0 + 1, D), f32, kind="Internal").ap()
        xs_dram = nc.dram_tensor("xs_dram", (SLOTS1, D), f32, kind="Internal").ap()
        ys_dram = nc.dram_tensor("ys_dram", (SLOTS1, D), f32, kind="Internal").ap()
        bp_dram = nc.dram_tensor("bp_dram", (PARTS, E * (F1 + D)), bf16, kind="Internal").ap()

        X = sb("X", [P, NT, D])
        H = sb("H", [P, NT, D])
        XF = sb("XF", [P, NT, D])
        CF = sb("CF", [P, const_f_in.shape[1]])
        CB = sb("CB", [P, const_b_in.shape[1]], bf16)
        ident = CF[:, 0:P]
        CO = 3 * P
        w8 = CF[:, CO:CO + E]
        base0 = CF[:, CO + E:CO + 2 * E]
        j128 = CF[:, CO + 2 * E:CO + 2 * E + 16]
        jt = CF[0:1, CO + 32:CO + 32 + NT1]
        neg_half = CF[:, CO + 64:CO + 64 + NT]
        headmask = CF[:, CO + 80:CO + 88]
        ones_row = CF[0:1, 2 * P:3 * P]
        identb = CB[:, 0:P]
        mask_q = CB[:, P:2 * P]
        mask_k = CB[:, 2 * P:3 * P]
        ones_b = CB[:, 3 * P:4 * P]
        tri_b = CB[:, 4 * P:5 * P]
        ones3 = CB[0:PARTS, 3 * P:4 * P]
        top_bits = CF[:, CO + 88:CO + 88 + NCAND]

        REG = sb("REG", [P, 2 * E * KC * F1])

        class Carve:
            def __init__(self, at=0, buf=None):
                self.at, self.buf = at, REG if buf is None else buf

            def __call__(self, shape, dt=f32, parts=P):
                n = 1
                for m in shape:
                    n *= m
                words = n if dt == f32 else n // 2
                a = self.buf[0:parts, self.at:self.at + words]
                self.at += words
                assert self.at <= self.buf.shape[1], self.at
                if dt != f32:
                    a = a.bitcast(dt)
                names = "abcd"[:len(shape)]
                if len(shape) > 1:
                    a = a.rearrange(f"p ({' '.join(names)}) -> p {' '.join(names)}",
                                    **{k: m for k, m in zip(names[1:], shape[1:])})
                return a

        c1 = Carve()
        VB = c1((NS, S // P, GH * HD))
        after_v = c1.at
        ctxT = c1((KC, B * LK))
        wq0T, wk0, wv0 = c1((KC, D)), c1((KC, D)), c1((KC, D))
        bq0, bk0, g1c = c1((KC,)), c1((KC,)), c1((KC,))
        bv0 = c1((D,))
        KT0 = c1((KC, B * LK))
        A0 = c1((KC, B * LK))
        CB0 = c1((B * LK,), f32, 1)
        V0 = c1((B, D), f32, LK)
        wqk, wv = c1((KC, 4 * P)), c1((KC, D))
        rope = c1((2, S))
        Z = c1((CT, D))
        ZT = c1((KC, CW))
        P0 = c1((CT, LK + 1))
        PT0 = c1((CW,), f32, LK)
        U = c1((CT, D))
        UT = c1((KC, CW))
        RT = c1((4, 2, CW))
        ROT = c1((2, 2, CW))
        PARTB = c1((PARTS, 2, 2, CW), bf16)
        XB = sb("XB", [P, 6928])
        cx = Carve(0, XB)
        KT = cx((BUFS, GH, S), bf16)
        WO = cx((KC, D))
        WR = cx((KC, E))
        G2 = cx((D,))
        c1.at = max(c1.at, REG.shape[1] - BUFS * GH * S // 2 - 320)
        MXP = c1((GH, 2 * CT, 2))
        NM = c1((GH, 2 * CT))
        NR = c1((GH, 2 * CT))
        MP = c1((PARTS, GH, 2 * CT), bf16)
        MT = c1((P,), bf16)
        QT = c1((BUFS, GH, S), bf16)
        c2 = Carve(after_v)
        PB = c2((2, GH, CW))
        VS = c2((BUFS, S // P, GH, VW))
        YT = c2((2, CW))
        RY = c2((CT, GH))
        ST = sb("ST", [P, CT, 6])
        MV = sb("MV", [P, CT, 2])
        SM = sb("SM", [P, 12, CT])
        VE, RSTD, MX, NB, RSUM, RRS, R1, S1, VE1, VE2, R2, TV = (SM[:, n, :] for n in range(12))
        R3 = (R2, RSTD)
        R1S1, VE12 = (SM[:, n:n + 2, :].rearrange("p a t -> p (a t)") for n in (6, 8))
        LG = sb("LG", [P, NT, E])

        ZERO = XF[:, 0:4, :].rearrange("p a d -> p (a d)")

        PS = ctx.enter_context(nc.psum_tensor("PS", [P, 8, 512], f32))

        s_spare = sem("spare")
        ld_wp, ld_tab = sem("ld_projections"), sem("ld_tables")
        ld_x, ld_xr, ld_c, ld_w = sem("ld_x"), sem("ld_x_rest"), sem("ld_consts"), sem("ld_weights1")
        s_chv, s_chp = sem("vector_chain"), sem("pool_chain")
        pre_k, pre_ks, pre_a, pre_as, pre_w = (sem("pre_" + n) for n in ("k", "ks", "a", "as", "w"))
        (s_var, s_rstd, s_z, s_zT, s_zTs, s_sc, s_nb, s_p, s_pT, s_pTs, s_o, s_var2, s_rstd2, s_u, s_uT, s_uTs,
         s_q, s_k, s_v, s_rq, s_rt, s_vs, s_rot, s_hi, s_res, s_mid, s_lo, s_qkst) = (
            sem("p1_" + n) for n in ("var", "rstd", "z", "zT", "zTs", "sc", "nb", "p", "pT", "pTs", "o", "var2",
                                     "rstd2", "u", "uT", "uTs", "q", "k", "v", "rope_q", "rt", "vs", "rot", "hi", "res", "mid",
                                     "lo", "qkst"))
        NK = S // P
        UNITS = []
        for i in range(NK):
            w = (i % CT + 1) * P
            per = max(1, 512 // w) if w != 3 * P else 1
            for h0 in range(0, GH, per):
                UNITS.append((i, h0, per, (i // CT) * CW, w, True))
            if i >= CT:
                for h0 in range(GH):
                    UNITS.append((i, h0, 1, 0, CW, False))
        NU = len(UNITS)
        STAGES = [(c, j) for c in range(CPB) for j in range(CT * (c + 1))]
        NSTG = len(STAGES)
        MSTG = NSTG - 3

        def q0_of(c, j):
            return max(0, P * (j - CT * c))

        def share():
            cost = [nh * w for _, _, nh, _, w, _ in UNITS]
            width = [CW - q0_of(c, j) for c, j in STAGES]
            rate = sum(cost) / sum(width)
            cut, done, u = [], 0, 0
            for k in list(range(MSTG, NSTG)) + list(range(MSTG)):
                if k == 0:
                    lead = u
                done, u0 = done + width[k] * rate, u
                while u < NU and sum(cost[:u]) + cost[u] / 2 <= done:
                    u += 1
                cut.append((u0, u))
            assert u == NU
            return cut[NSTG - MSTG:] + cut[:NSTG - MSTG], lead

        CUT, LEAD = share()
        NEND = 2
        for k in range(MSTG, NSTG):
            CUT[k] = tuple(min(u, LEAD - NEND) for u in CUT[k])

        def units(k, nxt, lead, do, half=None):
            u0, u1 = CUT[k]
            mid = (u0 + u1 + 1) // 2
            u0, u1 = {None: (u0, u1), 0: (u0, mid), 1: (mid, u1)}[half]
            for u in range(u0, u1):
                if k < MSTG and nxt:
                    do(1, u)
                if k >= MSTG and lead:
                    do(2, u)

        NLD = 2 * len(RUNS)
        m_ps = [PS[:, n, :] for n in range(2)]
        s_ps = [PS[:, 2 + 2 * n:4 + 2 * n, :] for n in range(2)]
        y_ps = PS[:, 6, :]
        t_ps = PS[:, 7, :]
        ld_qk = [sem(f"ld_qk{n}") for n in range(BUFS)]
        (s_mx, s_mfree, s_mp, s_mpt, s_mt, s_mrow, s_sT, s_sfree, s_pvd, s_y, s_yev, s_yt, s_yn, s_vst) = (
            sem("p2_" + n) for n in ("max_scores", "max_bank_free", "maxparts", "maxparts_T", "maxT",
                                     "maxrows", "scoresT", "exp_done", "pv_done", "y", "y_evac", "y_T", "y_norm",
                                     "v_staged"))

        c3 = Carve(0, XB)
        YCT = c3((KC, CW))
        XCT = c3((KC, CW))
        c3r = Carve(E * KC * F1)
        PR, G, SEL1, SEL2, TE1, TE2, EX = (c3r((NT, E)) for _ in range(7))
        GEb, EQb, KEEPb = (c3r((NT, E), bf16) for _ in range(3))
        M1, M2, VM, SU, RSU, GATE1, GATE2, IDF = (c3r((NT,)) for _ in range(8))
        CUR, CNT, TM, NGT = (c3r((E,)) for _ in range(4))
        CAND, TK = c3r((NCAND, E)), c3r((NCAND, E))
        STEP_BITS = c3r((8,))[:, 0:NCAND]
        REACH = c3r((NT, NCAND, E), bf16)
        IDX1, IDX2 = (c3r((NT,)).bitcast(u32) for _ in range(2))
        gathered_at = c3r.at
        XEB = c3r((2, 3, D))
        XET = c3r((2, KC, CAP))
        HTE = c3r((2, FC0, CAP))
        assert c3.at <= BUFS * GH * S // 2
        W1E = c3r((2, KC, F0))
        W2E = c3r((2, FC0, D))
        YEB = c3r((2, 3, D))
        TAIL = CAP - 2 * P
        ld_5 = sem("ld_last_experts")
        ld_3, ld_w1e, ld_w2e, ld_xe = (sem("ld_phase3"),) + tuple([sem(f"ld_{w}{n}") for n in range(2)] for w in ("w1e", "w2e", "xe"))
        (p3_yT, p3_yTs, p3_o, p3_h, p3_ms, p3_r, p3_xc, p3_xT, p3_xTs, p3_lg, p3_lgs) = (
            sem("p3_" + n) for n in ("yT", "yTs", "o", "h", "ms", "r", "xc", "xT", "xTs", "lg", "lgs"))
        (rt_sub, rt_exp, rt_ge, rt_cnt, rt_keep, rt_pos, rt_idx, rt_eqT) = (
            sem("route_" + n) for n in ("sub", "exp", "ge", "count", "keep", "pos", "idx", "eq_prefix"))
        s_scat = sem("scattered")
        (me_xT, me_xTs, me_h, me_hs, me_y, me_ys, me_out) = (
            sem("moe0_" + n) for n in ("xT", "xTs", "h", "hs", "y", "ys", "out"))
        ncand_ps = PS[:, 0, 0:NCAND * E].rearrange("p (j e) -> p j e", j=NCAND)
        yT3_ps, o3_ps = PS[:, 0:2, :], PS[:, 2:4, :].rearrange("p a (t d) -> p (a t) d", t=2)
        xT3_ps, lg_ps = PS[:, 4:6, :], PS[:, 6, 0:CT * E].rearrange("p (t e) -> p t e", t=CT)
        cnt_ps = PS[:, 0, 0:NT * E].rearrange("p (t e) -> p t e", t=NT)
        pfx_ps = PS[:, 1, 0:NT * E].rearrange("p (t e) -> p t e", t=NT)
        pos_ps = PS[:, 2, 0:NT * E].rearrange("p (t e) -> p t e", t=NT)
        xeT_ps = PS[:, 0:2, 0:CAP]
        he_ps = PS[:, 2:6, 0:CAP]
        ye_ps = PS[:, 6:8, :].rearrange("p a (t d) -> p (a t) d", t=2)
        HW = HD + 1
        c4 = Carve(0, XB)
        KBD = c4((B, KC, 8, LK))
        V1 = c4((B, HEADS, HW), f32, LK)
        NBLK = -(-HEADS * LK // P)
        SSB = c4((2, NBLK * P))
        SS = SSB[:, :, 0:HEADS * LK].rearrange("p n (h k) -> p n h k", h=HEADS)
        BO = c4((D,))
        WG = c4((KC, E))
        BG = c4((E,), f32, 1)
        BQ1 = c4((KC,))
        BK1 = c4((KC,))
        MX4 = c4((HEADS,))
        RO = c4((HEADS,))
        XFF = XF[:].rearrange("p t d -> p (t d)")
        HWIN = [(P * j // LK, min(HEADS, (P * (j + 1) - 1) // LK + 1)) for j in range(NBLK)]
        MAXH = max(h1 - h0 for h0, h1 in HWIN)
        VBD = c4((B, NBLK, MAXH, HW))
        c4f = Carve(0, XFF)
        Z4 = c4f((CT, D))
        Z4T = c4f((KC, CW))
        PT4 = c4f((NBLK, P))
        ZB = c4f((HEADS * HW,), bf16, 1)
        c4r = Carve(gathered_at)
        GB = c4r((CT, 2, D))
        WQ1, WO1 = c4r((KC, D)), c4r((KC, D))
        O4 = c4r((CT, D))
        Q4T = c4r((2, KC, CW))
        assert c4r.at <= 3 * E * KC * F1 // 2
        CT1, WK1, WV1 = c3r((KC, B * LK)), c3r((KC, D)), c3r((KC, D))
        KT1 = c3r((KC, B * LK))
        BV1 = c3r((D,))
        sc4_ps = PS[:, 0:3, 0:6 * LK]
        UBLK = [range(j, min(j + 4, NBLK)) for j in range(0, NBLK, 4)]
        NQ = len(UBLK)
        pT4_ps = [PS[:, 3 + n, :].rearrange("p (j n) -> p j n", j=4) for n in range(2)]
        o4_ps = PS[:, 5, 0:HEADS * HW].rearrange("p (h n) -> p h n", h=HEADS)
        o4f_ps = PS[:, 5, 0:HEADS * HW]
        zT4_ps = q4_ps = PS[:, 6:8, :]
        out4_ps = PS[:, 6:8, :].rearrange("p a (t d) -> p (a t) d", t=2)
        gate_ps = PS[:, 6, 0:CT * E].rearrange("p (t e) -> p t e", t=CT)
        SC4 = [(0, 0, 0, 0, 6), (1, 0, 0, 6, 2), (1, 2, 1, 0, 4), (2, 0, 1, 4, 4)]
        ld_4, k4_vb = sem("ld_phase4"), sem("pre4_v_blocks")
        s_gath = sem("gathered")
        (k4_k, k4_ks, k4_kb, k4_v, k4_vs) = (sem("pre4_" + n) for n in ("k", "ks", "kbd", "v", "vs"))
        (q4_x, q4_var, q4_r, q4_z, q4_bo, q4_zT, q4_zTs, q4_q, q4_qs, q4_sc, q4_sub, q4_p, q4_pT, q4_pTs,
         q4_o, q4_on, q4_oT, q4_oTs, q4_out, q4_xo, q4_var3, q4_r3, q4_z3, q4_z3T, q4_z3Ts, q4_g, q4_gs) = (
            sem("p4_" + n) for n in ("x", "var", "r", "z", "bo", "zT", "zTs", "q", "qs", "scores", "sub", "p",
                                     "pT", "pTs", "o", "on", "oT", "oTs", "out", "xo", "var3", "r3", "z3",
                                     "z3T", "z3Ts", "g", "gs"))
        W1S = REG[:, 0:E * KC * F1].rearrange("p (e k f) -> p e k f", e=E, k=KC)
        W2S = REG[:, E * KC * F1:2 * E * KC * F1].rearrange("p (e k d) -> p e k d", e=E, k=FC1)
        EH = E // 2
        NB1, NB2 = E * F1, E * D
        c5 = Carve(0, XB)
        BPS = c5((NB1 + NB2,), bf16, PARTS)
        YB5 = c5((2, D))
        T5, SEL5, SELF5 = c5((NT, E)), c5((NT, E)), c5((NT, E), bf16)
        M5, IDF5 = c5((NT,)), c5((NT,))
        IDX5 = c5((NT,)).bitcast(u32)
        CN, NTL, CUM, OFFS = (c5((E,)) for _ in range(4))
        CMP = c5((E, NT))
        TEX = c5((NT1, E - 1), f32, 1)
        TEF, TEG = c5((NT1,), f32, 1), c5((NT1,), f32, 1)
        TEI, TEP = c5((NT1,), f32, 1).bitcast(i32), c5((NT1,), f32, 1).bitcast(i32)
        BBF = c5(((NB1 + NB2) // P,))
        BBR = c5(((NB1 + NB2) // P,))
        BBP = c5((PARTS, (NB1 + NB2) // P), bf16)
        c5f = Carve(0, XFF)
        XS5 = c5f((2, D))
        XT5 = c5f((2, KC, P))
        HT5 = c5f((2, FC1, P))
        W1C = [H[:, 8 * n:8 * n + 8, :].rearrange("p t d -> p (t d)").rearrange("p (k f) -> p k f", k=KC) for n in range(2)]
        assert KC * F1 == 8 * D
        ld_b, ld_b2, ld_bp = sem("ld_bias"), sem("bias_parts_out"), sem("ld_bias_parts")
        m5_out = [sem(f"p5_rows_out{n}") for n in range(2)]
        ld_xs = [sem(f"ld_xs{n}") for n in range(2)]
        s_gat5 = [sem(f"gathered5_{c}") for c in range(NCH)]
        (b5_p, r5_sel, r5_pos, r5_cnt, r5_idx, s_scat5, m5_w, m5_xT, m5_xTs, m5_h, m5_hs, m5_y, m5_ys, s_fin, s_out) = (
            sem("p5_" + n) for n in ("bias_parts", "sel", "pos", "count", "idx", "scattered", "w1_placed", "xT", "xTs", "h", "hs",
                                     "y", "ys", "final", "stored"))
        hT5_ps = [PS[:, 2 * n:2 * n + 2, :].rearrange("p a (f n) -> p (a f) n", f=4) for n in range(2)]
        xT5_ps = PS[:, 6, 0:KC * P].rearrange("p (k n) -> p k n", k=KC)
        y5_ps = PS[:, 7, 0:D]
        s_zero, s_fill = sem("zeros_made"), sem("dram_cleared")
        NFILL = -(-SLOTS0 // (4 * P)) + -(-SLOTS1 // (4 * P)) + 1
        FIRST = 1
        block = ctx.enter_context(nc.Block())

        zT_ps = PS[:, 0:2, :]
        sc_ps = PS[:, 2, :].rearrange("p (t k) -> p t k", t=CT)
        pT_ps = PS[0:LK, 3, :]
        o_ps = PS[:, 0:2, :].rearrange("p a (t d) -> p (a t) d", t=2)
        uT_ps = PS[:, 6:8, :]
        qk_ps = PS[:, 4:8, :].rearrange("p (a r) n -> p a r n", a=2)
        v_ps = PS[:, 4:6, :].rearrange("p a (t d) -> p (a t) d", t=2)

        @block.sync
        def _(sp):
            for primed in (m5_out[0], m5_out[1]):
                sp.sem_inc(primed, FIRST)
            x_rows = x_in.rearrange("b (t p) d -> p (b t) d", p=P)
            sp.dma_start(X[:, 0:CT], x_rows[:, 0:CT]).then_inc(ld_x, 16)
            sp.dma_start(CF[:], const_f_in).then_inc(ld_c, 16)
            sp.dma_start(CB[:], const_b_in).then_inc(ld_c, 16)
            for a, b in ((ctxT, ctxT_in), (wk0, wk0_in), (bk0, bk0_in), (bq0, bq0_in), (wq0T, wq0T_in),
                         (wv0, wv0_in), (bv0, bv0_in.partition_broadcast(P))):
                sp.dma_start(a, b).then_inc(ld_w, 16)
            for a, b in ((wqk, wqk_in), (wv, wv_in), (g1c, g1_in)):
                sp.dma_start(a, b).then_inc(ld_wp, 16)
            sp.dma_start(X[:, CT:], x_rows[:, CT:]).then_inc(ld_xr, 16)
            sp.dma_start(rope, rope_in).then_inc(ld_tab, 16)

            def clear():
                sp.wait_ge(s_zero, 1)
                for dram, n in ((xe_dram, SLOTS0), (xs_dram, SLOTS1)):
                    for r0 in range(0, n, 4 * P):
                        m = min(4, (n - r0) // P)
                        sp.dma_start(dram[r0:r0 + m * P].rearrange("(a p) d -> p a d", p=P),
                                     ZERO[:, 0:m * D].rearrange("p (a d) -> p a d", a=m)).then_inc(s_fill, 16)
                sp.dma_start(ye_dram[SLOTS0:SLOTS0 + 1], ZERO[0:1, 0:D]).then_inc(s_fill, 16)

            def send_parts(c):
                b, cc = c // CPB, c % CPB
                for n, ready in enumerate((s_hi, s_mid, s_lo)):
                    sp.wait_ge(ready, c + 1)
                    for a in range(2):
                        for r in range(2):
                            at = n if a else PARTS - 1 - n
                            sp.dma_start(qk_dram[a, b * NG:(b + 1) * NG, at, r, :, cc * CW:(cc + 1) * CW],
                                         PARTB[:, n, a, r, :]).then_inc(s_qkst, 16)

            def load_qk(s, n):
                row = 0
                for run in RUNS:
                    for a, buf, p0 in ((0, QT, PARTS - run), (1, KT, 0)):
                        src = qk_dram[a].rearrange("s p r (i h) t -> s p (r i) (h t)", h=GH)
                        sp.dma_start(buf[row:row + run * HD, n].rearrange("p h t -> p (h t)"),
                                     src[s, p0:p0 + run].rearrange("p r c -> (p r) c")).then_inc(ld_qk[n], 16)
                    row += run * HD

            def load_max_rows(s, n):
                sp.wait_ge(s_mt, s + 1)
                sp.dma_start(QT[QROWS:AROWS, n].rearrange("p h (i t) -> p (h i) t", t=P), MT[0:PARTS * 32, :]).then_inc(s_mrow, 16)

            send_parts(0)
            clear()
            for c in range(1, CPB):
                send_parts(c)
            sp.wait_ge(s_qkst, 16 * 12 * CPB)
            load_qk(0, 0)
            sp.dma_start(KT[QROWS:AROWS].rearrange("p n h (a t) -> p (n h a) t", t=P),
                         const_b_in[0:PARTS, 3 * P:4 * P].unsqueeze(1).to_broadcast([PARTS, BUFS * GH * S // P, P])).then_inc(ld_tab, 16)
            for n in range(1, BUFS):
                load_qk(n, n)
            for c in range(CPB, NCH):
                send_parts(c)
            load_max_rows(0, 0)
            sp.wait_ge(s_qkst, 16 * 12 * NCH)
            for s in range(NS):
                if s + 1 < NS:
                    load_max_rows(s + 1, (s + 1) % BUFS)
                if s + BUFS < NS:
                    sp.wait_ge(s_sT, 2 * NSTG * (s + 1))
                    load_qk(s + BUFS, s % BUFS)
            for a, b in ((WO, wo_in), (G2, g2_in.partition_broadcast(P)), (WR, wr_in)):
                sp.dma_start(a, b).then_inc(ld_3, 16)

            def load_w1e(e, n):
                sp.dma_start(W1E[:, n], w1e_in.rearrange("e (k p) f -> e p k f", p=P)[ds(e, 1)].squeeze(0)).then_inc(ld_w1e[n], 16)

            def load_w2e(e, n):
                sp.dma_start(W2E[:, n], w2e_in.rearrange("e (k p) d -> e p k d", p=P)[ds(e, 1)].squeeze(0)).then_inc(ld_w2e[n], 16)

            def load_rows(e, n):
                sp.dma_start(XEB[:, n, 0:2], xe_dram[ds(e * CAP, 2 * P)].rearrange("(a p) d -> p a d", p=P)).then_inc(ld_xe[n], 16)
                sp.dma_start(XEB[0:TAIL, n, 2], xe_dram[ds(e * CAP + 2 * P, TAIL)]).then_inc(ld_xe[n], 16)

            sp.wait_ge(s_yn, 2 * NS)
            sp.wait_ge(ld_3, 16 * 3)
            for a, b in ((BO, bo1_in.partition_broadcast(P)), (WG, wg_in), (BG, bg_in.unsqueeze(0)), (BQ1, bq1_in), (BK1, bk1_in),
                         (CT1, ctxT_in), (WK1, wk1_in), (WV1, wv1_in), (BV1, bv1_in.partition_broadcast(P))):
                sp.dma_start(a, b).then_inc(ld_3, 16)
            for n in range(2):
                load_w1e(n, n)
                load_w2e(n, n)
            for e in range(E):
                sp.dma_start(REG[:, e * KC * F1:(e + 1) * KC * F1].rearrange("p (k f) -> p k f", k=KC),
                             w1_in.rearrange("e (k p) f -> e p k f", p=P)[e]).then_inc(ld_5, 16)
            sp.wait_ge(k4_vs, 2)
            for j, (h0, h1) in enumerate(HWIN):
                for h in range(h0, h1):
                    r0, r1 = max(LK * h, P * j), min(LK * (h + 1), P * (j + 1))
                    sp.dma_start(VBD[r0 - P * j:r1 - P * j, :, j, h - h0, :], V1[r0 - LK * h:r1 - LK * h, :, h, :]).then_inc(k4_vb, 16)
            sp.wait_ge(s_scat, 16 * 2 * NT)
            load_rows(0, 0)
            load_rows(1, 1)
            for e in range(E - 1):
                if e + 2 < E:
                    sp.wait_ge(me_xT, e + 1)
                    load_rows(e + 2, e % 2)
                    sp.wait_ge(me_h, e + 1)
                    load_w1e(e + 2, e % 2)
                if e:
                    sp.wait_ge(me_y, e)
                    load_w2e(e + 1, (e + 1) % 2)
            sp.wait_ge(p3_lg, NCH)
            sp.wait_ge(p3_lgs, NCH)
            sp.wait_ge(me_y, E)
            sp.wait_ge(me_out, 32 * E + FIRST)
            for a, b in ((WQ1, wq1_in), (WO1, wo1_in)):
                sp.dma_start(a, b).then_inc(ld_4, 16)
            sp.wait_ge(s_gath, 16 * 2 * CT * 2)
            for e in range(E // 2):
                at = (3 * E // 2 + e) * KC * F1
                sp.dma_start(REG[:, at:at + KC * F1].rearrange("p (k d) -> p k d", d=D),
                             w2_in.rearrange("e (k p) d -> e p k d", p=P)[e]).then_inc(ld_5, 16)
            sp.wait_ge(q4_gs, NCH)
            sp.wait_ge(q4_out, NCH)
            for e in range(EH):
                sp.dma_start(W2S[:, e], w2_in.rearrange("e (k p) d -> e p k d", p=P)[EH + e]).then_inc(ld_5, 16)
            sp.dma_start(BBF[:, 0:NB1 // P], b1_in.rearrange("e f -> (e f)").rearrange("(p n) -> p n", p=P)).then_inc(ld_b, 16)
            sp.dma_start(BBF[:, NB1 // P:], b2_in.rearrange("e f -> (e f)").rearrange("(p n) -> p n", p=P)).then_inc(ld_b, 16)
            sp.wait_ge(b5_p, 1)
            for n in range(PARTS):
                sp.dma_start(bp_dram[n, 0:NB1].rearrange("(p n) -> p n", p=P), BBP[:, n, 0:NB1 // P]).then_inc(ld_b2, 16)
                sp.dma_start(bp_dram[n, NB1:].rearrange("(p n) -> p n", p=P), BBP[:, n, NB1 // P:]).then_inc(ld_b2, 16)
            sp.wait_ge(ld_b2, 16 * 2 * PARTS)
            sp.dma_start(BPS, bp_dram).then_inc(ld_bp, 16)
            sp.wait_ge(s_scat5, 16 * NT)

            def load_tile(j, n):
                sp.dma_start(XS5[:, n], xs_dram[ds(j * P, P)]).then_inc(ld_xs[n], 16)

            def send_tile(j, n):
                sp.wait_ge(m5_ys, j + 1 + FIRST)
                sp.dma_start(ys_dram[ds(j * P, P)], YB5[:, n]).then_inc(m5_out[n], 16)

            load_tile(0, 0)
            load_tile(1, 1)
            with sp.Fori(0, (NT1 - 3) // 2) as it:
                for n in range(2):
                    j = 2 * it + n
                    sp.wait_ge(m5_xT, j + 1)
                    load_tile(j + 2, n)
                    send_tile(j, n)
            sp.wait_ge(m5_xT, NT1 - 2)
            load_tile(NT1 - 1, 0)
            for j in range(NT1 - 3, NT1):
                send_tile(j, j % 2)
            for c in range(NCH):
                sp.wait_ge(s_fin, c + 1)
                sp.dma_start(out.rearrange("b (t p) d -> p (b t) d", p=P)[:, c * CT:(c + 1) * CT], X[:, c * CT:(c + 1) * CT, :]).then_inc(s_out, 16)
            sp.wait_ge(s_out, 16 * NCH)

        @block.gpsimd
        def _(pool):
            chain = Chain(pool, s_chp)
            nc.gpsimd.memset(ZERO, 0.0).then_inc(s_zero, 1)
            pool.wait_ge(ld_c, 32)
            def rstd(c):
                pool.wait_ge(s_var, c + 1)
                nc.gpsimd.tensor_tensor(RSTD, VE, neg_half[:, 0:CT], ALU.pow).then_inc(s_rstd, 1)

            def rstd2(c):
                pool.wait_ge(s_var2, c + 1)
                nc.gpsimd.tensor_tensor(R1S1, VE12, neg_half[:, 0:2 * CT], ALU.pow).then_inc(s_rstd2, 1)

            rotf = ROT.rearrange("p a b n -> p (a b n)")
            part = PARTB.rearrange("p n a b m -> p n (a b m)")
            rstd(0)
            rstd(1)
            for c in range(NCH + 1):
                if c:
                    pool.wait_ge(s_rt, c)
                    if c > 1:
                        pool.wait_ge(s_lo, c - 1)
                    chain(nc.gpsimd.tensor_tensor(ROT[:, :, 0, :], RT[:, 0], RT[:, 1], ALU.subtract))
                if c < NCH:
                    rstd2(c)
                if c:
                    nc.gpsimd.tensor_tensor(ROT[:, :, 1, :], RT[:, 2], RT[:, 3], ALU.add).then_inc(s_rot, 1)
                    pool.wait_ge(s_hi, c)
                    nc.gpsimd.tensor_tensor(rotf, rotf, part[:, 0], ALU.subtract).then_inc(s_res, 1)
                if c + 2 < NCH:
                    rstd(c + 2)
                if c:
                    pool.wait_ge(s_mid, c)
                    nc.gpsimd.tensor_tensor(part[:, 2], rotf, part[:, 1], ALU.subtract).then_inc(s_lo, 1)
            pool.wait_ge(s_vs, NCH)
            pool.wait_ge(s_v, NCH)
            pool.wait_ge(s_lo, NCH)
            pool.wait_ge(s_qkst, 16 * 12 * NCH)
            chain(nc.gpsimd.memset(VS, 0.0))
            chain(nc.gpsimd.memset(VS[:, :, :, :, HD:HD + 1], 1.0))

            def stage_v(s, n):
                nc.gpsimd.tensor_copy(VS[:, n, :, :, 0:HD],
                                      VB[:, s].rearrange("p t (h d) -> p t h d", h=GH)).then_inc(s_vst, 1)

            for s in range(NS):
                if s >= BUFS:
                    pool.wait_ge(s_y, 2 * (s - BUFS + 1))
                stage_v(s, s % BUFS)
            for c in range(NCH):
                pool.wait_ge(p3_ms, c + 1)
                if c > 1:
                    pool.wait_ge(p3_xc, c - 1)
                nc.gpsimd.tensor_tensor(R3[c % 2], VE, neg_half[:, 0:CT], ALU.pow).then_inc(p3_r, 1)
            pool.wait_ge(s_fill, 16 * NFILL)
            pool.wait_ge(p3_xc, NCH)
            pool.wait_ge(rt_idx, 1)
            for t in range(NT):
                for idx in (IDX1, IDX2):
                    nc.gpsimd.indirect_dma_start(out=xe_dram, out_offset=bass.IndirectOffsetOnAxis(ap=idx[:, t:t + 1], axis=0),
                                                 in_=XF[:, t, :], in_offset=None, bounds_check=SLOTS0 - 1,
                                                 oob_is_err=False).then_inc(s_scat, 16)
            pool.wait_ge(me_out, 32 * E + FIRST)
            pool.wait_ge(s_fill, 16 * NFILL)

            def gather(c):
                for t in range(CT):
                    for a, idx in enumerate((IDX1, IDX2)):
                        nc.gpsimd.indirect_dma_start(out=GB[:, t, a, :], out_offset=None, in_=ye_dram,
                                                     in_offset=bass.IndirectOffsetOnAxis(ap=idx[:, c * CT + t:c * CT + t + 1], axis=0),
                                                     bounds_check=SLOTS0, oob_is_err=True).then_inc(s_gath, 16)

            def enter4(c):
                pool.wait_ge(q4_var, c + 1)
                nc.gpsimd.tensor_tensor(RSTD, VE, neg_half[:, 0:CT], ALU.pow).then_inc(q4_r, 1)
                if c + 1 < NCH:
                    pool.wait_ge(q4_x, c + 1)
                    gather(c + 1)
                pool.wait_ge(ld_3, 16 * 12)
                pool.wait_ge(q4_z, c + 1)
                xc = X[:, c * CT:(c + 1) * CT, :]
                nc.gpsimd.tensor_tensor(xc, xc, BO.unsqueeze(1).to_broadcast([P, CT, D]), ALU.add).then_inc(q4_bo, 1)

            def leave4(c):
                pool.wait_ge(q4_var3, c + 1)
                nc.gpsimd.tensor_tensor(RSTD, VE, neg_half[:, 0:CT], ALU.pow).then_inc(q4_r3, 1)

            gather(0)
            enter4(0)
            for c in range(NCH):
                if c + 1 < NCH:
                    enter4(c + 1)
                if c:
                    leave4(c - 1)
            leave4(NCH - 1)
            pool.wait_ge(q4_z3, NCH)
            pool.wait_ge(r5_idx, 1)
            for t in range(NT):
                nc.gpsimd.indirect_dma_start(out=xs_dram, out_offset=bass.IndirectOffsetOnAxis(ap=IDX5[:, t:t + 1], axis=0),
                                             in_=H[:, t, :], in_offset=None, bounds_check=SLOTS1 - 1,
                                             oob_is_err=True).then_inc(s_scat5, 16)
            pool.wait_ge(s_scat5, 16 * NT)
            pool.wait_ge(m5_out[0], 16 * ((NT1 + 1) // 2) + FIRST)
            pool.wait_ge(m5_out[1], 16 * (NT1 // 2) + FIRST)
            for t in range(NT):
                nc.gpsimd.indirect_dma_start(out=H[:, t, :], out_offset=None, in_=ys_dram,
                                             in_offset=bass.IndirectOffsetOnAxis(ap=IDX5[:, t:t + 1], axis=0),
                                             bounds_check=SLOTS1 - 1, oob_is_err=True).then_inc(s_gat5[t // CT], 16)

        @block.scalar
        def _(act):
            for primed in (me_out, me_ys):
                act.sem_inc(primed, FIRST)
            for m in range(KC):
                act.wait_ge(pre_k, m + 1)
                nc.scalar.activation(KT0[:, m, :], PS[:, m, 0:B * LK], ACT.Identity, bias=bk0[:, m:m + 1]).then_inc(pre_ks, 1)
            act.wait_ge(pre_a, 1)
            nc.scalar.activation(A0, PS[:, 2:2 + KC, 0:B * LK], ACT.Copy)
            nc.scalar.activation(CB0, PS[0:1, 4, 0:B * LK], ACT.Copy).then_inc(pre_as, 1)
            def evac_zT(c):
                act.wait_ge(s_zT, c + 1)
                nc.scalar.activation(ZT, zT_ps, ACT.Copy).then_inc(s_zTs, 1)

            def weights(c):
                act.wait_ge(s_nb, c + 1)
                for t in range(CT):
                    last = nc.scalar.activation(P0[:, t, 0:LK], sc_ps[:, t, 0:LK], ACT.Exp, bias=NB[:, t:t + 1],
                                                scale=1.0 / 16.0, accum_out=RSUM[:, t:t + 1])
                last.then_inc(s_p, 1)

            def evac_pT(c):
                act.wait_ge(s_pT, c + 1)
                nc.scalar.activation(PT0, pT_ps, ACT.Copy).then_inc(s_pTs, 1)

            def evac_v(c):
                act.wait_ge(s_v, c + 1)
                for t in range(CT):
                    last = nc.scalar.activation(
                        VB.rearrange("p (b g) t n -> p b t g n", b=B)[:, c // CPB, c % CPB * CT + t],
                        v_ps[:, t, :].rearrange("p (g n) -> p g n", g=NG), ACT.Copy)
                last.then_inc(s_vs, 1)

            rotf = ROT.rearrange("p a b n -> p (a b n)")
            part = PARTB.rearrange("p n a b m -> p n (a b m)")

            def hi(c):
                act.wait_ge(s_rot, c + 1)
                if c:
                    act.wait_ge(s_qkst, 16 * 12 * c)
                nc.scalar.activation(part[:, 0], rotf, ACT.Copy).then_inc(s_hi, 1)

            def mid(c):
                act.wait_ge(s_res, c + 1)
                nc.scalar.activation(part[:, 1], rotf, ACT.Copy).then_inc(s_mid, 1)

            evac_zT(0)
            weights(0)
            evac_pT(0)
            for c in range(NCH):
                if c:
                    evac_v(c - 1)
                if c + 1 < NCH:
                    evac_zT(c + 1)
                act.wait_ge(s_uT, c + 1)
                nc.scalar.activation(UT, uT_ps, ACT.Copy).then_inc(s_uTs, 1)
                if c:
                    hi(c - 1)
                if c + 1 < NCH:
                    weights(c + 1)
                    evac_pT(c + 1)
                if c:
                    mid(c - 1)
            evac_v(NCH - 1)
            hi(NCH - 1)
            mid(NCH - 1)
            def exps(s, n):
                for k, (c, j) in enumerate(STAGES):
                    q0 = q0_of(c, j)
                    act.wait_ge(s_pvd, NSTG * s + k + FIRST)
                    for pair in range(2):
                        act.wait_ge(s_sT, 2 * NSTG * s + 2 * k + pair + 1)
                        nc.scalar.activation(PB[:, k % 2, 2 * pair:2 * pair + 2, q0:CW], s_ps[pair][:, :, q0:CW],
                                             ACT.Exp, scale=0.25).then_inc(s_sfree, 1)

            act.wait_ge(s_v, NCH)
            act.wait_ge(s_lo, NCH)
            act.wait_ge(s_qkst, 16 * 12 * NCH)
            act.sem_inc(s_sfree, 2)
            with act.Fori(0, NS // 2) as it:
                for n in range(2):
                    exps(2 * it + n, n)
            for c in range(NCH + 1):
                if c < NCH:
                    act.wait_ge(p3_yT, c + 1)
                    nc.scalar.activation(YCT, yT3_ps, ACT.Copy).then_inc(p3_yTs, 1)
                if c:
                    act.wait_ge(p3_xT, c)
                    nc.scalar.activation(XCT, xT3_ps, ACT.Copy).then_inc(p3_xTs, 1)
            act.wait_ge(rt_sub, 1)
            nc.scalar.activation(EX, TE1, ACT.Exp).then_inc(rt_exp, 1)

            def send_rows(e, n):
                act.dma_start(ye_dram[ds(e * CAP, 2 * P)].rearrange("(a p) d -> p a d", p=P), YEB[:, n, 0:2]).then_inc(me_out, 16)
                act.dma_start(ye_dram[ds(e * CAP + 2 * P, TAIL)], YEB[0:TAIL, n, 2]).then_inc(me_out, 16)

            def evac_xT(e, n):
                act.wait_ge(me_xT, e + 1)
                nc.scalar.activation(XET[:, n], xeT_ps, ACT.Copy).then_inc(me_xTs, 1)

            def expert_rows(e, n):
                act.wait_ge(me_y, e + 1)
                act.wait_ge(me_out, 32 * e + FIRST)
                nc.scalar.activation(YEB[:, n, 0:2], ye_ps[:, 0:2], ACT.Copy)
                nc.scalar.activation(YEB[0:TAIL, n, 2], ye_ps[0:TAIL, 2], ACT.Copy).then_inc(me_ys, 1)
                act.wait_ge(me_ys, e + 1 + FIRST)
                send_rows(e, n)

            act.wait_ge(ld_3, 16 * 12)
            for m in range(KC):
                act.wait_ge(k4_k, m + 1)
                nc.scalar.activation(KT1[:, m, :], PS[:, 6 + m, 0:B * LK], ACT.Identity, bias=BK1[:, m:m + 1]).then_inc(k4_ks, 1)
            evac_xT(0, 0)
            evac_xT(1, 1)
            with act.Fori(0, E // 2 - 1) as it:
                for n in range(2):
                    evac_xT(2 * it + n + 2, n)
                    expert_rows(2 * it + n, n)
            expert_rows(E - 2, 0)
            expert_rows(E - 1, 1)
            act.wait_ge(me_ys, E + FIRST)

            def evac_T4(ready, done, c):
                act.wait_ge(ready, c + 1)
                nc.scalar.activation(Z4T, zT4_ps, ACT.Copy).then_inc(done, 1)

            def evac_q(c):
                act.wait_ge(q4_q, c + 1)
                for m in range(KC):
                    last = nc.scalar.activation(Q4T[:, c % 2, m, :], q4_ps[:, m, :], ACT.Identity, bias=BQ1[:, m:m + 1])
                last.then_inc(q4_qs, 1)

            def exp4(c, t):
                act.wait_ge(q4_sub, c * CT + t + 1)
                nc.scalar.activation(SS[:, t % 2], SS[:, t % 2], ACT.Exp, scale=0.25).then_inc(q4_p, 1)

            evac_T4(q4_zT, q4_zTs, 0)
            evac_q(0)
            exp4(0, 0)
            for c in range(NCH):
                for t in range(CT):
                    for q, blocks in enumerate(UBLK):
                        unit = (c * CT + t) * NQ + q
                        act.wait_ge(q4_pT, unit + 1)
                        nc.scalar.activation(PT4[:, blocks[0]:blocks[-1] + 1, :], pT4_ps[unit % 2][:, 0:len(blocks), :],
                                             ACT.Copy).then_inc(q4_pTs, 1)
                        if (t, q) == (0, 1) and c:
                            evac_T4(q4_oT, q4_oTs, c - 1)
                        if (t, q) == (2, 0) and c + 1 < NCH:
                            evac_T4(q4_zT, q4_zTs, c + 1)
                        if (t, q) == (2, 1) and c + 1 < NCH:
                            evac_q(c + 1)
                        if (t, q) == (3, 1) and c:
                            evac_T4(q4_z3T, q4_z3Ts, c - 1)
                    if c * CT + t + 1 < NT:
                        exp4(c + (t + 1) // CT, (t + 1) % CT)
            evac_T4(q4_oT, q4_oTs, NCH - 1)
            evac_T4(q4_z3T, q4_z3Ts, NCH - 1)
            def evac_xT5(j, n):
                act.wait_ge(m5_xT, j + 1)
                nc.scalar.activation(XT5[:, n], xT5_ps, ACT.Copy).then_inc(m5_xTs, 1)

            def place_w1(j, n):
                e = act.value_load(TEI[0:1, ds(j, 1)], min_val=0, max_val=E - 1)
                nc.scalar.activation(W1C[n].rearrange("p k f -> p (k f)").unsqueeze(1), W1S[:, ds(e, 1)].rearrange("p e k f -> p e (k f)"),
                                     ACT.Copy).then_inc(m5_w, 1)

            def next_w1(j, n):
                act.wait_ge(m5_h, j + 1)
                act.sem_inc(s_spare, 1)
                place_w1(j + 2, n)

            act.wait_ge(r5_idx, 2)
            act.wait_ge(ld_5, 16 * 2 * E)
            act.wait_ge(s_scat5, 16 * NT)
            place_w1(0, 0)
            evac_xT5(0, 0)
            place_w1(1, 1)
            evac_xT5(1, 1)
            with act.Fori(0, (NT1 - 3) // 2) as it:
                for n in range(2):
                    next_w1(2 * it + n, n)
                    evac_xT5(2 * it + n + 2, n)
            next_w1(NT1 - 3, 0)
            evac_xT5(NT1 - 1, 0)

        @block.vector
        def _(dve):
            for primed in (s_yev, m5_ys):
                dve.sem_inc(primed, FIRST)
            chain = Chain(dve, s_chv)

            def stats1(c):
                dve.wait_ge(*((ld_x, 16) if c == 0 else (ld_xr, 16)))
                for t in range(CT):
                    last = nc.vector.bn_stats(ST[:, t, :], X[:, c * CT + t, :])
                chain(last)
                for t in range(CT):
                    last = nc.vector.bn_aggr(MV[:, t, :], ST[:, t, :])
                chain(last)
                nc.vector.tensor_scalar(VE, MV[:, :, 1], LN_EPS, None, ALU.add).then_inc(s_var, 1)

            def normed1(c):
                dve.wait_ge(s_rstd, c + 1)
                if c:
                    dve.wait_ge(s_zT, c)
                for t in range(CT):
                    last = nc.vector.tensor_scalar(Z[:, t, :], X[:, c * CT + t, :], MV[:, t, 0:1], RSTD[:, t:t + 1],
                                                   ALU.subtract, ALU.mult)
                last.then_inc(s_z, 1)

            def maxima(c):
                dve.wait_ge(s_sc, c + 1)
                chain(nc.vector.reduce_max(MX, sc_ps[:, :, 0:LK], AX.X))
                nc.vector.tensor_scalar(NB, MX, -1.0 / 16.0, None, ALU.mult).then_inc(s_nb, 1)

            def rope_part(c, a):
                dve.wait_ge(ld_tab, 16)
                dve.wait_ge((s_q, s_k)[a], c + 1)
                if c:
                    dve.wait_ge(s_rot, c)
                cc = c % CPB
                for n, (r, t) in enumerate(((0, 0), (1, 1), (0, 1), (1, 0))):
                    last = nc.vector.tensor_tensor(RT[:, n, a], qk_ps[:, a, r, :], rope[:, t, cc * CW:(cc + 1) * CW], ALU.mult)
                last.then_inc((s_rq, s_rt)[a], 1)

            def add_heads(c):
                dve.wait_ge(s_p, c + 1)
                chain(nc.vector.reciprocal(RRS, RSUM))
                dve.wait_ge(s_o, c + 1)
                for t in range(CT):
                    xt = X[:, c * CT + t, :]
                    last = nc.vector.scalar_tensor_tensor(out=xt, in0=o_ps[:, t, :], scalar=RRS[:, t:t + 1], in1=xt,
                                                          op0=ALU.mult, op1=ALU.add)
                chain(last)
                for t in range(CT):
                    last = nc.vector.bn_stats(ST[:, t, :], X[:, c * CT + t, :])
                chain(last)
                for t in range(CT):
                    last = nc.vector.bn_aggr(MV[:, t, :], ST[:, t, :])
                chain(last)
                nc.vector.tensor_scalar(VE1, MV[:, :, 1], LN_EPS, None, ALU.add)
                nc.vector.tensor_scalar(VE2, MV[:, :, 1], 1.0 + RMS_EPS, LN_EPS * RMS_EPS, ALU.mult, ALU.add).then_inc(s_var2, 1)

            def normed2(c):
                dve.wait_ge(s_rstd2, c + 1)
                if c:
                    dve.wait_ge(s_uT, c)
                for t in range(CT):
                    last = nc.vector.tensor_scalar(U[:, t, :], X[:, c * CT + t, :], MV[:, t, 0:1], S1[:, t:t + 1],
                                                   ALU.subtract, ALU.mult)
                last.then_inc(s_u, 1)
                for t in range(CT):
                    last = nc.vector.tensor_scalar(H[:, c * CT + t, :], X[:, c * CT + t, :], MV[:, t, 0:1], R1[:, t:t + 1],
                                                   ALU.subtract, ALU.mult)
                chain(last)

            stats1(0)
            normed1(0)
            dve.wait_ge(ld_wp, 16 * 3)
            for k in range(KC):
                nc.vector.tensor_scalar(wqk[:, k], wqk[:, k], g1c[:, k:k + 1], None, ALU.mult)
                last = nc.vector.tensor_scalar(wv[:, k], wv[:, k], g1c[:, k:k + 1], None, ALU.mult)
            last.then_inc(pre_w, 1)
            dve.wait_ge(pre_a, 1)
            dve.wait_ge(ld_w, 16 * 7)
            nc.vector.tensor_tensor(V0, PS[0:LK, 5:7, 0:D], bv0[0:LK, :].unsqueeze(1).to_broadcast([LK, B, D]), ALU.add).then_inc(pre_w, 1)
            maxima(0)
            stats1(1)
            normed1(1)
            for c in range(NCH):
                add_heads(c)
                normed2(c)
                if c + 1 < NCH:
                    maxima(c + 1)
                if c + 2 < NCH:
                    stats1(c + 2)
                rope_part(c, 0)
                if c + 2 < NCH:
                    normed1(c + 2)
                rope_part(c, 1)
            def reduce_unit(s, u):
                i, h0, nh, k0, w, masked = UNITS[u]
                dve.wait_ge(s_mx, NU * s + u + 1)
                src = m_ps[u % 2][:, 0:nh * w].rearrange("p (h w) -> p h w", h=nh)
                last = nc.vector.reduce_max(MXP[:, h0:h0 + nh, i, int(not masked)], src, AX.X)
                last.then_inc(s_mfree, 1)

            def max_parts(s):
                dve.wait_ge(s_mfree, NU * (s + 1) + 2)
                chain(nc.vector.reduce_max(NR, MXP, AX.X))
                chain(nc.vector.tensor_scalar(NM, NR, -1.0, None, ALU.mult))
                chain(nc.vector.tensor_copy(MP[:, 0], NM))
                chain(nc.vector.tensor_tensor(NR, NM, MP[:, 0], ALU.subtract))
                chain(nc.vector.tensor_copy(MP[:, 1], NR))
                nc.vector.tensor_tensor(MP[:, 2], NR, MP[:, 1], ALU.subtract).then_inc(s_mp, 1)

            def max_rows(s):
                dve.wait_ge(s_mpt, s + 1)
                dve.wait_ge(s_mrow, 16 * s)
                nc.vector.tensor_copy(MT[0:96], t_ps.bitcast(bf16)[0:96, 0:P]).then_inc(s_mt, 1)

            def evac_y(s, c):
                dve.wait_ge(s_y, 2 * s + c + 1)
                nc.vector.tensor_copy(YT[:, c], y_ps).then_inc(s_yev, 1)

            def norm_y(s, c, b_, g):
                dve.wait_ge(s_yt, 2 * s + c + 1)
                back = t_ps.rearrange("p (t h d) -> p t h d", t=CT, h=GH)
                chain(nc.vector.reciprocal(RY, back[:, :, :, HD]))
                dst = XF.rearrange("p t (s x) -> p t s x", s=NG)
                for t in range(CT):
                    last = nc.vector.tensor_tensor(
                        dst[:, ds(b_ * NK + c * CT + t, 1), ds(g, 1), :].rearrange("p a b (h d) -> p (a b) h d", h=GH),
                        back[:, t:t + 1, :, 0:HD].rearrange("p a h d -> p a h d"),
                        RY[:, t:t + 1, :].unsqueeze(3).to_broadcast([P, 1, GH, HD]), ALU.mult)
                last.then_inc(s_yn, 1)

            chain(nc.vector.memset(MXP, -3.0e38))
            dve.sem_inc(s_mfree, 2)
            for u in range(NU):
                reduce_unit(0, u)
            max_parts(0)
            max_rows(0)
            for u in range(LEAD):
                reduce_unit(1, u)
            dve.wait_ge(s_lo, NCH)
            dve.wait_ge(s_qkst, 16 * 12 * NCH)
            dve.wait_ge(s_fill, 16 * NFILL)

            def dve_step(s, b_, g, nxt, lead):
                for k in range(NSTG):
                    if k == CT + 1:
                        evac_y(s, 0)
                    units(k, nxt, lead, lambda ahead, u: reduce_unit(s + ahead, u))
                    if k == 7:
                        norm_y(s, 0, b_, g)
                    if nxt and k == MSTG - 1:
                        max_parts(s + 1)
                        max_rows(s + 1)
                if lead:
                    for u in range(LEAD - NEND, LEAD - NEND // 2):
                        reduce_unit(s + 2, u)
                evac_y(s, 1)
                if lead:
                    for u in range(LEAD - NEND // 2, LEAD):
                        reduce_unit(s + 2, u)
                norm_y(s, 1, b_, g)

            STEP = 2 + 5
            with dve.Fori(0, B - 1) as b_:
                with dve.Fori(0, NG) as g:
                    chain.enter(b_ * NG + g, STEP)
                    dve_step(b_ * NG + g, b_, g, True, True)
            chain.leave((B - 1) * NG)
            with dve.Fori(0, NG - 2) as g:
                chain.enter(g, STEP)
                dve_step((B - 1) * NG + g, B - 1, g, True, True)
            chain.leave(NG - 2)
            dve_step(NS - 2, B - 1, NG - 2, True, False)
            dve_step(NS - 1, B - 1, NG - 1, False, False)
            dve.wait_ge(ld_3, 48)
            def add_projection(c):
                hc = H[:, c * CT:(c + 1) * CT, :]
                dve.wait_ge(p3_o, c + 1)
                nc.vector.tensor_tensor(hc, o3_ps, hc, ALU.add).then_inc(p3_h, 1)
                dve.wait_ge(p3_h, c + 1)
                for t in range(CT):
                    last = nc.vector.bn_stats(ST[:, t, :], H[:, c * CT + t, :])
                chain(last)
                for t in range(CT):
                    last = nc.vector.bn_aggr(MV[:, t, :], ST[:, t, :])
                chain(last)
                chain(nc.vector.tensor_tensor(TV, MV[:, :, 0], MV[:, :, 0], ALU.mult))
                if c:
                    dve.wait_ge(p3_r, c)
                nc.vector.scalar_tensor_tensor(out=VE, in0=TV, scalar=RMS_EPS, in1=MV[:, :, 1], op0=ALU.add, op1=ALU.add).then_inc(p3_ms, 1)

            def expert_rows(c):
                dve.wait_ge(p3_r, c + 1)
                dve.wait_ge(p3_yT, c + 1)
                for t in range(CT):
                    last = nc.vector.scalar_tensor_tensor(out=XF[:, c * CT + t, :], in0=H[:, c * CT + t, :], scalar=R3[c % 2][:, t:t + 1],
                                                          in1=G2, op0=ALU.mult, op1=ALU.mult)
                last.then_inc(p3_xc, 1)

            def keep_logits(c):
                dve.wait_ge(p3_lg, c + 1)
                nc.vector.tensor_copy(LG[:, c * CT:(c + 1) * CT, :], lg_ps).then_inc(p3_lgs, 1)

            for c in range(NCH + 2):
                if c < NCH:
                    add_projection(c)
                if 0 < c <= NCH:
                    expert_rows(c - 1)
                if c > 1:
                    keep_logits(c - 2)

            def over_e(a):
                return a.unsqueeze(2).to_broadcast([P, NT, E])

            def over_t(a):
                return a.unsqueeze(1).to_broadcast([P, NT, E])

            def first_max(src, top, sel, tmp):
                chain(nc.vector.reduce_max(top, src, AX.X))
                chain(nc.vector.tensor_tensor(tmp, src, over_e(top), ALU.is_equal))
                chain(nc.vector.tensor_tensor(tmp, tmp, over_t(w8), ALU.mult))
                chain(nc.vector.reduce_max(VM, tmp, AX.X))
                chain(nc.vector.tensor_tensor(sel, tmp, over_e(VM), ALU.is_equal))

            dve.wait_ge(p3_lgs, NCH)
            chain(nc.vector.reduce_max(M1, LG[:], AX.X))
            nc.vector.tensor_tensor(TE1, LG[:], over_e(M1), ALU.subtract).then_inc(rt_sub, 1)
            dve.wait_ge(rt_exp, 1)
            chain(nc.vector.reduce_sum(SU, EX, AX.X))
            chain(nc.vector.reciprocal(RSU, SU))
            chain(nc.vector.tensor_tensor(PR, EX, over_e(RSU), ALU.mult))
            first_max(PR, M1, SEL1, TE1)
            chain(nc.vector.scalar_tensor_tensor(out=TE2, in0=SEL1, scalar=-4.0, in1=PR, op0=ALU.mult, op1=ALU.add))
            first_max(TE2, M2, SEL2, TE1)
            chain(nc.vector.tensor_tensor(TE1, SEL1, SEL2, ALU.add))
            chain(nc.vector.tensor_tensor(G, TE1, PR, ALU.mult))
            chain(nc.vector.memset(CUR, 0.0))
            chain(nc.vector.tensor_copy(STEP_BITS, top_bits))
            with dve.Fori(0, BITS // BSTEP) as i:
                chain.enter(i, 5)
                chain(nc.vector.tensor_tensor(CAND.bitcast(i32), CUR.bitcast(i32).unsqueeze(1).to_broadcast([P, NCAND, E]),
                                              STEP_BITS.bitcast(i32).unsqueeze(2).to_broadcast([P, NCAND, E]), ALU.bitwise_or))
                nc.vector.tensor_tensor(REACH, G.unsqueeze(2).to_broadcast([P, NT, NCAND, E]),
                                        CAND.unsqueeze(1).to_broadcast([P, NT, NCAND, E]), ALU.is_ge).then_inc(rt_ge, 1)
                chain(nc.vector.tensor_scalar(STEP_BITS.bitcast(i32), STEP_BITS.bitcast(i32), BSTEP, None, ALU.logical_shift_right))
                dve.wait_ge(rt_cnt, i + 1)
                chain(nc.vector.scalar_tensor_tensor(out=TK, in0=ncand_ps, scalar=CAP - 0.5, in1=CAND, op0=ALU.is_ge, op1=ALU.mult))
                chain(nc.vector.reduce_max(TM, TK.rearrange("p j e -> p e j"), AX.X))
                chain(nc.vector.tensor_tensor(CUR, CUR, TM, ALU.max))
            chain.leave(BITS // BSTEP)
            chain(nc.vector.tensor_tensor(TE1, G, over_t(CUR), ALU.is_equal))
            chain(nc.vector.scalar_tensor_tensor(out=EQb, in0=G, scalar=0.0, in1=TE1, op0=ALU.is_gt, op1=ALU.mult))
            nc.vector.tensor_tensor(GEb, G, over_t(CUR), ALU.is_gt).then_inc(rt_ge, 1)
            dve.wait_ge(rt_cnt, BITS // BSTEP + 1)
            chain(nc.vector.reduce_sum(CNT, cnt_ps.rearrange("p t e -> p e t"), AX.X))
            chain(nc.vector.tensor_scalar(NGT, CNT, -1.0, float(CAP), ALU.mult, ALU.add))
            chain(nc.vector.tensor_tensor(TE1, pfx_ps, over_t(NGT), ALU.is_lt))
            chain(nc.vector.tensor_tensor(TE2, TE1, EQb, ALU.mult))
            chain(nc.vector.tensor_tensor(KEEPb, TE2, GEb, ALU.add))
            dve.sem_inc(rt_keep, 1)
            dve.wait_ge(rt_pos, 1)
            chain(nc.vector.tensor_tensor(TE1, pos_ps, over_t(base0), ALU.add))
            chain(nc.vector.tensor_tensor(TE1, TE1, KEEPb, ALU.mult))
            for sel, top, gate, idx in ((SEL1, M1, GATE1, IDX1), (SEL2, M2, GATE2, IDX2)):
                chain(nc.vector.tensor_tensor(TE2, TE1, sel, ALU.mult))
                chain(nc.vector.reduce_sum(IDF, TE2, AX.X))
                chain(nc.vector.tensor_scalar(idx, IDF, float(SLOTS0), None, ALU.add))
                chain(nc.vector.tensor_tensor(TE2, KEEPb, sel, ALU.mult))
                chain(nc.vector.reduce_sum(IDF, TE2, AX.X))
                chain(nc.vector.tensor_tensor(gate, IDF, top, ALU.mult))
            dve.sem_inc(rt_idx, 1)
            dve.wait_ge(ld_3, 16 * 12)
            dve.wait_ge(k4_ks, KC)
            for b in range(B):
                for k in range(KC):
                    for h in range(8):
                        last = nc.vector.tensor_scalar(KBD[:, b, k, h, :], KT1[:, k, b * LK:(b + 1) * LK], headmask[:, h:h + 1], None, ALU.mult)
            last.then_inc(k4_kb, 1)
            dve.wait_ge(k4_v, 1)
            nc.vector.memset(VBD, 0.0)
            nc.vector.memset(SSB, 0.0)
            nc.vector.memset(V1, 1.0).then_inc(k4_vs, 1)
            dve.wait_ge(k4_vs, 1)
            for b in range(B):
                last = nc.vector.tensor_tensor(V1[:, b, :, 0:HD], PS[0:LK, 4 + b, 0:D].rearrange("p (h d) -> p h d", h=HEADS),
                                               BV1[0:LK].rearrange("p (h d) -> p h d", h=HEADS), ALU.add)
            last.then_inc(k4_vs, 1)
            with dve.Fori(0, E // 2) as it:
                for n in range(2):
                    dve.wait_ge(me_h, 2 * it + n + 1)
                    nc.vector.tensor_scalar(HTE[:, n], he_ps, 0.0, None, ALU.max).then_inc(me_hs, 1)

            def stats(c, ready):
                for t in range(CT):
                    last = nc.vector.bn_stats(ST[:, t, :], X[:, c * CT + t, :])
                chain(last)
                for t in range(CT):
                    last = nc.vector.bn_aggr(MV[:, t, :], ST[:, t, :])
                chain(last)
                nc.vector.tensor_scalar(VE, MV[:, :, 1], LN_EPS, None, ALU.add).then_inc(ready, 1)

            def combine(c):
                dve.wait_ge(s_gath, 16 * 2 * CT * (c + 1))
                for a, gate in enumerate((GATE1, GATE2)):
                    for t in range(CT):
                        ht = H[:, c * CT + t, :]
                        last = nc.vector.scalar_tensor_tensor(out=ht, in0=GB[:, t, a, :], scalar=gate[:, c * CT + t:c * CT + t + 1], in1=ht,
                                                              op0=ALU.mult, op1=ALU.add)
                    chain(last)
                xc = X[:, c * CT:(c + 1) * CT, :]
                chain(nc.vector.tensor_tensor(xc, xc, H[:, c * CT:(c + 1) * CT, :], ALU.add))
                dve.sem_inc(q4_x, 1)

            def normed(c):
                dve.wait_ge(q4_r, c + 1)
                if c:
                    dve.wait_ge(q4_zT, c)
                for t in range(CT):
                    last = nc.vector.tensor_scalar(Z4[:, t, :], X[:, c * CT + t, :], MV[:, t, 0:1], RSTD[:, t:t + 1],
                                                   ALU.subtract, ALU.mult)
                last.then_inc(q4_z, 1)

            def add_out(c):
                dve.wait_ge(q4_out, c + 1)
                dve.wait_ge(q4_bo, c + 1)
                xc = X[:, c * CT:(c + 1) * CT, :]
                nc.vector.tensor_tensor(xc, out4_ps, xc, ALU.add).then_inc(q4_xo, 1)
                dve.wait_ge(q4_xo, c + 1)

            def normed3(c):
                dve.wait_ge(q4_r3, c + 1)
                for t in range(CT):
                    last = nc.vector.tensor_scalar(H[:, c * CT + t, :], X[:, c * CT + t, :], MV[:, t, 0:1], RSTD[:, t:t + 1],
                                                   ALU.subtract, ALU.mult)
                last.then_inc(q4_z3, 1)

            def gates(c):
                dve.wait_ge(q4_g, c + 1)
                nc.vector.tensor_copy(LG[:, c * CT:(c + 1) * CT, :], gate_ps).then_inc(q4_gs, 1)

            def subtract_max(c, t):
                dve.wait_ge(q4_sc, c * CT + t + 1)
                ab = sc4_ps[:, 0:2].rearrange("p a (h k) -> p a h k", h=6)
                cc_ = sc4_ps[:, 2, 0:4 * LK].rearrange("p (h k) -> p h k", h=4)
                nc.vector.reduce_max(MX4[:, 0:12], ab, AX.X)
                chain(nc.vector.reduce_max(MX4[:, 12:16], cc_, AX.X))
                for a in range(2):
                    nc.vector.tensor_tensor(SS[:, t % 2, 6 * a:6 * a + 6, :], ab[:, a], MX4[:, 6 * a:6 * a + 6].unsqueeze(2).to_broadcast([P, 6, LK]), ALU.subtract)
                nc.vector.tensor_tensor(SS[:, t % 2, 12:16, :], cc_, MX4[:, 12:16].unsqueeze(2).to_broadcast([P, 4, LK]), ALU.subtract).then_inc(q4_sub, 1)

            def heads_out(c, t):
                dve.wait_ge(q4_o, c * CT + t + 1)
                if c:
                    dve.wait_ge(q4_oT, c)
                chain(nc.vector.reciprocal(RO, o4_ps[:, :, HD]))
                nc.vector.tensor_tensor(O4[:, t, :].rearrange("p (h d) -> p h d", h=HEADS), o4_ps[:, :, 0:HD],
                                        RO.unsqueeze(2).to_broadcast([P, HEADS, HD]), ALU.mult).then_inc(q4_on, 1)

            dve.wait_ge(k4_v, 1)
            combine(0)
            chain(nc.vector.memset(ZB, 0.0))
            stats(0, q4_var)
            normed(0)
            subtract_max(0, 0)
            for c in range(NCH):
                enters, leaves = c + 1 < NCH, c > 0
                subtract_max(c, 1)
                if enters:
                    combine(c + 1)
                    stats(c + 1, q4_var)
                heads_out(c, 0)
                subtract_max(c, 2)
                if leaves:
                    add_out(c - 1)
                if enters:
                    normed(c + 1)
                heads_out(c, 1)
                subtract_max(c, 3)
                if leaves:
                    stats(c - 1, q4_var3)
                heads_out(c, 2)
                if enters:
                    subtract_max(c + 1, 0)
                if leaves:
                    normed3(c - 1)
                    gates(c - 1)
                heads_out(c, 3)
            add_out(NCH - 1)
            stats(NCH - 1, q4_var3)
            normed3(NCH - 1)
            gates(NCH - 1)
            dve.wait_ge(q4_gs, NCH)
            dve.wait_ge(q4_g, NCH)
            chain(nc.vector.reduce_max(M5, LG[:], AX.X))
            chain(nc.vector.tensor_tensor(T5, LG[:], over_e(M5), ALU.is_equal))
            chain(nc.vector.tensor_tensor(T5, T5, over_t(w8), ALU.mult))
            chain(nc.vector.reduce_max(M5, T5, AX.X))
            chain(nc.vector.tensor_tensor(SEL5, T5, over_e(M5), ALU.is_equal))
            nc.vector.tensor_copy(SELF5, SEL5).then_inc(r5_sel, 1)
            dve.wait_ge(r5_cnt, 1)
            chain(nc.vector.reduce_sum(CN, cnt_ps.rearrange("p t e -> p e t"), AX.X))
            chain(nc.vector.tensor_tensor(CMP, CN.unsqueeze(2).to_broadcast([P, E, NT]), j128.unsqueeze(1).to_broadcast([P, E, NT]), ALU.is_gt))
            chain(nc.vector.reduce_sum(NTL, CMP, AX.X))
            chain(nc.vector.tensor_copy(CUM[:, 0:1], NTL[:, 0:1]))
            for e in range(1, E):
                chain(nc.vector.tensor_tensor(CUM[:, e:e + 1], CUM[:, e - 1:e], NTL[:, e:e + 1], ALU.add))
            chain(nc.vector.tensor_tensor(OFFS, CUM, NTL, ALU.subtract))
            chain(nc.vector.tensor_scalar(OFFS, OFFS, float(P), None, ALU.mult))
            dve.wait_ge(r5_pos, 1)
            chain(nc.vector.tensor_tensor(T5, pos_ps, over_t(OFFS), ALU.add))
            chain(nc.vector.tensor_tensor(T5, T5, SEL5, ALU.mult))
            chain(nc.vector.reduce_sum(IDF5, T5, AX.X))
            nc.vector.tensor_copy(IDX5, IDF5).then_inc(r5_idx, 1)
            chain(nc.vector.tensor_tensor(TEX, CUM[0:1, 0:E - 1].unsqueeze(1).to_broadcast([1, NT1, E - 1]),
                                          jt.unsqueeze(2).to_broadcast([1, NT1, E - 1]), ALU.is_le))
            chain(nc.vector.reduce_sum(TEF, TEX, AX.X))
            chain(nc.vector.tensor_scalar(TEG, TEF, EH - 0.5, -float(E), ALU.is_ge, ALU.mult))
            chain(nc.vector.tensor_copy(TEI, TEF))
            nc.vector.scalar_tensor_tensor(out=TEP, in0=TEF, scalar=float(EH), in1=TEG, op0=ALU.add, op1=ALU.add).then_inc(r5_idx, 1)
            dve.wait_ge(ld_b, 32)
            chain(nc.vector.tensor_copy(BBP[:, 0], BBF))
            chain(nc.vector.tensor_tensor(BBR, BBF, BBP[:, 0], ALU.subtract))
            chain(nc.vector.tensor_copy(BBP[:, 1], BBR))
            nc.vector.tensor_tensor(BBP[:, 2], BBR, BBP[:, 1], ALU.subtract).then_inc(b5_p, 1)

            def relu5(j, n):
                dve.wait_ge(m5_h, j + 1)
                nc.vector.tensor_scalar(HT5[:, n], hT5_ps[n], 0.0, None, ALU.max).then_inc(m5_hs, 1)

            def evac_y5(j, n, it):
                dve.wait_ge(m5_y, j + 1 + FIRST)
                dve.wait_ge(m5_out[n], 16 * it + FIRST)
                nc.vector.tensor_copy(YB5[:, n], y5_ps).then_inc(m5_ys, 1)

            relu5(0, 0)
            with dve.Fori(0, (NT1 - 3) // 2) as it:
                for n in range(2):
                    relu5(2 * it + n + 1, 1 - n)
                    evac_y5(2 * it + n, n, it)
            relu5(NT1 - 2, 1)
            evac_y5(NT1 - 3, 0, (NT1 - 3) // 2)
            relu5(NT1 - 1, 0)
            evac_y5(NT1 - 2, 1, (NT1 - 3) // 2)
            evac_y5(NT1 - 1, 0, (NT1 - 1) // 2)
            for c in range(NCH):
                dve.wait_ge(s_gat5[c], 16 * CT)
                xc = X[:, c * CT:(c + 1) * CT, :]
                nc.vector.tensor_tensor(xc, xc, H[:, c * CT:(c + 1) * CT, :], ALU.add).then_inc(s_fin, 1)

        @block.tensor
        def _(pe):
            for primed in (s_pvd, m5_y):
                pe.sem_inc(primed, FIRST)
            pe.wait_ge(ld_c, 32)
            pe.wait_ge(ld_w, 16 * 7)
            for m in range(KC):
                for k in range(KC):
                    last = nc.tensor.matmul(PS[:, m, 0:B * LK], wk0[:, k, m * P:(m + 1) * P], ctxT[:, k, :],
                                            start=(k == 0), stop=(k == KC - 1))
                last.then_inc(pre_k, 1)
            pe.wait_ge(pre_ks, KC)
            for m in range(KC):
                for k in range(KC):
                    nc.tensor.matmul(PS[:, 2 + m, 0:B * LK], wq0T[:, k, m * P:(m + 1) * P], KT0[:, k, :],
                                     start=(k == 0), stop=(k == KC - 1))
            for k in range(KC):
                nc.tensor.matmul(PS[0:1, 4, 0:B * LK], bq0[:, k:k + 1], KT0[:, k, :], start=(k == 0), stop=(k == KC - 1))
            for b in range(B):
                for k in range(KC):
                    last = nc.tensor.matmul(PS[0:LK, 5 + b, 0:D], ctxT[:, k, b * LK:(b + 1) * LK], wv0[:, k, :],
                                            start=(k == 0), stop=(k == KC - 1))
            last.then_inc(pre_a, 1)

            def rows_T1(rows, dst, ready, done, c):
                pe.wait_ge(ready, c + 1)
                for t in range(CT):
                    for k in range(KC):
                        last = nc.tensor.transpose(dst[:, k, t * P:(t + 1) * P], rows[:, t, k * P:(k + 1) * P], ident)
                last.then_inc(done, 1)

            def scores1(c):
                b = c // CPB
                pe.wait_ge(s_zTs, c + 1)
                if c:
                    pe.wait_ge(s_p, c)
                for t in range(CT):
                    for k in range(KC):
                        nc.tensor.matmul(sc_ps[:, t, 0:LK], ZT[:, k, t * P:(t + 1) * P], A0[:, k, b * LK:(b + 1) * LK],
                                         start=(k == 0), stop=False)
                    last = nc.tensor.matmul(sc_ps[:, t, 0:LK], ones_row, CB0[:, b * LK:(b + 1) * LK], start=False, stop=True)
                last.then_inc(s_sc, 1)

            def weights_T1(c):
                pe.wait_ge(s_p, c + 1)
                if c:
                    pe.wait_ge(s_pTs, c)
                for t in range(CT):
                    last = nc.tensor.transpose(pT_ps[:, t * P:(t + 1) * P], P0[:, t, 0:LK], ident)
                last.then_inc(s_pT, 1)

            def heads1(c):
                pe.wait_ge(s_pTs, c + 1)
                for t in range(CT):
                    last = nc.tensor.matmul(o_ps[:, t, :], PT0[:, t * P:(t + 1) * P], V0[:, c // CPB, :],
                                            start=True, stop=True)
                last.then_inc(s_o, 1)

            def project(c, a):
                pe.wait_ge(s_uTs, c + 1)
                if a == 0 and c:
                    pe.wait_ge(s_vs, c)
                for r in range(2):
                    for k in range(KC):
                        m = 2 * a + r
                        last = nc.tensor.matmul(qk_ps[:, a, r, :], wqk[:, k, m * P:(m + 1) * P], UT[:, k, :],
                                                start=(k == 0), stop=(k == KC - 1))
                last.then_inc((s_q, s_k)[a], 1)

            def values(c):
                pe.wait_ge(s_rq, c + 1)
                for t in range(CT):
                    for k in range(KC):
                        last = nc.tensor.matmul(v_ps[:, t, :], UT[:, k, t * P:(t + 1) * P], wv[:, k, :],
                                                start=(k == 0), stop=(k == KC - 1))
                last.then_inc(s_v, 1)

            pe.wait_ge(pre_as, 1)
            rows_T1(Z, zT_ps, s_z, s_zT, 0)
            scores1(0)
            weights_T1(0)
            pe.wait_ge(pre_w, 2)
            for c in range(NCH):
                heads1(c)
                if c:
                    values(c - 1)
                if c + 1 < NCH:
                    pe.wait_ge(s_var2, c + 1)
                    rows_T1(Z, zT_ps, s_z, s_zT, c + 1)
                if c:
                    pe.wait_ge(s_rt, c)
                rows_T1(U, uT_ps, s_u, s_uT, c)
                if c + 1 < NCH:
                    scores1(c + 1)
                project(c, 0)
                if c + 1 < NCH:
                    weights_T1(c + 1)
                project(c, 1)
            values(NCH - 1)
            def max_unit(s, n, u):
                i, h0, nh, k0, w, masked = UNITS[u]
                pe.wait_ge(s_mfree, NU * s + u + 1)
                for h in range(nh):
                    dst = m_ps[u % 2][:, h * w:(h + 1) * w]
                    last = nc.tensor.matmul(dst, QT[0:QROWS, n, h0 + h, i * P:(i + 1) * P],
                                            KT[0:QROWS, n, h0 + h, k0:k0 + w], start=True, stop=not masked)
                    if masked:
                        last = nc.tensor.matmul(dst[:, w - P:w], identb, mask_q, start=False, stop=True)
                last.then_inc(s_mx, 1)

            def scores(s, n, k):
                c, j = STAGES[k]
                q0 = q0_of(c, j)
                for pair in range(2):
                    pe.wait_ge(s_sfree, 2 * NSTG * s + 2 * k + pair + 1)
                    for h in range(2):
                        hh = 2 * pair + h
                        dst = s_ps[pair][:, h, q0:CW]
                        masked = j >= CT * c
                        last = nc.tensor.matmul(dst, KT[0:AROWS, n, hh, j * P:(j + 1) * P],
                                                QT[0:AROWS, n, hh, c * CW + q0:(c + 1) * CW], start=True, stop=not masked)
                        if masked:
                            last = nc.tensor.matmul(dst[:, 0:P], identb, mask_k, start=False, stop=True)
                    last.then_inc(s_sT, 1)

            def weighted(s, n, k):
                c, j = STAGES[k]
                q0 = q0_of(c, j)
                if j == 0:
                    pe.wait_ge(s_yev, 2 * s + c + FIRST)
                pe.wait_ge(s_sfree, 2 * NSTG * s + 2 * k + 4)
                for h in range(GH):
                    last = nc.tensor.matmul(PS[VW * h:VW * (h + 1), 6, q0:CW], VS[:, n, j, h, :], PB[:, k % 2, h, q0:CW],
                                            start=(j == 0), stop=(j == CT * (c + 1) - 1))
                last.then_inc(s_pvd, 1)
                if j == CT * (c + 1) - 1:
                    pe.wait_ge(s_pvd, NSTG * s + k + 2 + FIRST)
                    pe.sem_inc(s_y, 1)

            def back(s, c):
                pe.wait_ge(s_yev, 2 * s + c + 1 + FIRST)
                for t in range(CT):
                    last = nc.tensor.transpose(t_ps[:, t * P:(t + 1) * P], YT[:, c, t * P:(t + 1) * P], ident)
                last.then_inc(s_yt, 1)

            def parts_T(s):
                pe.wait_ge(s_mp, s + 1)
                nc.tensor.transpose(t_ps.bitcast(bf16)[0:96, 0:P], MP.rearrange("p n h i -> p (n h i)"), identb).then_inc(s_mpt, 1)

            def pe_step(s, n, nxt, it, lead):
                after = (n + 1) % BUFS
                pe.wait_ge(s_vst, s + 1)
                if nxt:
                    pe.wait_ge(ld_qk[after], 16 * NLD * (it + 1 + (n + 1) // BUFS))
                for k in range(NSTG):
                    if k:
                        scores(s, n, k)
                    if lead and k == MSTG:
                        pe.wait_ge(ld_qk[(n + 2) % BUFS], 16 * NLD * (it + 1 + (n + 2) // BUFS))
                    units(k, nxt, lead, lambda ahead, u: max_unit(s + ahead, (n + ahead) % BUFS, u), 0)
                    if k:
                        weighted(s, n, k - 1)
                    if nxt and k == MSTG:
                        pe.wait_ge(s_yn, 2 * s + 1)
                        parts_T(s + 1)
                    units(k, nxt, lead, lambda ahead, u: max_unit(s + ahead, (n + ahead) % BUFS, u), 1)
                    if k == 6:
                        back(s, 0)
                if nxt:
                    pe.wait_ge(s_mrow, 16 * (s + 2))
                    scores(s + 1, after, 0)
                if lead:
                    for u in range(LEAD - NEND, LEAD - NEND // 2):
                        max_unit(s + 2, (n + 2) % BUFS, u)
                weighted(s, n, NSTG - 1)
                if lead:
                    for u in range(LEAD - NEND // 2, LEAD):
                        max_unit(s + 2, (n + 2) % BUFS, u)
                back(s, 1)

            pe.sem_inc(s_pvd, 1)
            pe.wait_ge(ld_tab, 32)
            pe.wait_ge(ld_qk[0], 16 * NLD)
            for u in range(NU):
                max_unit(0, 0, u)
            pe.wait_ge(s_rt, NCH)
            parts_T(0)
            pe.wait_ge(s_vs, NCH)
            pe.wait_ge(s_mrow, 16)
            scores(0, 0, 0)
            pe.wait_ge(ld_qk[1], 16 * NLD)
            for u in range(LEAD):
                max_unit(1, 1, u)
            with pe.Fori(0, (NS - 1) // BUFS) as it:
                for n in range(BUFS):
                    pe_step(BUFS * it + n, n, True, it, True)
            for s in range((NS - 1) // BUFS * BUFS, NS):
                pe_step(s, s % BUFS, s + 1 < NS, s // BUFS, s + 2 < NS)
            pe.wait_ge(ld_3, 48)
            pe.wait_ge(s_yn, 2 * NS)
            def attended_T(c):
                if c:
                    pe.wait_ge(p3_yTs, c)
                for t in range(CT):
                    for k in range(KC):
                        last = nc.tensor.transpose(yT3_ps[:, k, t * P:(t + 1) * P], XF[:, c * CT + t, k * P:(k + 1) * P], ident)
                last.then_inc(p3_yT, 1)

            def project_out(c):
                pe.wait_ge(p3_yTs, c + 1)
                if c:
                    pe.wait_ge(p3_h, c)
                for t in range(CT):
                    for k in range(KC):
                        last = nc.tensor.matmul(o3_ps[:, t, :], YCT[:, k, t * P:(t + 1) * P], WO[:, k, :], start=(k == 0), stop=(k == KC - 1))
                last.then_inc(p3_o, 1)

            def rows_T3(c):
                pe.wait_ge(p3_xc, c + 1)
                for t in range(CT):
                    for k in range(KC):
                        last = nc.tensor.transpose(xT3_ps[:, k, t * P:(t + 1) * P], XF[:, c * CT + t, k * P:(k + 1) * P], ident)
                last.then_inc(p3_xT, 1)

            def logits(c):
                pe.wait_ge(p3_xTs, c + 1)
                if c:
                    pe.wait_ge(p3_lgs, c)
                for t in range(CT):
                    for k in range(KC):
                        last = nc.tensor.matmul(lg_ps[:, t, :], XCT[:, k, t * P:(t + 1) * P], WR[:, k, :], start=(k == 0), stop=(k == KC - 1))
                last.then_inc(p3_lg, 1)

            attended_T(0)
            for c in range(NCH + 2):
                if c < NCH:
                    project_out(c)
                if c + 1 < NCH:
                    attended_T(c + 1)
                if c > 1:
                    logits(c - 2)
                if 0 < c <= NCH:
                    rows_T3(c - 1)

            def prefix(dst, ones_zeros, done):
                nc.tensor.matmul(dst, tri_b, ones_zeros, start=True, stop=False)
                for d in range(1, NT):
                    last = nc.tensor.matmul(dst[:, d:NT, :], ones_b, ones_zeros[:, 0:NT - d, :], start=False, stop=(d == NT - 1))
                last.then_inc(done, 1)

            with pe.Fori(0, BITS // BSTEP) as i:
                pe.wait_ge(rt_ge, i + 1)
                for t in range(NT):
                    last = nc.tensor.matmul(ncand_ps.rearrange("p j e -> p (j e)"), ones_b, REACH[:, t].rearrange("p j e -> p (j e)"),
                                            start=(t == 0), stop=(t == NT - 1))
                last.then_inc(rt_cnt, 1)
            pe.wait_ge(rt_ge, BITS // BSTEP + 1)
            prefix(pfx_ps, EQb, rt_eqT)
            nc.tensor.matmul(cnt_ps, ones_b, GEb, start=True, stop=True).then_inc(rt_cnt, 1)
            pe.wait_ge(rt_keep, 1)
            prefix(pos_ps, KEEPb, rt_pos)

            pe.wait_ge(ld_3, 16 * 12)
            for m in range(KC):
                for k in range(KC):
                    last = nc.tensor.matmul(PS[:, 6 + m, 0:B * LK], WK1[:, k, m * P:(m + 1) * P], CT1[:, k, :], start=(k == 0), stop=(k == KC - 1))
                last.then_inc(k4_k, 1)
            for b in range(B):
                for k in range(KC):
                    last = nc.tensor.matmul(PS[0:LK, 4 + b, 0:D], CT1[:, k, b * LK:(b + 1) * LK], WV1[:, k, :], start=(k == 0), stop=(k == KC - 1))
            last.then_inc(k4_v, 1)
            pe.wait_ge(k4_ks, KC)
            pe.wait_ge(k4_vs, 2)

            def rows_T(e, n, count, first=False):
                pe.wait_ge(ld_xe[n], 32 * count)
                if not first:
                    pe.wait_ge(me_xTs, e)
                for t, w in ((0, P), (1, P), (2, TAIL)):
                    for k in range(KC):
                        last = nc.tensor.transpose(xeT_ps[:, k, t * P:t * P + w], XEB[0:w, n, t, k * P:(k + 1) * P], ident[0:w, 0:w])
                last.then_inc(me_xT, 1)

            def expert_h(e, n, count, first=False):
                pe.wait_ge(me_xTs, e + 1)
                pe.wait_ge(ld_w1e[n], 16 * count)
                if not first:
                    pe.wait_ge(me_hs, e)
                for f in range(FC0):
                    for k in range(KC):
                        last = nc.tensor.matmul(he_ps[:, f, :], W1E[:, n, k, f * P:(f + 1) * P], XET[:, n, k, :], start=(k == 0), stop=(k == KC - 1))
                last.then_inc(me_h, 1)

            def expert_y(e, n, count):
                pe.wait_ge(me_hs, e + 1)
                pe.wait_ge(me_ys, e + FIRST)
                pe.wait_ge(ld_w2e[n], 16 * count)
                for t, w in ((0, P), (1, P), (2, TAIL)):
                    for f in range(FC0):
                        last = nc.tensor.matmul(ye_ps[0:w, t, :], HTE[:, n, f, t * P:t * P + w], W2E[:, n, f, :], start=(f == 0), stop=(f == FC0 - 1))
                last.then_inc(me_y, 1)

            pe.wait_ge(rt_idx, 1)
            rows_T(0, 0, 1, first=True)
            expert_h(0, 0, 1, first=True)
            rows_T(1, 1, 1)
            with pe.Fori(0, E // 2 - 1) as it:
                for n in range(2):
                    e = 2 * it + n
                    expert_h(e + 1, 1 - n, it + 1 + n)
                    rows_T(e + 2, n, it + 2)
                    expert_y(e, n, it + 1)
            expert_h(E - 1, 1, E // 2)
            expert_y(E - 2, 0, E // 2)
            expert_y(E - 1, 1, E // 2)
            pe.wait_ge(ld_4, 16 * 2)
            pe.wait_ge(k4_kb, 1)
            pe.wait_ge(me_ys, E + FIRST)

            def rows_T4(rows, done):
                for t in range(CT):
                    for k in range(KC):
                        last = nc.tensor.transpose(zT4_ps[:, k, t * P:(t + 1) * P], rows[:, t, k * P:(k + 1) * P], ident)
                last.then_inc(done, 1)

            def enter_zT(c):
                pe.wait_ge(q4_z, c + 1)
                if c > 1:
                    pe.wait_ge(q4_xo, c - 1)
                rows_T4(Z4, q4_zT)

            def enter_q(c):
                pe.wait_ge(q4_zTs, c + 1)
                for m in range(KC):
                    for k in range(KC):
                        last = nc.tensor.matmul(q4_ps[:, m, :], WQ1[:, k, m * P:(m + 1) * P], Z4T[:, k, :], start=(k == 0), stop=(k == KC - 1))
                last.then_inc(q4_q, 1)

            def scores4(c, t):
                if t == 0:
                    pe.wait_ge(q4_qs, c + 1)
                if c or t:
                    pe.wait_ge(q4_sub, c * CT + t)
                for bank, off, k, h0, nh in SC4:
                    last = nc.tensor.matmul(sc4_ps[:, bank, off * LK:(off + nh) * LK], Q4T[:, c % 2, k, t * P:(t + 1) * P],
                                            KBD[:, c // CPB, k, h0:h0 + nh, :].rearrange("p h k -> p (h k)"), start=True, stop=True)
                last.then_inc(q4_sc, 1)

            def leave_oT(c):
                pe.wait_ge(q4_on, (c + 1) * CT)
                if c:
                    pe.wait_ge(q4_gs, c)
                rows_T4(O4, q4_oT)

            def leave_out(c):
                pe.wait_ge(q4_oTs, c + 1)
                for t in range(CT):
                    for k in range(KC):
                        last = nc.tensor.matmul(out4_ps[:, t, :], Z4T[:, k, t * P:(t + 1) * P], WO1[:, k, :], start=(k == 0), stop=(k == KC - 1))
                last.then_inc(q4_out, 1)

            def leave_z3T(c):
                pe.wait_ge(q4_z3, c + 1)
                if c + 2 < NCH:
                    pe.wait_ge(q4_qs, c + 3)
                rows_T4(H[:, c * CT:(c + 1) * CT], q4_z3T)

            def leave_gates(c):
                pe.wait_ge(q4_z3Ts, c + 1)
                for t in range(CT):
                    for k in range(KC):
                        nc.tensor.matmul(gate_ps[:, t, :], Z4T[:, k, t * P:(t + 1) * P], WG[:, k, :], start=(k == 0), stop=False)
                    last = nc.tensor.matmul(gate_ps[:, t, :], ones_row, BG, start=False, stop=True)
                last.then_inc(q4_g, 1)

            def weights_T(c, t, q):
                n = (c * CT + t) * NQ + q
                pe.wait_ge(q4_p, c * CT + t + 1)
                if n > 1:
                    pe.wait_ge(q4_pTs, n - 1)
                for i, j in enumerate(UBLK[q]):
                    last = nc.tensor.transpose(pT4_ps[n % 2][:, i, :], SSB[:, t % 2, j * P:(j + 1) * P], ident)
                last.then_inc(q4_pT, 1)

            def heads(c, t, q):
                pe.wait_ge(q4_pTs, (c * CT + t) * NQ + q + 1)
                if q == 0:
                    if c or t:
                        pe.wait_ge(q4_on, c * CT + t)
                    nc.tensor.matmul(o4f_ps, ones_b[0:1, :], ZB, start=True, stop=False)
                for j in UBLK[q]:
                    h0, h1 = HWIN[j]
                    last = nc.tensor.matmul(o4f_ps[:, h0 * HW:h1 * HW], PT4[:, j, :],
                                            VBD[:, c // CPB, j, 0:h1 - h0, :].rearrange("p h n -> p (h n)"), start=False, stop=(j == NBLK - 1))
                if q == NQ - 1:
                    last.then_inc(q4_o, 1)

            enter_zT(0)
            enter_q(0)
            scores4(0, 0)
            pe.wait_ge(k4_vb, 16 * sum(h1 - h0 for h0, h1 in HWIN))
            for c in range(NCH):
                for t in range(CT):
                    if c * CT + t + 1 < NT:
                        scores4(c + (t + 1) // CT, (t + 1) % CT)
                    if c or t:
                        heads(c - (t == 0), (t - 1) % CT, NQ - 1)
                    for q in range(NQ):
                        weights_T(c, t, q)
                        if q:
                            heads(c, t, q - 1)
                        if (t, q) == (0, 1) and c:
                            leave_oT(c - 1)
                        if (t, q) == (0, 2) and c:
                            leave_out(c - 1)
                        if (t, q) == (2, 0) and c + 1 < NCH:
                            enter_zT(c + 1)
                        if (t, q) == (2, 1) and c + 1 < NCH:
                            enter_q(c + 1)
                        if (t, q) == (3, 1) and c:
                            leave_z3T(c - 1)
                        if (t, q) == (3, 2) and c:
                            leave_gates(c - 1)
            heads(NCH - 1, CT - 1, NQ - 1)
            leave_oT(NCH - 1)
            leave_out(NCH - 1)
            leave_z3T(NCH - 1)
            leave_gates(NCH - 1)
            pe.wait_ge(q4_gs, NCH)
            pe.wait_ge(r5_sel, 1)
            nc.tensor.matmul(cnt_ps, ones_b, SELF5, start=True, stop=True).then_inc(r5_cnt, 1)
            prefix(pos_ps, SELF5, r5_pos)

            def xT5(j, n, it):
                pe.wait_ge(ld_xs[n], 16 * (it + 1))
                pe.wait_ge(m5_xTs, j)
                for k in range(KC):
                    last = nc.tensor.transpose(xT5_ps[:, k, :], XS5[:, n, k * P:(k + 1) * P], ident)
                last.then_inc(m5_xT, 1)

            def expert_of(j):
                return pe.value_load(TEI[0:1, ds(j, 1)], min_val=0, max_val=E - 1)

            def w2_of(j):
                return pe.value_load(TEP[0:1, ds(j, 1)], min_val=0, max_val=E - 1)

            def h5(j, n, e):
                pe.wait_ge(m5_w, j + 1)
                pe.wait_ge(m5_xTs, j + 1)
                for f in range(FC1):
                    for k in range(KC):
                        nc.tensor.matmul(hT5_ps[n][:, f, :], W1C[n][:, k, f * P:(f + 1) * P], XT5[:, n, k, :], start=(k == 0), stop=False)
                    last = nc.tensor.matmul(hT5_ps[n][:, f, :], BPS[:, ds(e * F1 + f * P, P)], ones3, start=False, stop=True)
                last.then_inc(m5_h, 1)

            def y5(j, n, e, at):
                pe.wait_ge(m5_hs, j + 1)
                pe.wait_ge(m5_ys, j + FIRST)
                for f in range(FC1):
                    nc.tensor.matmul(y5_ps, HT5[:, n, f, :], W2S[:, ds(at, 1), f, :].squeeze(1), start=(f == 0), stop=False)
                nc.tensor.matmul(y5_ps, ones3, BPS[:, ds(e * D + NB1, D)], start=False, stop=True).then_inc(m5_y, 1)

            pe.wait_ge(r5_idx, 2)
            xT5(0, 0, 0)
            pe.wait_ge(ld_bp, 16)
            pe.wait_ge(ld_5, 16 * 2 * E)
            h5(0, 0, expert_of(0))
            xT5(1, 1, 0)
            with pe.Fori(0, (NT1 - 3) // 2) as it:
                for n in range(2):
                    j = 2 * it + n
                    e, at, e_next = expert_of(j), w2_of(j), expert_of(j + 1)
                    h5(j + 1, 1 - n, e_next)
                    xT5(j + 2, n, it + 1)
                    y5(j, n, e, at)
            h5(NT1 - 2, 1, expert_of(NT1 - 2))
            xT5(NT1 - 1, 0, (NT1 - 1) // 2)
            y5(NT1 - 3, 0, expert_of(NT1 - 3), w2_of(NT1 - 3))
            h5(NT1 - 1, 0, expert_of(NT1 - 1))
            y5(NT1 - 2, 1, expert_of(NT1 - 2), w2_of(NT1 - 2))
            y5(NT1 - 1, 0, expert_of(NT1 - 1), w2_of(NT1 - 1))


def _consts(D, S, NT, E, CAP):
    import numpy as np
    P = 128
    i = np.arange(P)
    cf = np.zeros((P, 3 * P + 96), np.float32)
    cf[:, 0:P] = np.eye(P)
    cf[:, P:2 * P] = i[:, None] < i[None, :]
    cf[:, 2 * P:3 * P] = 1.0
    o = 3 * P
    cf[:, o:o + E] = E - np.arange(E)
    cf[:, o + E:o + 2 * E] = np.arange(E) * CAP - E * CAP
    cf[:, o + 2 * E:o + 2 * E + 16] = P * np.arange(16)
    cf[:, o + 32:o + 32 + NT + E - 1] = np.arange(NT + E - 1)
    cf[:, o + 64:o + 64 + NT] = -0.5
    cf[:, o + 80:o + 88] = (i[:, None] // 16) == np.arange(8)[None, :]
    cf[:, o + 88:o + 95] = (np.arange(1, 8, dtype=np.int32) << 27).view(np.float32)
    cb = np.zeros((P, 5 * P), np.float32)
    cb[:, 0:P] = np.eye(P)
    cb[:, P:2 * P] = np.where(i[None, :] > i[:, None], -1.0e30, 0.0)
    cb[:, 2 * P:3 * P] = np.where(i[:, None] > i[None, :], -1.0e30, 0.0)
    cb[:, 3 * P:4 * P] = 1.0
    cb[:, 4 * P:5 * P] = i[:, None] < i[None, :]
    theta = (10000.0 ** (-2.0 * (np.arange(8, dtype=np.float32) / np.float32(16)))).astype(np.float32)
    pair = (i % 32) // 4
    angle = (np.arange(S, dtype=np.float32)[None, :] * theta[pair][:, None]).astype(np.float32).astype(np.float64)
    rope = np.stack([np.cos(angle), np.sin(angle)], 1).astype(np.float32)
    return cf, cb.astype(mybir.dt.np(mybir.dt.bfloat16)), rope


def _lay_out(i):
    import numpy as np
    P = 128

    def rows(w):
        return w.reshape(-1, P, w.shape[1]).transpose(1, 0, 2)

    def column(v):
        return v.reshape(-1, P).T

    x, ctx = i["x"], i["ctx_1024"]
    D = x.shape[2]
    cf, cb, rope = _consts(D, x.shape[1], x.shape[0] * x.shape[1] // P, 8, 320)
    wqkv = i["L0_ffn_w_qkv"]
    p = np.arange(P)
    g, pair, hh = p // 32, (p % 32) // 4, p % 4
    cols = [a * D + (4 * g + hh) * 16 + 2 * pair + r for a in range(2) for r in range(2)]
    wqk = wqkv[:, np.concatenate(cols)]
    return dict(
        x=x, ctxT=rows(ctx.transpose(2, 0, 1).reshape(D, -1)), const_f=cf, const_b=cb, rope=rope,
        wq0T=rows(i["L0_xattn_Wq"].T), bq0=column(i["L0_xattn_bq"]), wk0=rows(i["L0_xattn_Wk"]),
        bk0=column(i["L0_xattn_bk"]), wv0=rows(i["L0_xattn_Wv"]), bv0=i["L0_xattn_bv"],
        g1=column(i["L0_ffn_g1"]), wqk=rows(wqk), wv=rows(wqkv[:, 2 * D:]), wo=rows(i["L0_ffn_w_o"]),
        g2=i["L0_ffn_g2"], wr=rows(i["L0_ffn_w_router"]), w1e=i["L0_ffn_w1"], w2e=i["L0_ffn_w2"],
        wq1=rows(i["L1_xattn_Wq"].T), bq1=column(i["L1_xattn_bq"]), wk1=rows(i["L1_xattn_Wk"].T),
        bk1=column(i["L1_xattn_bk"]), wv1=rows(i["L1_xattn_Wv"].T), bv1=i["L1_xattn_bv"],
        wo1=rows(i["L1_xattn_Wo"].T), bo1=i["L1_xattn_bo"], wg=rows(i["L1_ffn_Wg"]), bg=i["L1_ffn_bg"],
        w1=i["L1_ffn_W1"], b1=i["L1_ffn_b1"], w2=i["L1_ffn_W2"], b2=i["L1_ffn_b2"])


def kernel(**inputs):
    import numpy as _np
    import concourse.bacc as _bacc
    from concourse import mybir as _mybir
    from concourse.bass_utils import run_bass_kernel_spmd as _run

    nc = _bacc.Bacc("TRN2", target_bir_lowering=False, num_devices=1)
    arrays, args = {}, []
    for name, a in _lay_out({k: _np.asarray(v) for k, v in inputs.items()}).items():
        a = _np.ascontiguousarray(a)
        arrays[name + "_dram"] = a
        args.append(nc.dram_tensor(name + "_dram", a.shape, _mybir.dt.from_np(a.dtype), kind="ExternalInput").ap())
    shape = inputs["x"].shape
    args.append(nc.dram_tensor("out_dram", shape, _mybir.dt.float32, kind="ExternalOutput").ap())
    build_program(nc, *args)
    r = _run(nc, [arrays], core_ids=[0])
    return r.results[0]["out_dram"]
```
